# Optimizing a Trainium2 kernel written in Bass

```python
import numpy as np
import jax
import jax.numpy as jnp

def _softmax(x, axis=-1):
    return jax.nn.softmax(x, axis=axis)

def _gelu(x):
    return jax.nn.gelu(x, approximate=True)

def _silu(x):
    return jax.nn.silu(x)

def _sigmoid(x):
    return jax.nn.sigmoid(x)

def _layernorm(x, axis=-1, eps=1e-05):
    m = jnp.mean(x, axis=axis, keepdims=True)
    v = jnp.var(x, axis=axis, keepdims=True)
    return (x - m) / jnp.sqrt(v + eps)

def _scatter_add(tgt, idx, src, axis=0):
    return tgt.at[idx].add(src)

def _segment_sum(src, seg, n):
    return jax.ops.segment_sum(src, seg, n)
kernel_name = 'mk_early_fusion_d1_tok_img768_r4_8a1f9f'

def setup_inputs(seed: int=0):
    np.random.seed(seed)
    _w = jnp.asarray

    def _rec_inputs():
        import jax
        import jax.numpy as jnp
        _rk = jax.random.key(seed)
        x = jax.random.uniform(jax.random.fold_in(_rk, 1), (16, 3, 96, 96), jnp.float32, 0.0, 1)
        txt = 0.0181629 + 1.04976 * jax.random.normal(jax.random.fold_in(_rk, 2), (16, 128, 192), jnp.float32)
        return (x, txt)
    x, txt = _rec_inputs()

    def _L0_tok_setup():
        import jax, jax.numpy as jnp
        import numpy as np
        B, C, H, W, P, D = (32, 3, 96, 96, 16, 192)
        N = H // P * (W // P)
        key = jax.random.key(seed)
        k0, k1, k2, k3 = jax.random.split(key, 4)
        x = jax.random.uniform(k0, (B, C, H, W), dtype=jnp.float32)
        proj_w = jax.random.normal(k1, (D, P * P * C), dtype=jnp.float32) * 0.02
        proj_b = jnp.zeros((D,), jnp.float32)
        cls_token = jax.random.normal(k2, (1, 1, D), dtype=jnp.float32)
        pos_embedding = jax.random.normal(k3, (1, N + 1, D), dtype=jnp.float32)
        return {'x': x, 'proj_w': proj_w, 'proj_b': proj_b, 'cls_token': cls_token, 'pos_embedding': pos_embedding}
    _L0_tok_all = _L0_tok_setup()
    _L0_tok_in = {k: v for k, v in _L0_tok_all.items() if k in ('proj_w', 'proj_b', 'cls_token', 'pos_embedding')}
    del _L0_tok_all

    def _L0_attn_setup():
        import jax, jax.numpy as jnp
        import numpy as np
        import math
        B, L, D, H, R = (2, 256, 192, 12, 64)
        DH = D // H

        def layernorm(x, g, b, eps=1e-05):
            mu = jnp.mean(x, axis=-1, keepdims=True)
            var = jnp.mean((x - mu) ** 2, axis=-1, keepdims=True)
            return (x - mu) / jnp.sqrt(var + eps) * g + b

        def _reference_tuple_inner(x, conv_w, conv_b, ln_g, ln_b, qkv_w, qkv_b, bn_w1, bn_w2, temperature, proj_w, proj_b, mn_g, mn_b):
            Bx, Lx, Dx = x.shape
            xp = jnp.pad(x, ((0, 0), (2, 0), (0, 0)))
            conv = xp[:, 0:Lx] * conv_w[:, 0] + xp[:, 1:Lx + 1] * conv_w[:, 1] + xp[:, 2:Lx + 2] * conv_w[:, 2] + conv_b
            x_conv = x + conv
            xn = layernorm(x_conv, ln_g, ln_b)
            qkv = xn @ qkv_w.T + qkv_b
            q, k, v = jnp.split(qkv, 3, axis=-1)
            params = (jax.nn.silu(xn @ bn_w1.T) @ bn_w2.T).reshape(Bx, Lx, H, 5)
            sem_amp = jax.nn.sigmoid(params[..., 0])
            sem_phase = jnp.tanh(params[..., 1]) * math.pi
            ctx_amp = jax.nn.sigmoid(params[..., 2])
            ctx_phase = jnp.tanh(params[..., 3]) * math.pi
            decay = 0.3 + 0.65 * jax.nn.sigmoid(params[..., 4])
            gate = jax.nn.sigmoid(sem_amp * ctx_amp * jnp.cos(sem_phase - ctx_phase) * temperature[0])
            q_f = (jax.nn.elu(q) + 1.0).reshape(Bx, Lx, H, DH)
            k_f = (jax.nn.elu(k) + 1.0).reshape(Bx, Lx, H, DH)
            v_f = v.reshape(Bx, Lx, H, DH)
            one_minus = 1.0 - decay
            kv_input = jnp.einsum('blhd,blhe->blhde', k_f, v_f)
            kv_input = jnp.clip(kv_input * (gate * one_minus)[..., None, None], -5.0, 5.0)
            df = jnp.exp(jnp.cumsum(jnp.log(decay), axis=1))
            safe_df = df + 1e-08
            kv_states = jnp.cumsum(kv_input / safe_df[..., None, None], axis=1) * df[..., None, None]
            z = jnp.cumsum(k_f * one_minus[..., None] / safe_df[..., None], axis=1) * df[..., None]
            z = jnp.clip(z, -10000.0, 10000.0)
            out_num = jnp.einsum('blhd,blhde->blhe', q_f, kv_states)
            den = jnp.sum(q_f * z, axis=-1, keepdims=True) + 0.0001
            out = layernorm(out_num / den, mn_g, mn_b)
            y = out.reshape(Bx, Lx, Dx) @ proj_w.T + proj_b
            return (y, gate)
        key = jax.random.key(seed)
        ks = jax.random.split(key, 8)
        x = jax.random.normal(ks[0], (B, L, D), dtype=jnp.float32)
        conv_w = jax.random.normal(ks[1], (D, 3), dtype=jnp.float32) * 0.3
        conv_b = jnp.zeros((D,), jnp.float32)
        ln_g = jnp.ones((D,), jnp.float32)
        ln_b = jnp.zeros((D,), jnp.float32)
        qkv_w = jax.random.normal(ks[2], (3 * D, D), dtype=jnp.float32) / math.sqrt(D)
        qkv_b = jnp.zeros((3 * D,), jnp.float32)
        bn_w1 = jax.random.normal(ks[3], (R, D), dtype=jnp.float32) / math.sqrt(D)
        bn_w2 = jax.random.normal(ks[4], (H * 5, R), dtype=jnp.float32) / math.sqrt(R)
        temperature = jnp.ones((1,), jnp.float32) * 0.5
        proj_w = jax.random.normal(ks[5], (D, D), dtype=jnp.float32) / math.sqrt(D)
        proj_b = jnp.zeros((D,), jnp.float32)
        mn_g = jnp.ones((DH,), jnp.float32)
        mn_b = jnp.zeros((DH,), jnp.float32)
        return {'x': x, 'conv_w': conv_w, 'conv_b': conv_b, 'ln_g': ln_g, 'ln_b': ln_b, 'qkv_w': qkv_w, 'qkv_b': qkv_b, 'bn_w1': bn_w1, 'bn_w2': bn_w2, 'temperature': temperature, 'proj_w': proj_w, 'proj_b': proj_b, 'mn_g': mn_g, 'mn_b': mn_b}
    _L0_attn_all = _L0_attn_setup()
    _L0_attn_in = {k: v for k, v in _L0_attn_all.items() if k in ('conv_w', 'conv_b', 'ln_g', 'ln_b', 'qkv_w', 'qkv_b', 'bn_w1', 'bn_w2', 'temperature', 'proj_w', 'proj_b', 'mn_g', 'mn_b')}
    del _L0_attn_all

    def _L0_ffn_setup():
        import jax, jax.numpy as jnp
        import numpy as np
        B, S, D, F, E = (2, 256, 192, 768, 8)
        key = jax.random.key(seed)
        k0, k1, k2, k3, k4, k5 = jax.random.split(key, 6)
        scale = 0.02
        return {'hidden_states': jax.random.normal(k0, (B, S, D), dtype=jnp.float32), 'Wg': jax.random.normal(k1, (D, E), dtype=jnp.float32) * scale, 'W1': jax.random.normal(k2, (E, D, F), dtype=jnp.float32) * scale, 'b1': jnp.zeros((E, F), dtype=jnp.float32), 'W2': jax.random.normal(k3, (E, F, D), dtype=jnp.float32) * scale, 'b2': jnp.zeros((E, D), dtype=jnp.float32)}
    _L0_ffn_all = _L0_ffn_setup()
    _L0_ffn_in = {k: v for k, v in _L0_ffn_all.items() if k in ('Wg', 'W1', 'b1', 'W2', 'b2')}
    del _L0_ffn_all
    return {'x': x, 'txt': txt, 'L0_tok_proj_w': _L0_tok_in['proj_w'], 'L0_tok_proj_b': _L0_tok_in['proj_b'], 'L0_tok_cls_token': _L0_tok_in['cls_token'], 'L0_tok_pos_embedding': _L0_tok_in['pos_embedding'], 'L0_attn_conv_w': _L0_attn_in['conv_w'], 'L0_attn_conv_b': _L0_attn_in['conv_b'], 'L0_attn_ln_g': _L0_attn_in['ln_g'], 'L0_attn_ln_b': _L0_attn_in['ln_b'], 'L0_attn_qkv_w': _L0_attn_in['qkv_w'], 'L0_attn_qkv_b': _L0_attn_in['qkv_b'], 'L0_attn_bn_w1': _L0_attn_in['bn_w1'], 'L0_attn_bn_w2': _L0_attn_in['bn_w2'], 'L0_attn_temperature': _L0_attn_in['temperature'], 'L0_attn_proj_w': _L0_attn_in['proj_w'], 'L0_attn_proj_b': _L0_attn_in['proj_b'], 'L0_attn_mn_g': _L0_attn_in['mn_g'], 'L0_attn_mn_b': _L0_attn_in['mn_b'], 'L0_ffn_Wg': _L0_ffn_in['Wg'], 'L0_ffn_W1': _L0_ffn_in['W1'], 'L0_ffn_b1': _L0_ffn_in['b1'], 'L0_ffn_W2': _L0_ffn_in['W2'], 'L0_ffn_b2': _L0_ffn_in['b2']}

def reference(x, txt, L0_tok_proj_w, L0_tok_proj_b, L0_tok_cls_token, L0_tok_pos_embedding, L0_attn_conv_w, L0_attn_conv_b, L0_attn_ln_g, L0_attn_ln_b, L0_attn_qkv_w, L0_attn_qkv_b, L0_attn_bn_w1, L0_attn_bn_w2, L0_attn_temperature, L0_attn_proj_w, L0_attn_proj_b, L0_attn_mn_g, L0_attn_mn_b, L0_ffn_Wg, L0_ffn_W1, L0_ffn_b1, L0_ffn_W2, L0_ffn_b2):
    import jax
    import jax.numpy as jnp

    def _L0_tok_ref(x, proj_w, proj_b, cls_token, pos_embedding):
        import jax, jax.numpy as jnp
        import numpy as np
        B, C, H, W, P, D = (32, 3, 96, 96, 16, 192)
        N = H // P * (W // P)
        b, c, h, w = x.shape
        hp, wp = (h // P, w // P)
        patches = x.reshape(b, c, hp, P, wp, P).transpose(0, 2, 4, 1, 3, 5).reshape(b, hp * wp, c * P * P)
        tok = jnp.einsum('bnk,dk->bnd', patches, proj_w) + proj_b
        cls = jnp.broadcast_to(cls_token, (b, 1, cls_token.shape[-1]))
        z0 = jnp.concatenate([cls, tok], axis=1) + pos_embedding
        return z0

    def _L0_attn_ref(x, conv_w, conv_b, ln_g, ln_b, qkv_w, qkv_b, bn_w1, bn_w2, temperature, proj_w, proj_b, mn_g, mn_b):
        import jax, jax.numpy as jnp
        import numpy as np
        import math
        B, L, D, H, R = (2, 256, 192, 12, 64)
        DH = D // H

        def layernorm(x, g, b, eps=1e-05):
            mu = jnp.mean(x, axis=-1, keepdims=True)
            var = jnp.mean((x - mu) ** 2, axis=-1, keepdims=True)
            return (x - mu) / jnp.sqrt(var + eps) * g + b

        def _reference_tuple_inner(x, conv_w, conv_b, ln_g, ln_b, qkv_w, qkv_b, bn_w1, bn_w2, temperature, proj_w, proj_b, mn_g, mn_b):
            Bx, Lx, Dx = x.shape
            xp = jnp.pad(x, ((0, 0), (2, 0), (0, 0)))
            conv = xp[:, 0:Lx] * conv_w[:, 0] + xp[:, 1:Lx + 1] * conv_w[:, 1] + xp[:, 2:Lx + 2] * conv_w[:, 2] + conv_b
            x_conv = x + conv
            xn = layernorm(x_conv, ln_g, ln_b)
            qkv = xn @ qkv_w.T + qkv_b
            q, k, v = jnp.split(qkv, 3, axis=-1)
            params = (jax.nn.silu(xn @ bn_w1.T) @ bn_w2.T).reshape(Bx, Lx, H, 5)
            sem_amp = jax.nn.sigmoid(params[..., 0])
            sem_phase = jnp.tanh(params[..., 1]) * math.pi
            ctx_amp = jax.nn.sigmoid(params[..., 2])
            ctx_phase = jnp.tanh(params[..., 3]) * math.pi
            decay = 0.3 + 0.65 * jax.nn.sigmoid(params[..., 4])
            gate = jax.nn.sigmoid(sem_amp * ctx_amp * jnp.cos(sem_phase - ctx_phase) * temperature[0])
            q_f = (jax.nn.elu(q) + 1.0).reshape(Bx, Lx, H, DH)
            k_f = (jax.nn.elu(k) + 1.0).reshape(Bx, Lx, H, DH)
            v_f = v.reshape(Bx, Lx, H, DH)
            one_minus = 1.0 - decay
            kv_input = jnp.einsum('blhd,blhe->blhde', k_f, v_f)
            kv_input = jnp.clip(kv_input * (gate * one_minus)[..., None, None], -5.0, 5.0)
            df = jnp.exp(jnp.cumsum(jnp.log(decay), axis=1))
            safe_df = df + 1e-08
            kv_states = jnp.cumsum(kv_input / safe_df[..., None, None], axis=1) * df[..., None, None]
            z = jnp.cumsum(k_f * one_minus[..., None] / safe_df[..., None], axis=1) * df[..., None]
            z = jnp.clip(z, -10000.0, 10000.0)
            out_num = jnp.einsum('blhd,blhde->blhe', q_f, kv_states)
            den = jnp.sum(q_f * z, axis=-1, keepdims=True) + 0.0001
            out = layernorm(out_num / den, mn_g, mn_b)
            y = out.reshape(Bx, Lx, Dx) @ proj_w.T + proj_b
            return (y, gate)
        return _reference_tuple_inner(x, conv_w, conv_b, ln_g, ln_b, qkv_w, qkv_b, bn_w1, bn_w2, temperature, proj_w, proj_b, mn_g, mn_b)[0]

    def _L0_ffn_ref(hidden_states, Wg, W1, b1, W2, b2):
        import jax, jax.numpy as jnp
        import numpy as np
        B, S, D, F, E = (2, 256, 192, 768, 8)
        b, s, d = hidden_states.shape
        e = W1.shape[0]
        x = hidden_states.reshape(-1, d)
        logits = x @ Wg
        probs = jax.nn.softmax(logits, axis=-1)
        gate = jnp.max(probs, axis=-1)
        expert_idx = jnp.argmax(probs, axis=-1)
        h = jax.nn.silu(jnp.einsum('td,edf->etf', x, W1) + b1[:, None, :])
        y = jnp.einsum('etf,efd->etd', h, W2) + b2[:, None, :]
        combine = jax.nn.one_hot(expert_idx, e, dtype=x.dtype) * gate[:, None]
        out = jnp.einsum('te,etd->td', combine, y)
        return out.reshape(b, s, d)
    h = _L0_tok_ref(x, L0_tok_proj_w, L0_tok_proj_b, L0_tok_cls_token, L0_tok_pos_embedding)
    h = jnp.concatenate([h, txt], axis=1)
    h = h + _L0_attn_ref(_layernorm(h, axis=-1), L0_attn_conv_w, L0_attn_conv_b, L0_attn_ln_g, L0_attn_ln_b, L0_attn_qkv_w, L0_attn_qkv_b, L0_attn_bn_w1, L0_attn_bn_w2, L0_attn_temperature, L0_attn_proj_w, L0_attn_proj_b, L0_attn_mn_g, L0_attn_mn_b)
    h = h + _L0_ffn_ref(_layernorm(h, axis=-1), L0_ffn_Wg, L0_ffn_W1, L0_ffn_b1, L0_ffn_W2, L0_ffn_b2)
    return h

_drawn_inputs = setup_inputs


def setup_inputs(seed=0):
    import zlib

    import numpy as np

    out = dict(_drawn_inputs(seed))
    spreads = {'L0_tok_proj_b': (0.0, 0.1),
     'L0_attn_conv_b': (0.0, 0.1),
     'L0_attn_ln_g': (1.0, 0.2),
     'L0_attn_ln_b': (0.0, 0.1),
     'L0_attn_qkv_b': (0.0, 0.1),
     'L0_attn_proj_b': (0.0, 0.1),
     'L0_attn_mn_g': (1.0, 0.2),
     'L0_attn_mn_b': (0.0, 0.1),
     'L0_ffn_b1': (0.0, 0.8),
     'L0_ffn_b2': (0.0, 0.532)}
    factors = {'L0_ffn_Wg': 3.079, 'L0_ffn_W1': 4.814, 'L0_ffn_W2': 4.454}
    for name, (base, spread) in spreads.items():
        noise = np.random.default_rng([zlib.crc32(name.encode()), seed]).standard_normal(out[name].shape)
        drawn = base * np.exp(spread * noise) if base else spread * noise
        out[name] = jnp.asarray(drawn.astype(out[name].dtype))
    for name, factor in factors.items():
        out[name] = (out[name] * factor).astype(out[name].dtype)
    return out
```

```python
from contextlib import ExitStack

import concourse.bass as bass
from concourse import mybir

F32 = mybir.dt.float32
ALU = mybir.AluOpType
ACT = mybir.ActivationFunctionType
AX = mybir.AxisListType

B = 16
NPATCH = 36
LP = NPATCH + 1
LT = 128
L = LP + LT
D = 192
KP = 768
H = 12
DH = D // H
R = 64
NG = 5
E = 8
FF = 768

P = 128
C = D // 2
KC = KP // P
PAIRS = B // 2
NT = 3 * PAIRS
HALF = 64
QK, V0, HID0, MEAN = 0, 2 * D, 3 * D, 3 * D + R
WCOLS = 3 * D + R
ident0, utt0, upp0, sel0, before0, ones0 = 0, P, 2 * P, 3 * P, 5 * P, 6 * P
CMAT = 7 * P
SLOT_TILES = (B * L + E * (P - 1)) // P
MAXN = -(-B * L // P)
ROW = D + 4
MEAN_AT, RSTD_AT, GATE_AT, ID_AT = D, D + 1, D + 2, D + 3
NOWHERE = 1 << 20
valid0 = 0
token0 = valid0 + NT
nowhere0 = token0 + NT
down0 = nowhere0 + NT
steps0 = down0 + E
tile0 = steps0 + E * MAXN
CSMALL = tile0 + SLOT_TILES * E


def wait_apart(eng, sem, value):
    if isinstance(value, int):
        eng.wait_ge(sem, value)
        return
    value = eng.to_reg(value)
    eng.wait_ge(sem, 1)
    eng.wait_ge(sem, value)


def early_fusion_layer(nc, patches, txt, tok_w, pos_rows, first_rows, conv_w, ln_gb, w_in, b_in, bn2, temp,
                       w_out, b_out, mn_gb, wg, w1, w2, b2, consts, counts, out, dbg=None):
    ds = bass.ds
    with ExitStack() as top:
        def sbuf(name, shape, dt=F32):
            return top.enter_context(nc.sbuf_tensor(name, shape, dt))

        cst = sbuf("cst", [P, CMAT])
        ident = cst[:, ident0:ident0 + P]
        u_txt = cst[:, utt0:utt0 + P]
        u_pre = cst[:, upp0:upp0 + P]
        prefix_of = [cst[:, sel0 + b * P:sel0 + (b + 1) * P] for b in range(2)]
        u_before = cst[:, before0:before0 + P]
        u_ones = cst[:, ones0:ones0 + P]
        rows = sbuf("rows", [P, NT, ROW])
        hid = rows[:, :, 0:D]
        logits = sbuf("logits", [P, NT, E])
        moments = sbuf("moments", [P, NT, 2])
        w1s = sbuf("w1s", [C + 1, E, 2, FF])
        empty = sbuf("empty", [P, ROW])
        sorted_rows = nc.dram_tensor("sorted_rows", (SLOT_TILES * P, ROW), F32, kind="Internal").ap()
        w1_in = top.enter_context(nc.semaphore("w1_in"))
        slots_clear = top.enter_context(nc.semaphore("slots_clear"))

        mid = top.enter_context(ExitStack())

        def sbuf(name, shape, dt=F32):
            return mid.enter_context(nc.sbuf_tensor(name, shape, dt))

        qk = sbuf("qk", [P, NT, 2 * D])
        val = sbuf("val", [P, NT, D])
        gates = sbuf("gates", [P, NT, H * NG])
        decay = sbuf("decay", [P, NT, H])
        gain_kv = sbuf("gain_kv", [P, NT, H])
        gain_z = sbuf("gain_z", [P, NT, H])
        clip_hi = sbuf("clip_hi", [P, NT, H])
        clip_lo = sbuf("clip_lo", [P, NT, H])

        with ExitStack() as ctx:
            def sb(name, shape):
                return ctx.enter_context(nc.sbuf_tensor(name, shape, F32))

            def ps(name, shape):
                return ctx.enter_context(nc.psum_tensor(name, shape, F32))

            def sem(name):
                return ctx.enter_context(nc.semaphore(name))

            tokw = sb("tokw", [P, KC, D])
            posb = sb("posb", [P, D])
            firstb = sb("firstb", [P, D])
            convs = sb("convs", [C, 2, 4])
            lng = sb("lng", [C, 2, 2])
            win = sb("win", [C, 2, WCOLS + 1])
            wgain = sb("wgain", [C, 2, WCOLS])
            bin_ = sb("bin_", [P, WCOLS])
            bin_raw = sb("bin_raw", [P, WCOLS])
            win_raw = sb("win_raw", [C, 2, WCOLS])
            ones_d = sb("ones_d", [C, P])
            lnb_wide = sb("lnb_wide", [C, 2, P])
            bn2s = sb("bn2s", [R, H * NG])
            pat = sb("pat", [P, 2, KC, P])
            neg_half = sb("neg_half", [P, 3])
            mv = sb("mv", [P, 3, 2])
            bst = sb("bst", [P, 3, 6])
            vare = sb("vare", [P, 3])
            rstd = sb("rstd", [P, 3])
            xa = sb("xa", [P, 3, D])
            xat = sb("xat", [C, 2, 2, L + 2])
            xct = sb("xct", [C, 2, 2, 2, L])
            xpre = sb("xpre", [C, 2, 2, P])
            xsq = sb("xsq", [C, 2, 2, 3 * P])
            stat = sb("stat", [P, 2, 2])
            nvar = sb("nvar", [P, 2])
            vare2 = sb("vare2", [P, 2])
            rstd2 = sb("rstd2", [P, 2])
            qkr = sb("qkr", [P, 2, 2 * D])
            qkm = sb("qkm", [P, 2, 2 * D])
            qke = sb("qke", [P, 2, 2 * D])
            hr = sb("hr", [P, 2, R])
            ht = sb("ht", [P, 2, R])
            hs = sb("hs", [P, 2, R])
            hst = sb("hst", [R, P])

            p_tok = ps("p_tok", [P, 512])
            p_tr = ps("p_tr", [P, 2, 512])
            p_qk = ps("p_qk", [P, 2, 512])
            p_v = ps("p_v", [P, 2, 512])
            p_h = ps("p_h", [P, 512])

            weights_in = sem("weights_in")
            small_in = sem("small_in")
            text_in = sem("text_in")
            patches_in = [sem(f"patches_in{u}") for u in range(2)]
            prep_v = sem("prep_v")
            prep_pe = sem("prep_pe")
            halves_set = sem("halves_set")
            w_ready = sem("w_ready")
            pads_zero = sem("pads_zero")
            tok_ready = sem("tok_ready")
            h_ready = sem("h_ready")
            st_done = sem("st_done")
            mv_ready = sem("mv_ready")
            vare_done = sem("vare_done")
            rstd_ready = sem("rstd_ready")
            xa_ready = sem("xa_ready")
            tr_ready = sem("tr_ready")
            xat_ready = sem("xat_ready")
            conv_first = sem("conv_first")
            conv_step = sem("conv_step")
            conv_ready = sem("conv_ready")
            xsq_ready = sem("xsq_ready")
            xpre_ready = sem("xpre_ready")
            proj_ready = sem("proj_ready")
            stat_copied = sem("stat_copied")
            nvar_ready = sem("nvar_ready")
            vare2_done = sem("vare2_done")
            rstd2_ready = sem("rstd2_ready")
            qk_raw = sem("qk_raw")
            banks_read = sem("banks_read")
            hid_raw = sem("hid_raw")
            qk_min = sem("qk_min")
            qk_exp = sem("qk_exp")
            hid_tanh = sem("hid_tanh")
            qk_done = sem("qk_done")
            hid_silu = sem("hid_silu")
            hid_tr = sem("hid_tr")
            hidt_ready = sem("hidt_ready")
            par_ready = sem("par_ready")
            par_read = sem("par_read")

            SMALL = 9

            def bodies(eng, body):
                with eng.Fori(0, PAIRS // 2 - 1) as i:
                    body(2 * i, 0, True)
                    body(2 * i + 1, 1, True)
                body(PAIRS - 2, 0, True)
                body(PAIRS - 1, 1, False)

            with nc.Block() as block:
                @block.sync
                def _(sp):
                    for u in range(2):
                        sp.dma_start(pat[:, u], patches[u]).then_inc(patches_in[u], 16)
                        if u == 0:
                            sp.dma_start(tokw[:], tok_w).then_inc(weights_in, 16)
                    sp.dma_start(win_raw[:], w_in).then_inc(weights_in, 16)
                    for e in range(E):
                        sp.dma_start(w1s[:, e], w1[:, e]).then_inc(w1_in, 16)
                    with sp.Fori(1, PAIRS // 2) as i:
                        for u in range(2):
                            sp.wait_ge(tok_ready, 2 * i + u - 1)
                            sp.dma_start(pat[:, u], patches[ds(2 * i + u, 1)].rearrange("o p c n -> p (o c) n")).then_inc(patches_in[u], 16)

                @block.scalar
                def _(act):
                    act.dma_start(cst[:], consts).then_inc(small_in, 16)
                    act.dma_start(posb[:], pos_rows).then_inc(small_in, 16)
                    act.dma_start(firstb[:], first_rows).then_inc(small_in, 16)
                    act.dma_start(convs[:], conv_w).then_inc(small_in, 16)
                    act.dma_start(lng[:], ln_gb).then_inc(small_in, 16)
                    act.dma_start(bin_raw[:], b_in).then_inc(small_in, 16)
                    act.dma_start(bn2s[:], bn2).then_inc(small_in, 16)
                    hv = hid.rearrange("p (g j) d -> p g j d", j=3)
                    tv = txt.rearrange("(g b) t d -> t g b d", b=2)
                    for b in range(2):
                        act.dma_start(hv[:, :, 1 + b, :], tv[:, :, b, :]).then_inc(text_in, 16)

                    def transposed(p, u):
                        act.wait_ge(tr_ready, p + 1)
                        act.wait_ge(conv_ready, 2 * p) if not isinstance(p, int) or p else None
                        for c in range(2):
                            nc.scalar.copy(xat[:, c, :, 2:2 + LP],
                                           p_tr[0:C, c, 0:P].rearrange("p (b t) -> p b t", b=2)[:, :, 0:LP]).then_inc(xat_ready, 1)
                            nc.scalar.copy(xat[:, c, :, 2 + LP:],
                                           p_tr[0:C, c, P:3 * P].rearrange("p (b t) -> p b t", b=2)).then_inc(xat_ready, 1)

                    def conv_last_tap(p, u, pb):
                        if pb is not None:
                            act.wait_ge(proj_ready, 3 * pb + 1)
                        act.wait_ge(xat_ready, 4 * p + 4)
                        for c in range(2):
                            nc.scalar.activation(xct[:, u, c], xat[:, c, :, 2:], ACT.Identity,
                                                 scale=convs[:, c, 2:3], bias=convs[:, c, 3:4]).then_inc(conv_first, 1)

                    def squares(p, u):
                        act.wait_ge(conv_ready, 2 * p + 2)
                        for c in range(2):
                            nc.scalar.activation(xsq[:, u, c, 0:P].rearrange("p (b t) -> p b t", b=2),
                                                 xct[:, u, c, :, 0:HALF], ACT.Square).then_inc(xsq_ready, 1)
                            nc.scalar.activation(xsq[:, u, c, P:].rearrange("p (b t) -> p b t", b=2),
                                                 xct[:, u, c, :, LP:], ACT.Square).then_inc(xsq_ready, 1)

                    def nonlinear(p, u, j):
                        s = (u + j) % 2
                        t = 3 * p + j
                        act.wait_ge(hid_raw, t + 1)
                        nc.scalar.activation(ht[:, s], hr[:, s], ACT.Tanh, scale=0.5).then_inc(hid_tanh, 1)
                        act.wait_ge(qk_min, t + 1)
                        nc.scalar.activation(qke[:, s], qkm[:, s], ACT.Exp).then_inc(qk_exp, 1)

                    def hidden_out(p, u, j):
                        t = 3 * p + j
                        act.wait_ge(hid_tr, t + 1)
                        nc.scalar.copy(hst[:], p_h[0:R, 0:P]).then_inc(hidt_ready, 1)
                        act.wait_ge(par_ready, t + 1)
                        nc.scalar.activation(gates[:, ds(t, 1), :], p_h[:, P:P + H * NG].rearrange("p (o n) -> p o n", o=1),
                                             ACT.Identity, scale=0.5).then_inc(par_read, 1)

                    def body(p, u, more):
                        if more:
                            transposed(p + 1, 1 - u)
                            conv_last_tap(p + 1, 1 - u, p)
                        nonlinear(p, u, 0)
                        nonlinear(p, u, 1)
                        hidden_out(p, u, 0)
                        nonlinear(p, u, 2)
                        hidden_out(p, u, 1)
                        if more:
                            squares(p + 1, 1 - u)
                        hidden_out(p, u, 2)

                    act.sem_inc(par_read, 1)
                    act.wait_ge(pads_zero, 4)
                    transposed(0, 0)
                    conv_last_tap(0, 0, None)
                    squares(0, 0)
                    bodies(act, body)

                @block.gpsimd
                def _(pool):
                    pool.wait_ge(pads_zero, 2)
                    pool.dma_start(sorted_rows.rearrange("(i p) c -> p i c", p=P),
                                   empty[:].unsqueeze(1).broadcast_to([P, SLOT_TILES, ROW])).then_inc(slots_clear, 16)
                    nc.gpsimd.memset(neg_half[:], -0.5).then_inc(halves_set, 1)
                    pool.wait_ge(halves_set, 1)

                    def first_norm(p):
                        wait_apart(pool, mv_ready, 3 * p + 3)
                        nc.gpsimd.tensor_scalar(vare[:], mv[:, :, 1], 1e-5, None, ALU.add).then_inc(vare_done, 1)
                        wait_apart(pool, vare_done, p + 1)
                        nc.gpsimd.tensor_tensor(rstd[:], vare[:], neg_half[:], ALU.pow).then_inc(rstd_ready, 1)

                    def second_norm(p, u, j):
                        s = (u + j) % 2
                        t = 3 * p + j
                        wait_apart(pool, nvar_ready, t + 1)
                        nc.gpsimd.tensor_scalar(vare2[:, s:s + 1], nvar[:, s:s + 1], -1.0, 1e-5, ALU.mult, ALU.add).then_inc(vare2_done, 1)
                        wait_apart(pool, vare2_done, t + 1)
                        nc.gpsimd.tensor_tensor(rstd2[:, s:s + 1], vare2[:, s:s + 1], neg_half[:, 0:1], ALU.pow).then_inc(rstd2_ready, 1)

                    def prefixes(p, u):
                        wait_apart(pool, conv_ready, 2 * p + 2)
                        nc.gpsimd.tensor_copy(xpre[:, u].rearrange("p c (b t) -> p c b t", b=2),
                                              xct[:, u, :, :, 0:HALF]).then_inc(xpre_ready, 1)

                    def body(p, u, more):
                        if more:
                            first_norm(p + 1)
                        for j in range(3):
                            second_norm(p, u, j)
                        if more:
                            prefixes(p + 1, 1 - u)

                    first_norm(0)
                    prefixes(0, 0)
                    bodies(pool, body)

                @block.vector
                def _(dve):
                    v = nc.vector
                    v.memset(empty[:, 0:ID_AT], 0.0).then_inc(pads_zero, 1)
                    v.memset(empty[:, ID_AT:], float(NOWHERE)).then_inc(pads_zero, 1)
                    v.memset(xat[:, :, :, 0:2], 0.0).then_inc(pads_zero, 1)
                    v.memset(ones_d[:], 1.0 / D).then_inc(prep_v, 1)
                    dve.wait_ge(small_in, 16 * 7)
                    v.tensor_tensor(posb[:], posb[:], firstb[:], ALU.add).then_inc(prep_v, 1)
                    v.tensor_scalar(convs[:, :, 2], convs[:, :, 2], 1.0, None, ALU.add).then_inc(pads_zero, 1)
                    dve.wait_ge(prep_v, 2)
                    for c in range(2):
                        v.tensor_scalar(lnb_wide[:, c], ones_d[:], float(D), lng[:, c, 1:2], ALU.mult, ALU.mult).then_inc(prep_v, 1)

                    def stats(p):
                        dve.wait_ge(tok_ready, p + 1)
                        v.tensor_tensor(hid[:, ds(3 * p, 1), :], p_tok[:, 0:D].rearrange("p (o d) -> p o d", o=1),
                                        posb[:].rearrange("p (o d) -> p o d", o=1), ALU.add).then_inc(h_ready, 1)
                        for j in (1, 2, 0):
                            if j == 0:
                                wait_apart(dve, h_ready, p + 1)
                            v.bn_stats(bst[:, j], hid[:, ds(3 * p + j, 1), :].rearrange("p o d -> p (o d)")).then_inc(st_done, 1)
                        wait_apart(dve, st_done, 3 * p + 3)
                        for j in range(3):
                            v.bn_aggr(mv[:, j], bst[:, j]).then_inc(mv_ready, 1)

                    def norm(p):
                        dve.wait_ge(rstd_ready, p + 1)
                        for j in range(3):
                            v.tensor_scalar(xa[:, j:j + 1], hid[:, ds(3 * p + j, 1), :], mv[:, j, 0:1], rstd[:, j:j + 1],
                                            ALU.subtract, ALU.mult).then_inc(xa_ready, 1)

                    def conv(p, u):
                        dve.wait_ge(conv_first, 2 * p + 2)
                        for c in range(2):
                            v.scalar_tensor_tensor(xct[:, u, c], xat[:, c, :, 1:1 + L], convs[:, c, 1:2], xct[:, u, c],
                                                   ALU.mult, ALU.add).then_inc(conv_step, 1)
                        for c in range(2):
                            dve.wait_ge(conv_step, 2 * p + 1 + c)
                            v.scalar_tensor_tensor(xct[:, u, c], xat[:, c, :, 0:L], convs[:, c, 0:1], xct[:, u, c],
                                                   ALU.mult, ALU.add).then_inc(conv_ready, 1)

                    def second_stats(p, u, j):
                        s = (u + j) % 2
                        t = 3 * p + j
                        dve.wait_ge(proj_ready, t + 1)
                        v.tensor_copy(stat[:, s], p_v[:, s, D + R:D + R + 2]).then_inc(stat_copied, 1)
                        dve.wait_ge(stat_copied, t + 1)
                        v.scalar_tensor_tensor(nvar[:, s:s + 1], stat[:, s, 0:1], stat[:, s, 0:1], stat[:, s, 1:2],
                                               ALU.mult, ALU.subtract).then_inc(nvar_ready, 1)

                    def scaled(p, u, j):
                        s = (u + j) % 2
                        t = 3 * p + j
                        dve.wait_ge(rstd2_ready, t + 1)
                        dve.wait_ge(qk_done, t + 1)
                        r = rstd2[:, s:s + 1]
                        v.scalar_tensor_tensor(hr[:, s], p_v[:, s, D:D + R], r, bin_[:, HID0:HID0 + R], ALU.mult, ALU.add).then_inc(hid_raw, 1)
                        v.scalar_tensor_tensor(qkr[:, s], p_qk[:, s, 0:2 * D], r, bin_[:, 0:2 * D], ALU.mult, ALU.add).then_inc(qk_raw, 1)
                        v.scalar_tensor_tensor(val[:, ds(t, 1), :], p_v[:, s:s + 1, 0:D], r,
                                               bin_[:, V0:V0 + D].rearrange("p (o d) -> p o d", o=1), ALU.mult, ALU.add).then_inc(banks_read, 1)
                        dve.wait_ge(qk_raw, t + 1)
                        v.tensor_scalar(qkm[:, s], qkr[:, s], 0.0, None, ALU.min).then_inc(qk_min, 1)

                    def finished(p, u, j):
                        s = (u + j) % 2
                        t = 3 * p + j
                        dve.wait_ge(hid_tanh, t + 1)
                        v.scalar_tensor_tensor(hs[:, s], ht[:, s], 1.0, hr[:, s], ALU.add, ALU.mult).then_inc(hid_silu, 1)
                        dve.wait_ge(qk_exp, t + 1)
                        v.scalar_tensor_tensor(qk[:, ds(t, 1), :], qkr[:, s:s + 1], 0.0, qke[:, s:s + 1], ALU.max, ALU.add).then_inc(qk_done, 1)

                    def body(p, u, more):
                        if more:
                            stats(p + 1)
                        second_stats(p, u, 0)
                        if more:
                            norm(p + 1)
                        second_stats(p, u, 1)
                        scaled(p, u, 0)
                        second_stats(p, u, 2)
                        scaled(p, u, 1)
                        finished(p, u, 0)
                        scaled(p, u, 2)
                        finished(p, u, 1)
                        if more:
                            conv(p + 1, 1 - u)
                        finished(p, u, 2)

                    dve.wait_ge(text_in, 32)
                    dve.wait_ge(prep_v, 2)
                    v.sem_inc(banks_read, 2)
                    v.sem_inc(qk_done, 2)
                    stats(0)
                    norm(0)
                    dve.wait_ge(weights_in, 32)
                    for c in range(2):
                        v.tensor_scalar(wgain[:, c], win_raw[:, c], lng[:, c, 0:1], None, ALU.mult).then_inc(prep_v, 1)
                    v.memset(win[:, :, MEAN:MEAN + 1], 1.0 / D).then_inc(w_ready, 1)
                    dve.wait_ge(prep_pe, 4)
                    for c in range(2):
                        v.tensor_tensor(win[:, c, 0:512], wgain[:, c, 0:512], p_qk[0:C, 0, 0:512], ALU.subtract).then_inc(w_ready, 1)
                        v.tensor_tensor(win[:, c, 512:WCOLS], wgain[:, c, 512:WCOLS], p_qk[0:C, 1, 0:WCOLS - 512], ALU.subtract).then_inc(w_ready, 1)
                    v.tensor_tensor(bin_[:, 0:512], bin_raw[:, 0:512], p_v[:, 0, 0:512], ALU.add).then_inc(w_ready, 1)
                    v.tensor_tensor(bin_[:, 512:WCOLS], bin_raw[:, 512:WCOLS], p_v[:, 1, 0:WCOLS - 512], ALU.add).then_inc(w_ready, 1)
                    conv(0, 0)
                    dve.wait_ge(w_ready, 7)
                    bodies(dve, body)

                @block.tensor
                def _(pe):
                    mm = nc.tensor.matmul

                    def tokens(p, u, turn):
                        pe.wait_ge(patches_in[u], 16 * turn + 16)
                        for k in range(KC):
                            last = mm(p_tok[:, 0:D], pat[:, u, k], tokw[:, k], start=(k == 0), stop=(k == KC - 1))
                        last.then_inc(tok_ready, 1)

                    def transposes(p):
                        pe.wait_ge(xa_ready, 3 * p + 3)
                        for c in range(2):
                            for j in range(3):
                                last = nc.tensor.transpose(p_tr[0:C, c, j * P:(j + 1) * P], xa[:, j, c * C:(c + 1) * C], ident)
                        last.then_inc(tr_ready, 1)

                    def project(p, u, j):
                        s = (u + j) % 2
                        t = 3 * p + j
                        pe.wait_ge(banks_read, t + 1)
                        for c in range(2):
                            rows = [xpre[:, u, c], xct[:, u, c, 0, LP:], xct[:, u, c, 1, LP:]][j]
                            mm(p_qk[:, s, 0:2 * D], rows, win[:, c, 0:2 * D], start=(c == 0), stop=(c == 1))
                        for c in range(2):
                            rows = [xpre[:, u, c], xct[:, u, c, 0, LP:], xct[:, u, c, 1, LP:]][j]
                            mm(p_v[:, s, 0:D + R + 1], rows, win[:, c, V0:MEAN + 1], start=(c == 0), stop=(c == 1))
                        for c in range(2):
                            rows = xsq[:, u, c, j * P:(j + 1) * P]
                            last = mm(p_v[:, s, D + R + 1:D + R + 2], rows, win[:, c, MEAN:MEAN + 1], start=False, stop=(c == 1), skip_group_check=True)
                        last.then_inc(proj_ready, 1)

                    def gate_params(p, u, j):
                        s = (u + j) % 2
                        t = 3 * p + j
                        wait_apart(pe, par_read, t + 1)
                        pe.wait_ge(hid_silu, t + 1)
                        nc.tensor.transpose(p_h[0:R, 0:P], hs[:, s], ident).then_inc(hid_tr, 1)
                        pe.wait_ge(hidt_ready, t + 1)
                        mm(p_h[:, P:P + H * NG], hst[:], bn2s[:], start=True, stop=True).then_inc(par_ready, 1)

                    def body(p, u, more):
                        if more:
                            pe.wait_ge(h_ready, p + 1)
                            tokens(p + 1, 1 - u, (p + 1) // 2)
                        pe.wait_ge(xsq_ready, 4 * p + 4)
                        pe.wait_ge(xpre_ready, p + 1)
                        project(p, u, 0)
                        if more:
                            pe.wait_ge(xat_ready, 4 * p + 4)
                            transposes(p + 1)
                        project(p, u, 1)
                        project(p, u, 2)
                        for j in range(3):
                            gate_params(p, u, j)

                    pe.wait_ge(weights_in, 32)
                    pe.wait_ge(small_in, 16 * 7)
                    tokens(0, 0, 0)
                    transposes(0)
                    pe.wait_ge(prep_v, 6)
                    for half, (a, b) in enumerate(((0, 512), (512, WCOLS))):
                        for c in range(2):
                            last = mm(p_qk[0:C, half, 0:b - a], ones_d[:, 0:C], wgain[:, c, a:b], start=(c == 0), stop=(c == 1))
                        last.then_inc(prep_pe, 1)
                    for half, (a, b) in enumerate(((0, 512), (512, WCOLS))):
                        for c in range(2):
                            last = mm(p_v[:, half, 0:b - a], lnb_wide[:, c], win_raw[:, c, a:b], start=(c == 0), stop=(c == 1))
                        last.then_inc(prep_pe, 1)
                    pe.wait_ge(w_ready, 7)
                    bodies(pe, body)

        with ExitStack() as ctx:
            def sb(name, shape):
                return ctx.enter_context(nc.sbuf_tensor(name, shape, F32))

            def sem(name):
                return ctx.enter_context(nc.semaphore(name))

            tanhs = sb("tanhs", [P, NG, NT, H])
            phase = sb("phase", [P, NT, H])
            sine = sb("sine", [P, NT, H])
            cosine = sb("cosine", [P, NT, H])
            amp = sb("amp", [P, NT, H])
            amps = sb("amps", [P, NT, H])
            gate = sb("gate", [P, NT, H])
            rate = sb("rate", [P, NT, H])
            log_rate = sb("log_rate", [P, NT, H])
            keep = sb("keep", [P, NT, H])
            safe = sb("safe", [P, NT, H])
            inv_df = sb("inv_df", [P, NT, H])
            half_temp = sb("half_temp", [P, 1])
            p_sum = ctx.enter_context(nc.psum_tensor("p_sum", [P, 512], F32))
            temp_in, tanh_done, steps, sine_done, rate_log, gate_tanh, sums_ready, df_ready = (
                sem(x) for x in ("temp_in", "tanh_done", "steps", "sine_done", "rate_log", "gate_tanh", "sums_ready", "df_ready"))

            with nc.Block() as block:
                @block.sync
                def _(sp):
                    sp.dma_start(half_temp[:], temp).then_inc(temp_in, 16)

                @block.scalar
                def _(act):
                    raw = gates[:].rearrange("p t (h n) -> p n t h", n=NG)
                    for n in (4, 1, 3, 0, 2):
                        nc.scalar.activation(tanhs[:, n], raw[:, n], ACT.Tanh, scale=1.0 if n % 2 else 0.5).then_inc(tanh_done, 1)
                    act.wait_ge(steps, 3)
                    nc.scalar.activation(sine[:], phase[:], ACT.Sin, scale=1.5707962).then_inc(sine_done, 1)
                    act.wait_ge(steps, 8)
                    nc.scalar.activation(gate[:], amps[:], ACT.Tanh, scale=half_temp[:, 0:1]).then_inc(gate_tanh, 1)
                    act.wait_ge(steps, 1)
                    nc.scalar.activation(log_rate[:], rate[:], ACT.Ln).then_inc(rate_log, 1)
                    act.wait_ge(sums_ready, 1)
                    nc.scalar.activation(decay[:], p_sum[:, 0:NT * H].rearrange("p (t h) -> p t h", h=H), ACT.Exp).then_inc(df_ready, 1)

                @block.tensor
                def _(pe):
                    pe.wait_ge(rate_log, 1)
                    of = log_rate[:].rearrange("p (g j) h -> p j g h", j=3)
                    to = p_sum[:, 0:NT * H].rearrange("p (g j h) -> p j g h", j=3, h=H)
                    nc.tensor.matmul(to[:, 0], u_pre, of[:, 0], start=True, stop=True, skip_group_check=True)
                    for b in range(2):
                        nc.tensor.matmul(to[:, 1 + b], u_txt, of[:, 1 + b], start=False, stop=False, skip_group_check=True)
                        last = nc.tensor.matmul(to[:, 1 + b], prefix_of[b], of[:, 0], start=False, stop=True, skip_group_check=True)
                    last.then_inc(sums_ready, 1)

                @block.vector
                def _(dve):
                    v = nc.vector

                    def step(n, ins):
                        ins.then_inc(steps, 1)
                        dve.wait_ge(steps, n)

                    dve.wait_ge(tanh_done, 1)
                    step(1, v.tensor_scalar(rate[:], tanhs[:, 4], 0.325, 0.625, ALU.mult, ALU.add))
                    step(2, v.tensor_scalar(keep[:], rate[:], -1.0, 1.0, ALU.mult, ALU.add))
                    dve.wait_ge(tanh_done, 3)
                    step(3, v.tensor_tensor(phase[:], tanhs[:, 1], tanhs[:, 3], ALU.subtract))
                    dve.wait_ge(tanh_done, 5)
                    step(4, v.tensor_scalar(amp[:], tanhs[:, 0], 0.5, 0.5, ALU.mult, ALU.add))
                    step(5, v.tensor_scalar(cosine[:], tanhs[:, 2], 0.5, 0.5, ALU.mult, ALU.add))
                    step(6, v.tensor_tensor(amp[:], amp[:], cosine[:], ALU.mult))
                    dve.wait_ge(temp_in, 16)
                    dve.wait_ge(sine_done, 1)
                    v.tensor_scalar(half_temp[:], half_temp[:], 0.5, None, ALU.mult)
                    step(7, v.tensor_tensor(cosine[:], amp[:], sine[:], ALU.mult))
                    v.tensor_tensor(cosine[:], cosine[:], sine[:], ALU.mult).then_inc(temp_in, 1)
                    dve.wait_ge(temp_in, 17)
                    step(8, v.scalar_tensor_tensor(amps[:], cosine[:], -2.0, amp[:], ALU.mult, ALU.add))
                    dve.wait_ge(df_ready, 1)
                    step(9, v.tensor_scalar(safe[:], decay[:], 1e-8, None, ALU.add))
                    step(10, v.reciprocal(inv_df[:], safe[:]))
                    v.tensor_scalar(clip_hi[:], inv_df[:], 5.0, None, ALU.mult).then_inc(steps, 1)
                    v.tensor_scalar(clip_lo[:], inv_df[:], -5.0, None, ALU.mult).then_inc(steps, 1)
                    step(13, v.tensor_tensor(gain_z[:], keep[:], inv_df[:], ALU.mult))
                    dve.wait_ge(gate_tanh, 1)
                    step(14, v.tensor_scalar(gate[:], gate[:], 0.5, 0.5, ALU.mult, ALU.add))
                    step(15, v.tensor_tensor(gain_kv[:], gate[:], gain_z[:], ALU.mult))

        with ExitStack() as ctx:
            def sb(name, shape):
                return ctx.enter_context(nc.sbuf_tensor(name, shape, F32))

            def ps(name, shape):
                return ctx.enter_context(nc.psum_tensor(name, shape, F32))

            def sem(name):
                return ctx.enter_context(nc.semaphore(name))

            HG = 4
            NHG = H // HG
            UC = HG * DH * DH
            wout_raw = sb("wout_raw", [C, 2, D])
            wout = sb("wout", [C, 2, D])
            mn = sb("mn", [C, 2])
            mnb_wide = sb("mnb_wide", [C, P])
            bout = sb("bout", [P, D])
            wg_raw = sb("wg_raw", [C, 2, E])
            wgc = sb("wgc", [C, 2, E])
            mean_w = sb("mean_w", [C, P])
            k_kv = sb("k_kv", [P, 3, D])
            k_z = sb("k_z", [P, 3, D])
            z = sb("z", [P, 3, D])
            zq = sb("zq", [P, 3, D])
            den = sb("den", [P, 3, H])
            den1 = sb("den1", [P, 3, H])
            rden = sb("rden", [P, 3, H])
            ratio = sb("ratio", [P, 3, H])
            outer = sb("outer", [P, 2, 3, UC])
            prod = sb("prod", [P, 2, UC])
            num = sb("num", [P, 3, D])
            att = sb("att", [P, 3, D])
            sums = sb("sums", [P, 3, H])
            means = sb("means", [P, 3, H])
            centred = sb("centred", [P, 3, D])
            sq = sb("sq", [P, 3, D])
            var = sb("var", [P, 3, H])
            var_eps = sb("var_eps", [P, 3, H])
            neg_half = sb("neg_half2", [P, 3, H])
            rstd = sb("rstd3", [P, 3, H])
            attn = sb("attn", [P, 3, D])
            attn_t = sb("attn_t", [C, 2, P])
            hid_t = sb("hid_t", [C, 2, P])
            new_hid = sb("new_hid", [P, 3, D])
            bst = sb("bst2", [P, 3, 6])
            mv = sb("mv2", [P, 3, 2])

            p_z = ps("p_z", [P, 2, 512])
            p_s = ps("p_s", [P, 2, 1024])
            p_t = ps("p_t", [P, 512])
            p_o = ps("p_o", [P, 512])

            (small_in, prep, prep_pe, fold, k_ready, z_ready, z_step, den_step, ratio_ready, outer_made, outer_ready,
             state_ready, prod_ready, state_read, num_ready, att_step, sq_ready, var_ready, var_step, rstd_ready,
             attn_ready, att_tr, attn_t_ready, proj_ready, hid_ready, st_done, mv_ready, hid_tr, hid_t_ready,
             logit_ready, logit_read) = (sem(x) for x in (
                 "c_small_in", "c_prep", "c_prep_pe", "c_fold", "k_ready", "z_ready", "z_step", "den_step", "ratio_ready",
                 "outer_made", "outer_ready", "state_ready", "prod_ready", "state_read", "num_ready", "att_step",
                 "sq_ready", "var_ready", "var_step", "c_rstd_ready", "attn_ready", "att_tr", "attn_t_ready",
                 "c_proj_ready", "hid_ready", "c_st_done", "c_mv_ready", "c_hid_tr", "hid_t_ready", "logit_ready",
                 "logit_read"))

            def per_head(ap):
                return ap.rearrange("p j (h d) -> p (j h) d", d=DH)

            def wide(ap, n):
                return ap.rearrange("p j h -> p (j h)").unsqueeze(2).broadcast_to([P, ap.shape[1] * ap.shape[2], n])

            with nc.Block() as block:
                @block.sync
                def _(sp):
                    sp.dma_start(wout_raw[:], w_out).then_inc(small_in, 16)
                    sp.dma_start(mn[:], mn_gb).then_inc(small_in, 16)
                    sp.dma_start(bout[:], b_out).then_inc(small_in, 16)
                    sp.dma_start(wg_raw[:], wg).then_inc(small_in, 16)

                @block.gpsimd
                def _(pool):
                    g = nc.gpsimd
                    g.memset(neg_half[:], -0.5).then_inc(prep, 1)
                    pool.wait_ge(fold, 4)
                    with pool.Fori(0, NT) as t:
                        g.tensor_tensor(hid[:, ds(t, 1), :], hid[:, ds(t, 1), :], bout[:].unsqueeze(1), ALU.add).then_inc(prep, 1)
                    pool.wait_ge(prep, NT + 1)
                    with pool.Fori(0, PAIRS) as p:
                        pool.wait_ge(state_read, 9 * p + 1)
                        kk = qk[:, ds(3 * p, 3), D:2 * D].rearrange("p j (h d) -> p j h d", d=DH)
                        g.tensor_tensor(k_z[:].rearrange("p j (h d) -> p j h d", d=DH), kk,
                                        gain_z[:, ds(3 * p, 3), :].unsqueeze(3).broadcast_to([P, 3, H, DH]), ALU.mult).then_inc(k_ready, 1)
                        g.tensor_tensor(k_kv[:].rearrange("p j (h d) -> p j h d", d=DH), kk,
                                        gain_kv[:, ds(3 * p, 3), :].unsqueeze(3).broadcast_to([P, 3, H, DH]), ALU.mult).then_inc(k_ready, 1)
                        wait_apart(pool, var_ready, p + 1)
                        g.tensor_scalar(var_eps[:], var[:], 1.0 / DH, 1e-5, ALU.mult, ALU.add).then_inc(var_step, 1)
                        wait_apart(pool, var_step, p + 1)
                        g.tensor_tensor(rstd[:], var_eps[:], neg_half[:], ALU.pow).then_inc(rstd_ready, 1)

                @block.scalar
                def _(act):
                    with act.Fori(0, PAIRS) as p:
                        act.wait_ge(att_step, 4 * p + 4)
                        nc.scalar.activation(sq[:], centred[:], ACT.Square).then_inc(sq_ready, 1)
                        for j in range(3):
                            act.wait_ge(att_tr, 3 * p + j + 1)
                            nc.scalar.copy(attn_t[:], p_t[0:C, 0:2 * P].rearrange("p (c t) -> p c t", c=2)).then_inc(attn_t_ready, 1)
                            act.wait_ge(hid_tr, 3 * p + j + 1)
                            nc.scalar.copy(hid_t[:], p_t[0:C, 0:2 * P].rearrange("p (c t) -> p c t", c=2)).then_inc(hid_t_ready, 1)

                @block.tensor
                def _(pe):
                    mm = nc.tensor.matmul
                    pe.wait_ge(fold, 3)
                    mm(p_z[:, 0, 0:D], mnb_wide[:], wout_raw[:, 0], start=True, stop=False)
                    mm(p_z[:, 0, 0:D], mnb_wide[:], wout_raw[:, 1], start=False, stop=True).then_inc(prep_pe, 1)
                    mm(p_z[0:C, 1, 0:E], mean_w[:, 0:C], wg_raw[:, 0], start=True, stop=False)
                    mm(p_z[0:C, 1, 0:E], mean_w[:, 0:C], wg_raw[:, 1], start=False, stop=True).then_inc(prep_pe, 1)
                    pe.wait_ge(fold, 6)
                    with pe.Fori(0, PAIRS) as p:
                        pe.wait_ge(k_ready, 2 * p + 1)
                        pe.wait_ge(z_step, 4 * p + 4)
                        mm(p_z[:, 0, 0:D], u_pre, k_z[:, 0], start=True, stop=True, skip_group_check=True)
                        mm(p_z[:, 0, D:2 * D], u_txt, k_z[:, 1], start=True, stop=False, skip_group_check=True)
                        mm(p_z[:, 0, D:2 * D], prefix_of[0], k_z[:, 0], start=False, stop=True, skip_group_check=True).then_inc(z_ready, 1)
                        mm(p_z[:, 1, 0:D], u_txt, k_z[:, 2], start=True, stop=False)
                        mm(p_z[:, 1, 0:D], prefix_of[1], k_z[:, 0], start=False, stop=True).then_inc(z_ready, 1)
                        for g in range(NHG):
                            for j in range(3):
                                n = 3 * g + j
                                pe.wait_ge(outer_ready, HG * (9 * p + n + 1))
                                pe.wait_ge(state_read, 9 * p + 1 + max(n - 1, 0))
                                for half in range(2):
                                    cols = slice(512 * half, 512 * half + 512)
                                    last = mm(p_s[:, n % 2, cols], u_txt if j else u_pre, outer[:, g % 2, j, cols], start=True, stop=(j == 0))
                                    if j:
                                        last = mm(p_s[:, n % 2, cols], prefix_of[j - 1], outer[:, g % 2, 0, cols], start=False, stop=True)
                                last.then_inc(state_ready, 1)
                        wait_apart(pe, attn_ready, p + 1)
                        for j in range(3):
                            t = 3 * p + j
                            wait_apart(pe, logit_read, t + 1)
                            for c in range(2):
                                last = nc.tensor.transpose(p_t[0:C, c * P:(c + 1) * P], attn[:, j, c * C:(c + 1) * C], ident)
                            last.then_inc(att_tr, 1)
                            pe.wait_ge(attn_t_ready, t + 1)
                            for c in range(2):
                                last = mm(p_o[:, 0:D], attn_t[:, c], wout[:, c], start=(c == 0), stop=(c == 1))
                            last.then_inc(proj_ready, 1)
                            wait_apart(pe, hid_ready, t + 1)
                            for c in range(2):
                                last = nc.tensor.transpose(p_t[0:C, c * P:(c + 1) * P], new_hid[:, j, c * C:(c + 1) * C], ident)
                            last.then_inc(hid_tr, 1)
                            pe.wait_ge(hid_t_ready, t + 1)
                            for c in range(2):
                                last = mm(p_o[:, 0:E], hid_t[:, c], wgc[:, c], start=(c == 0), stop=(c == 1))
                            last.then_inc(logit_ready, 1)

                @block.vector
                def _(dve):
                    v = nc.vector
                    dve.wait_ge(small_in, 64)
                    v.memset(mean_w[:], 1.0 / D).then_inc(fold, 1)
                    v.tensor_copy(mnb_wide[:], mn[:, 1:2].broadcast_to([C, P])).then_inc(fold, 1)
                    v.tensor_scalar(wout[:].rearrange("p c d -> p (c d)"), wout_raw[:].rearrange("p c d -> p (c d)"), mn[:, 0:1], None, ALU.mult).then_inc(fold, 1)
                    dve.wait_ge(prep_pe, 2)
                    v.tensor_tensor(bout[:], bout[:], p_z[:, 0, 0:D], ALU.add).then_inc(fold, 1)
                    for c in range(2):
                        v.tensor_tensor(wgc[:, c], wg_raw[:, c], p_z[0:C, 1, 0:E], ALU.subtract).then_inc(fold, 1)
                    v.sem_inc(z_step, 4)
                    v.sem_inc(state_read, 1)
                    v.sem_inc(logit_read, 1)

                    with dve.Fori(0, PAIRS) as p:
                        def products(g):
                            for j in range(3):
                                n = 3 * g + j
                                hs = slice(g * HG * DH, (g + 1) * HG * DH)
                                kk = k_kv[:, j, hs].rearrange("p (h d) -> p h d", d=DH).unsqueeze(3).broadcast_to([P, HG, DH, DH])
                                vv = val[:, ds(3 * p + j, 1), hs].rearrange("p o (h e) -> p (o h) e", e=DH).unsqueeze(2).broadcast_to([P, HG, DH, DH])
                                o = outer[:, g % 2, j].rearrange("p (h d e) -> p h d e", d=DH, e=DH)
                                v.tensor_tensor(o, kk, vv, ALU.mult).then_inc(outer_made, 1)
                            for j in range(3):
                                n = 3 * g + j
                                wait_apart(dve, outer_made, 9 * p + n + 1)
                                for h in range(HG):
                                    head = g * HG + h
                                    hi, lo = (x[:, ds(3 * p + j, 1), head:head + 1].rearrange("p a b -> p (a b)") for x in (clip_hi, clip_lo))
                                    o = outer[:, g % 2, j, h * DH * DH:(h + 1) * DH * DH]
                                    v.tensor_scalar(o, o, hi, lo, ALU.min, ALU.max).then_inc(outer_ready, 1)

                        def contract(g):
                            for j in range(3):
                                n = 3 * g + j
                                hs = slice(g * HG * DH, (g + 1) * HG * DH)
                                dve.wait_ge(state_ready, 9 * p + n + 1)
                                qq = qk[:, ds(3 * p + j, 1), hs].rearrange("p o (h d) -> p (o h) d", d=DH).unsqueeze(3).broadcast_to([P, HG, DH, DH])
                                st = p_s[:, n % 2].rearrange("p (h d e) -> p h d e", d=DH, e=DH)
                                pr = prod[:, n % 2].rearrange("p (h d e) -> p h d e", d=DH, e=DH)
                                v.tensor_tensor(pr, st, qq, ALU.mult).then_inc(state_read, 1)
                                wait_apart(dve, state_read, 9 * p + n + 2)
                                v.tensor_reduce(num[:, j, hs].rearrange("p (h e) -> p h e", e=DH), prod[:, n % 2].rearrange("p (h d e) -> p h e d", d=DH, e=DH),
                                                AX.X, ALU.add).then_inc(num_ready, 1)

                        dve.wait_ge(k_ready, 2 * p + 2)
                        products(0)
                        dec = decay[:, ds(3 * p, 3), :]
                        for b in range(2):
                            js = slice(0, 2) if b == 0 else slice(2, 3)
                            n = 2 - b
                            dve.wait_ge(z_ready, 2 * p + b + 1)
                            v.tensor_tensor(per_head(z[:, js]), p_z[:, b, 0:n * D].rearrange("p (h d) -> p h d", d=DH),
                                            wide(decay[:, ds(3 * p + 2 * b, n), :], DH), ALU.mult).then_inc(z_step, 1)
                        wait_apart(dve, z_step, 4 * p + 6)
                        v.scalar_tensor_tensor(zq[:], z[:], 1e4, qk[:, ds(3 * p, 3), 0:D], ALU.min, ALU.mult).then_inc(z_step, 1)
                        wait_apart(dve, z_step, 4 * p + 7)
                        v.tensor_reduce(den[:].rearrange("p j h -> p (j h)"), per_head(zq[:]), AX.X, ALU.add).then_inc(z_step, 1)
                        wait_apart(dve, z_step, 4 * p + 8)
                        v.tensor_scalar(den1[:], den[:], 1e-4, None, ALU.add).then_inc(den_step, 1)
                        products(1)
                        wait_apart(dve, den_step, 2 * p + 1)
                        v.reciprocal(rden[:], den1[:]).then_inc(den_step, 1)
                        contract(0)
                        wait_apart(dve, den_step, 2 * p + 2)
                        v.tensor_tensor(ratio[:], rden[:], dec, ALU.mult).then_inc(ratio_ready, 1)
                        products(2)
                        contract(1)
                        contract(2)
                        wait_apart(dve, num_ready, 9 * p + 9)
                        v.tensor_tensor(per_head(att[:]), per_head(num[:]), wide(ratio[:], DH), ALU.mult).then_inc(att_step, 1)
                        wait_apart(dve, att_step, 4 * p + 1)
                        v.tensor_reduce(sums[:].rearrange("p j h -> p (j h)"), per_head(att[:]), AX.X, ALU.add).then_inc(att_step, 1)
                        wait_apart(dve, att_step, 4 * p + 2)
                        v.tensor_scalar(means[:], sums[:], 1.0 / DH, None, ALU.mult).then_inc(att_step, 1)
                        wait_apart(dve, att_step, 4 * p + 3)
                        v.tensor_tensor(per_head(centred[:]), per_head(att[:]), wide(means[:], DH), ALU.subtract).then_inc(att_step, 1)
                        dve.wait_ge(sq_ready, p + 1)
                        v.tensor_reduce(var[:].rearrange("p j h -> p (j h)"), per_head(sq[:]), AX.X, ALU.add).then_inc(var_ready, 1)
                        dve.wait_ge(rstd_ready, p + 1)
                        v.tensor_tensor(per_head(attn[:]), per_head(centred[:]), wide(rstd[:], DH), ALU.mult).then_inc(attn_ready, 1)
                        for j in range(3):
                            t = 3 * p + j
                            dve.wait_ge(proj_ready, t + 1)
                            v.tensor_tensor(new_hid[:, j:j + 1], hid[:, ds(t, 1), :], p_o[:, 0:D].unsqueeze(1), ALU.add).then_inc(hid_ready, 1)
                            wait_apart(dve, hid_ready, t + 1)
                            v.tensor_copy(hid[:, ds(t, 1), :], new_hid[:, j:j + 1]).then_inc(st_done, 1)
                            v.bn_stats(bst[:, j], new_hid[:, j]).then_inc(st_done, 1)
                            wait_apart(dve, st_done, 2 * t + 2)
                            v.bn_aggr(mv[:, j], bst[:, j]).then_inc(mv_ready, 1)
                            dve.wait_ge(logit_ready, t + 1)
                            v.tensor_copy(logits[:, ds(t, 1), :], p_o[:, 0:E].unsqueeze(1)).then_inc(logit_read, 1)
                        wait_apart(dve, mv_ready, 4 * p + 3)
                        v.tensor_copy(moments[:, ds(3 * p, 3), :], mv[:]).then_inc(mv_ready, 1)

        if dbg:
            dump(nc, dbg, dict(hid=hid, logits=logits, moments=moments, decay=decay, qk=qk, val=val))
        mid.close()

        def sbuf(name, shape, dt=F32):
            return top.enter_context(nc.sbuf_tensor(name, shape, dt))

        w2s = sbuf("w2s", [P, E, KC, D])
        b2s = sbuf("b2s", [P, E, D])
        expert_of = sbuf("expert_of", [P, SLOT_TILES], mybir.dt.int32)
        w2_in = top.enter_context(nc.semaphore("w2_in"))
        with ExitStack() as ctx:
            def sb(name, shape, dt=F32):
                return ctx.enter_context(nc.sbuf_tensor(name, shape, dt))

            def sem(name):
                return ctx.enter_context(nc.semaphore(name))

            cs = sb("cs", [P, CSMALL])
            valid = cs[:, valid0:valid0 + NT]
            token = cs[:, token0:token0 + NT]
            nowhere = cs[:, nowhere0:nowhere0 + NT]
            down = cs[:, down0:down0 + E]
            tile_steps = cs[:, steps0:steps0 + E * MAXN].rearrange("p (e n) -> p e n", n=MAXN)
            tile_no = cs[:, tile0:tile0 + SLOT_TILES * E].rearrange("p (i e) -> p i e", e=E)
            neg_half = sb("neg_half4", [P, NT])
            var_eps = sb("var_eps4", [P, NT])
            lg = sb("lg", [P, NT, E])
            shifted = sb("shifted", [P, NT, E])
            expd = sb("expd", [P, NT, E])
            total = sb("total", [P, NT])
            best = sb("best", [P, NT])
            mark = sb("mark", [P, NT, E])
            first = sb("first", [P, NT])
            choice = sb("choice", [P, NT, E])
            rank = sb("rank", [P, NT, E])
            tot = sb("tot", [P, NT, E])
            cum = sb("cum", [P, 2, NT, E])
            over = sb("over", [P, E, MAXN])
            tiles_e = sb("tiles_e", [P, E])
            ends = sb("ends", [P, 2, E])
            base = sb("base", [P, E])
            spot = sb("spot", [P, NT, E])
            place = sb("place", [P, NT])
            place_u = sb("place_u", [P, NT], mybir.dt.uint32)
            past = sb("past", [P, SLOT_TILES, E])
            owner = sb("owner", [P, SLOT_TILES])
            p_r = ctx.enter_context(nc.psum_tensor("p_r", [P, 512], F32))
            p_n = ctx.enter_context(nc.psum_tensor("p_n", [P, 512], F32))
            cs_in, steps, halves, deviation, choice_ready, exp_ready, counted, placed, scattered = (
                sem(x) for x in ("cs_in", "d_steps", "d_halves", "deviation", "choice_ready", "exp_ready", "counted",
                                 "placed", "scattered"))

            with nc.Block() as block:
                @block.sync
                def _(sp):
                    sp.dma_start(cs[:], counts).then_inc(cs_in, 16)
                    for e in range(E):
                        sp.dma_start(w2s[:, e], w2[:, e]).then_inc(w2_in, 16)
                    sp.dma_start(b2s[:], b2).then_inc(w2_in, 16)

                @block.gpsimd
                def _(pool):
                    g = nc.gpsimd
                    g.memset(neg_half[:], -0.5).then_inc(halves, 1)
                    g.tensor_scalar(var_eps[:], moments[:, :, 1], 1e-5, None, ALU.add).then_inc(halves, 1)
                    pool.wait_ge(halves, 2)
                    g.tensor_tensor(rows[:, :, RSTD_AT], var_eps[:], neg_half[:], ALU.pow).then_inc(deviation, 1)
                    g.tensor_copy(rows[:, :, MEAN_AT], moments[:, :, 0]).then_inc(deviation, 1)
                    pool.wait_ge(cs_in, 16)
                    g.tensor_copy(rows[:, :, ID_AT], token).then_inc(deviation, 1)
                    pool.wait_ge(deviation, 3)
                    pool.wait_ge(slots_clear, 16)
                    pool.wait_ge(placed, 1)
                    for t in range(NT):
                        g.indirect_dma_start(out=sorted_rows, out_offset=bass.IndirectOffsetOnAxis(ap=place_u[:, t:t + 1], axis=0),
                                             in_=rows[:, t, :], in_offset=None, bounds_check=SLOT_TILES * P - 1,
                                             oob_is_err=False).then_inc(scattered, 16)
                    pool.wait_ge(scattered, 16 * NT)

                @block.scalar
                def _(act):
                    act.wait_ge(steps, 3)
                    nc.scalar.activation(expd[:], shifted[:], ACT.Exp).then_inc(exp_ready, 1)

                @block.tensor
                def _(pe):
                    pe.wait_ge(choice_ready, 1)
                    flat = choice[:].rearrange("p t e -> p (t e)")
                    nc.tensor.matmul(p_r[:, 0:NT * E], u_before, flat, start=True, stop=True).then_inc(counted, 1)
                    nc.tensor.matmul(p_n[:, 0:NT * E], u_ones, flat, start=True, stop=True).then_inc(counted, 1)

                @block.vector
                def _(dve):
                    v = nc.vector
                    made = [0]

                    def step(ins):
                        made[0] += 1
                        ins.then_inc(steps, 1)
                        dve.wait_ge(steps, made[0])

                    def each(ap):
                        return ap.unsqueeze(2).broadcast_to([P, NT, E])

                    dve.wait_ge(deviation, 1)
                    step(v.tensor_tensor(lg[:], logits[:], each(rows[:, :, RSTD_AT]), ALU.mult))
                    step(v.tensor_reduce(best[:], lg[:], AX.X, ALU.max))
                    step(v.tensor_tensor(shifted[:], lg[:], each(best[:]), ALU.subtract))
                    step(v.tensor_scalar(mark[:], shifted[:], 0.0, None, ALU.is_equal))
                    dve.wait_ge(cs_in, 16)
                    down_all = down.unsqueeze(1).broadcast_to([P, NT, E])
                    step(v.tensor_tensor(mark[:], mark[:], down_all, ALU.mult))
                    step(v.tensor_reduce(first[:], mark[:], AX.X, ALU.max))
                    step(v.tensor_tensor(choice[:], each(first[:]), down_all, ALU.is_equal))
                    v.tensor_tensor(choice[:], choice[:], each(valid), ALU.mult).then_inc(choice_ready, 1)
                    dve.wait_ge(exp_ready, 1)
                    step(v.tensor_reduce(total[:], expd[:], AX.X, ALU.add))
                    step(v.reciprocal(rows[:, :, GATE_AT], total[:]))
                    dve.wait_ge(counted, 2)
                    step(v.tensor_copy(rank[:], p_r[:, 0:NT * E].rearrange("p (t e) -> p t e", e=E)))
                    step(v.tensor_copy(tot[:], p_n[:, 0:NT * E].rearrange("p (t e) -> p t e", e=E)))
                    src, shift = tot[:], 1
                    while shift < NT:
                        dst = cum[:, (shift.bit_length() - 1) % 2]
                        step(v.tensor_tensor(dst[:, shift:], src[:, shift:], src[:, :NT - shift], ALU.add))
                        step(v.tensor_copy(dst[:, :shift], src[:, :shift]))
                        src, shift = dst, 2 * shift
                    n_e = src[:, NT - 1].unsqueeze(2).broadcast_to([P, E, MAXN])
                    step(v.tensor_tensor(over[:], n_e, tile_steps, ALU.is_gt))
                    step(v.tensor_reduce(tiles_e[:], over[:], AX.X, ALU.add))
                    end, shift = tiles_e[:], 1
                    while shift < E:
                        dst = ends[:, (shift.bit_length() - 1) % 2]
                        step(v.tensor_tensor(dst[:, shift:], end[:, shift:], end[:, :E - shift], ALU.add))
                        step(v.tensor_copy(dst[:, :shift], end[:, :shift]))
                        end, shift = dst, 2 * shift
                    step(v.tensor_tensor(past[:], tile_no, end.unsqueeze(1).broadcast_to([P, SLOT_TILES, E]), ALU.is_ge))
                    step(v.tensor_reduce(owner[:], past[:], AX.X, ALU.add))
                    step(v.tensor_scalar(expert_of[:], owner[:], float(E - 1), None, ALU.min))
                    step(v.tensor_tensor(base[:], end, tiles_e[:], ALU.subtract))
                    step(v.tensor_scalar(base[:], base[:], float(P), None, ALU.mult))
                    step(v.tensor_tensor(spot[:], src, tot[:], ALU.subtract))
                    step(v.tensor_tensor(spot[:], spot[:], rank[:], ALU.add))
                    step(v.tensor_tensor(spot[:], spot[:], base[:].unsqueeze(1).broadcast_to([P, NT, E]), ALU.add))
                    step(v.tensor_tensor(spot[:], spot[:], choice[:], ALU.mult))
                    step(v.tensor_reduce(place[:], spot[:], AX.X, ALU.add))
                    step(v.tensor_tensor(place[:], place[:], nowhere, ALU.add))
                    v.tensor_copy(place_u[:], place[:]).then_inc(placed, 1)
        if dbg:
            dump(nc, dbg, dict(rows=rows, sorted=sorted_rows, experts=expert_of))

        with ExitStack() as ctx:
            def sb(name, shape, dt=F32):
                return ctx.enter_context(nc.sbuf_tensor(name, shape, dt))

            def ps(name, shape):
                return ctx.enter_context(nc.psum_tensor(name, shape, F32))

            def sem(name):
                return ctx.enter_context(nc.semaphore(name))

            RING = 4
            xs = sb("xs", [P, RING, ROW])
            ids = sb("ids", [P, RING], mybir.dt.uint32)
            xn = sb("xn", [P, D])
            xt = sb("xt", [C + 1, 2, 2, P])
            hidden = sb("hidden", [P, 2, FF])
            hidden_t = sb("hidden_t", [P, 2, KC, P])
            yb = sb("yb", [P, D])
            ys = sb("ys", [P, RING, D])
            p_x = ps("p_x", [P, 512])
            p_h = ps("p_h2", [P, 2, 1024])
            p_ht = ps("p_ht", [P, 1024])
            p_y = ps("p_y", [P, 512])
            xs_in = [sem(f"xs_in{r}") for r in range(RING)]
            stored = [sem(f"stored{r}") for r in range(RING)]
            (ones_set, ids_ready, xn_ready, x_tr, xt_ready, up_ready, hidden_ready, hid_tr, hidt_a, hidt_v, down_ready,
             y_read, y_ready) = (sem(x) for x in (
                 "ones_set", "ids_ready", "xn_ready", "x_tr", "xt_ready", "up_ready", "hidden_ready", "e_hid_tr",
                 "hidt_a", "hidt_v", "down_ready", "y_read", "y_ready"))

            assert SLOT_TILES % RING == 0

            def tiles(eng, body):
                last = SLOT_TILES // RING - 1
                for r in range(RING):
                    body(0, r, 2)
                with eng.Fori(1, last) as turn:
                    for r in range(RING):
                        body(turn, r, 2)
                for r in range(RING):
                    body(last, r, RING - 1 - r)

            with nc.Block() as block:
                @block.sync
                def _(sp):
                    by_tile = sorted_rows.rearrange("(i p) c -> i p c", p=P)
                    for r in range(RING):
                        sp.dma_start(xs[:, r], by_tile[r]).then_inc(xs_in[r], 16)
                    with sp.Fori(1, SLOT_TILES // RING) as turn:
                        for r in range(RING):
                            sp.wait_ge(y_ready, RING * (turn - 1) + r + 1)
                            sp.dma_start(xs[:, r], by_tile[ds(RING * turn + r, 1)].rearrange("o p c -> (o p) c")).then_inc(xs_in[r], 16)

                @block.gpsimd
                def _(pool):
                    def body(turn, r, ahead):
                        i = RING * turn + r
                        done = i + 1 if isinstance(i, int) else pool.to_reg(i + 1)
                        wait_apart(pool, y_ready, done)
                        pool.wait_ge(ids_ready, done)
                        nc.gpsimd.indirect_dma_start(out=out.rearrange("b t d -> (b t) d"),
                                                     out_offset=bass.IndirectOffsetOnAxis(ap=ids[:, r:r + 1], axis=0),
                                                     in_=ys[:, r], in_offset=None, bounds_check=B * L - 1,
                                                     oob_is_err=False).then_inc(stored[r], 16)

                    tiles(pool, body)
                    for r in range(RING):
                        pool.wait_ge(stored[r], 16 * (SLOT_TILES // RING))

                @block.scalar
                def _(act):
                    def x_out(i, u):
                        act.wait_ge(x_tr, i + 1)
                        nc.scalar.copy(xt[0:C, u], p_x[0:C, 0:2 * P].rearrange("p (c t) -> p c t", c=2)).then_inc(xt_ready, 1)

                    def silu(i, u):
                        act.wait_ge(up_ready, i + 1)
                        nc.scalar.activation(hidden[:, u], p_h[:, u, 0:FF], ACT.Silu).then_inc(hidden_ready, 1)

                    def body(turn, r, ahead):
                        i = RING * turn + r
                        u = r % 2
                        if ahead >= 1:
                            silu(i + 1, 1 - u)
                        act.wait_ge(hid_tr, 2 * i + 1)
                        nc.scalar.copy(hidden_t[:, u, 0:4], p_ht[:, 0:512].rearrange("p (k t) -> p k t", k=4)).then_inc(hidt_a, 1)
                        if ahead >= 2:
                            x_out(i + 2, u)

                    act.wait_ge(ones_set, 1)
                    x_out(0, 0)
                    x_out(1, 1)
                    silu(0, 0)
                    tiles(act, body)

                @block.tensor
                def _(pe):
                    mm = nc.tensor.matmul

                    def x_in(i, u):
                        pe.wait_ge(xn_ready, i + 1)
                        for c in range(2):
                            last = nc.tensor.transpose(p_x[0:C, c * P:(c + 1) * P], xn[:, c * C:(c + 1) * C], ident)
                        last.then_inc(x_tr, 1)

                    def up(i, u):
                        e = pe.value_load(expert_of[0:1, ds(i, 1)], min_val=0, max_val=E - 1)
                        pe.wait_ge(xt_ready, i + 1)
                        for a, b in ((0, 512), (512, FF)):
                            for c in range(2):
                                n = C + c
                                last = mm(p_h[:, u, a:b], xt[0:n, u, c], w1s[0:n, ds(e, 1), c, a:b].rearrange("p o f -> p (o f)"),
                                          start=(c == 0), stop=(c == 1))
                        last.then_inc(up_ready, 1)

                    def down(i, u):
                        e = pe.value_load(expert_of[0:1, ds(i, 1)], min_val=0, max_val=E - 1)
                        wait_apart(pe, hidt_a, i + 1)
                        wait_apart(pe, hidt_v, i + 1)
                        for k in range(KC):
                            last = mm(p_y[:, 0:D], hidden_t[:, u, k], w2s[:, ds(e, 1), k].rearrange("p o d -> p (o d)"),
                                      start=(k == 0), stop=(k == KC - 1))
                        last.then_inc(down_ready, 1)

                    def body(turn, r, ahead):
                        i = RING * turn + r
                        u = r % 2
                        if ahead >= 1:
                            up(i + 1, 1 - u)
                        wait_apart(pe, hidden_ready, i + 1)
                        for k in range(KC):
                            last = nc.tensor.transpose(p_ht[:, k * P:(k + 1) * P], hidden[:, u, k * P:(k + 1) * P], ident)
                            if k == 3:
                                last.then_inc(hid_tr, 1)
                        last.then_inc(hid_tr, 1)
                        if ahead >= 2:
                            x_in(i + 2, u)
                        wait_apart(pe, y_read, i + 1)
                        down(i, u)

                    pe.wait_ge(w1_in, 16 * E)
                    x_in(0, 0)
                    pe.wait_ge(xt_ready, 1)
                    x_in(1, 1)
                    up(0, 0)
                    pe.wait_ge(w2_in, 16 * (E + 1))
                    tiles(pe, body)

                @block.vector
                def _(dve):
                    v = nc.vector

                    def norm(i, r, turn):
                        dve.wait_ge(xs_in[r], 16 * turn + 16)
                        v.tensor_scalar(xn[:], xs[:, r, 0:D], xs[:, r, MEAN_AT:MEAN_AT + 1], xs[:, r, RSTD_AT:RSTD_AT + 1],
                                        ALU.subtract, ALU.mult).then_inc(xn_ready, 1)

                    def body(turn, r, ahead):
                        i = RING * turn + r
                        u = r % 2
                        e = dve.value_load(expert_of[0:1, ds(i, 1)], min_val=0, max_val=E - 1)
                        if ahead >= 2:
                            wait_apart(dve, x_tr, i + 2)
                            norm(i + 2, (r + 2) % RING, turn + (r + 2) // RING)
                        dve.wait_ge(hid_tr, 2 * i + 2)
                        v.tensor_copy(hidden_t[:, u, 4:6], p_ht[:, 512:768].rearrange("p (k t) -> p k t", k=2)).then_inc(hidt_v, 1)
                        if not isinstance(turn, int) or turn:
                            wait_apart(dve, stored[r], 16 * turn)
                        v.tensor_copy(ids[:, r:r + 1], xs[:, r, ID_AT:ID_AT + 1]).then_inc(ids_ready, 1)
                        dve.wait_ge(down_ready, i + 1)
                        v.tensor_tensor(yb[:], p_y[:, 0:D], b2s[:, ds(e, 1)].rearrange("p o d -> p (o d)"), ALU.add).then_inc(y_read, 1)
                        wait_apart(dve, y_read, i + 2)
                        v.scalar_tensor_tensor(ys[:, r], yb[:], xs[:, r, GATE_AT:GATE_AT + 1], xs[:, r, 0:D], ALU.mult, ALU.add).then_inc(y_ready, 1)

                    v.sem_inc(y_read, 1)
                    v.memset(xt[C:C + 1, :], 1.0).then_inc(ones_set, 1)
                    norm(0, 0, 0)
                    dve.wait_ge(x_tr, 1)
                    norm(1, 1, 0)
                    tiles(dve, body)


def dump(nc, dbg, what):
    with nc.semaphore("dumped") as s:
        with nc.Block() as block:
            @block.sync
            def _(sp):
                n = 0
                for k, t in what.items():
                    if k in dbg:
                        sp.dma_start(dbg[k], t[:]).then_inc(s, 16)
                        n += 16
                if n:
                    sp.wait_ge(s, n)


def layouts(x, txt, L0_tok_proj_w, L0_tok_proj_b, L0_tok_cls_token, L0_tok_pos_embedding, L0_attn_conv_w,
            L0_attn_conv_b, L0_attn_ln_g, L0_attn_ln_b, L0_attn_qkv_w, L0_attn_qkv_b, L0_attn_bn_w1, L0_attn_bn_w2,
            L0_attn_temperature, L0_attn_proj_w, L0_attn_proj_b, L0_attn_mn_g, L0_attn_mn_b, L0_ffn_Wg, L0_ffn_W1,
            L0_ffn_b1, L0_ffn_W2, L0_ffn_b2):
    import numpy as np

    f = np.float32

    def chunks(a, n, rows):
        return np.ascontiguousarray(np.moveaxis(a.reshape(n, rows, *a.shape[1:]), 0, 1))

    G = 96 // 16
    pt = x.reshape(B, 3, G, 16, G, 16).transpose(1, 3, 5, 0, 2, 4).reshape(KC, P, PAIRS, 2, NPATCH)
    patches = np.zeros((PAIRS, P, KC, 2, HALF), f)
    patches[..., 1:LP] = pt.transpose(2, 1, 0, 3, 4)
    pos_rows = np.zeros((2, HALF, D), f)
    pos_rows[:, :LP] = L0_tok_pos_embedding
    first_rows = np.zeros((2, HALF, D), f)
    first_rows[:, 0] = L0_tok_cls_token[0, 0]
    first_rows[:, 1:LP] = L0_tok_proj_b
    conv_w = np.concatenate([L0_attn_conv_w, L0_attn_conv_b[:, None]], 1)
    w_in = np.concatenate([L0_attn_qkv_w, L0_attn_bn_w1], 0).T
    b_in = np.concatenate([L0_attn_qkv_b, np.zeros(R, f)])
    w1 = np.zeros((C + 1, E, 2, FF), f)
    w1[:C] = L0_ffn_W1.reshape(E, 2, C, FF).transpose(2, 0, 1, 3)
    w1[C, :, 1] = L0_ffn_b1
    s, t = np.arange(P)[:, None], np.arange(P)[None, :]
    u_pre = (s // HALF == t // HALF) & (s <= t) & (s % HALF < LP)
    consts = [s == t, s <= t, u_pre] + [(s // HALF == b) & (s % HALF < LP) & (t >= 0) for b in range(2)] + [s < t, t >= 0]
    counts = np.zeros((P, CSMALL), f)
    r = np.arange(P)
    for g in range(NT):
        b, j = 2 * (g // 3), g % 3
        real = (r % HALF < LP) if j == 0 else r >= 0
        number = (b + r // HALF) * L + r % HALF if j == 0 else (b + j - 1) * L + LP + r
        counts[:, valid0 + g] = real
        counts[:, token0 + g] = number
        counts[:, nowhere0 + g] = np.where(real, 0, NOWHERE)
    counts[:, down0:steps0] = E - np.arange(E)
    counts[:, steps0:tile0] = np.tile(P * np.arange(MAXN), E)
    counts[:, tile0:] = np.repeat(np.arange(SLOT_TILES), E)
    return {
        "patches": patches.reshape(PAIRS, P, KC, P),
        "txt": np.ascontiguousarray(txt),
        "tok_w": chunks(L0_tok_proj_w.T, KC, P),
        "pos_rows": pos_rows.reshape(P, D),
        "first_rows": first_rows.reshape(P, D),
        "conv_w": chunks(conv_w, 2, C),
        "ln_gb": chunks(np.stack([L0_attn_ln_g, L0_attn_ln_b], 1), 2, C),
        "w_in": chunks(w_in, 2, C),
        "b_in": np.tile(b_in, (P, 1)),
        "bn2": np.ascontiguousarray(L0_attn_bn_w2.T),
        "temp": np.tile(L0_attn_temperature, (P, 1)),
        "w_out": chunks(L0_attn_proj_w.T, 2, C),
        "b_out": np.tile(L0_attn_proj_b, (P, 1)),
        "mn_gb": np.tile(np.stack([L0_attn_mn_g, L0_attn_mn_b], 1), (C // DH, 1)),
        "wg": chunks(L0_ffn_Wg, 2, C),
        "w1": w1,
        "w2": np.ascontiguousarray(L0_ffn_W2.reshape(E, KC, P, D).transpose(2, 0, 1, 3)),
        "b2": np.tile(L0_ffn_b2[None], (P, 1, 1)),
        "consts": np.concatenate([np.broadcast_to(c, (P, P)) for c in consts], 1).astype(f),
        "counts": counts,
    }


def kernel(**inputs):
    import numpy as np
    import concourse.bacc as bacc
    from concourse.bass_utils import run_bass_kernel_spmd

    nc = bacc.Bacc("TRN2", target_bir_lowering=False, num_devices=1)
    arrays = layouts(**{k: np.asarray(v) for k, v in inputs.items()})
    args = {k: nc.dram_tensor(k, a.shape, mybir.dt.from_np(a.dtype), kind="ExternalInput").ap() for k, a in arrays.items()}
    out = nc.dram_tensor("out", (B, L, D), F32, kind="ExternalOutput").ap()
    early_fusion_layer(nc, out=out, **args)
    r = run_bass_kernel_spmd(nc, [arrays], core_ids=[0])
    return r.results[0]["out"]
```

```python
from contextlib import ExitStack

import concourse.bass as bass
from concourse import mybir

F32 = mybir.dt.float32
ALU = mybir.AluOpType
ACT = mybir.ActivationFunctionType
AX = mybir.AxisListType

B = 16
NPATCH = 36
LP = NPATCH + 1
LT = 128
L = LP + LT
D = 192
KP = 768
H = 12
DH = D // H
R = 64
NG = 5
E = 8
FF = 768

P = 128
C = D // 2
KC = KP // P
PAIRS = B // 2
NT = 3 * PAIRS
HALF = 64
QK, V0, HID0, MEAN = 0, 2 * D, 3 * D, 3 * D + R
WCOLS = 3 * D + R
ident0, utt0, upp0, sel0, before0, ones0 = 0, P, 2 * P, 3 * P, 5 * P, 6 * P
head0 = 7 * P
same0 = head0 + C // DH
CMAT = same0 + C
HG = 4
NHG = H // HG
UNITS = PAIRS * NHG
SLOT_TILES = (B * L + E * (P - 1)) // P
MAXN = -(-B * L // P)
ROW = D + 4
MEAN_AT, RSTD_AT, GATE_AT, ID_AT = D, D + 1, D + 2, D + 3
NOWHERE = 1 << 20
valid0 = 0
token0 = valid0 + NT
nowhere0 = token0 + NT
down0 = nowhere0 + NT
steps0 = down0 + E
tile0 = steps0 + E * MAXN
CSMALL = tile0 + SLOT_TILES * E


def wait_apart(eng, sem, value):
    if isinstance(value, int):
        eng.wait_ge(sem, value)
        return
    value = eng.to_reg(value)
    eng.wait_ge(sem, 1)
    eng.wait_ge(sem, value)


def after(eng, sem, value):
    if not isinstance(value, int):
        wait_apart(eng, sem, value)
    elif value > 0:
        eng.wait_ge(sem, value)


def early_fusion_layer(nc, patches, txt, tok_w, pos_rows, first_rows, conv_w, ln_gb, w_in, b_in, bn2, temp,
                       w_out, b_out, mn_gb, wg, w1, w2, b2, consts, counts, out, dbg=None):
    ds = bass.ds
    with ExitStack() as top:
        def sbuf(name, shape, dt=F32):
            return top.enter_context(nc.sbuf_tensor(name, shape, dt))

        cst = sbuf("cst", [P, CMAT])
        ident = cst[:, ident0:ident0 + P]
        u_txt = cst[:, utt0:utt0 + P]
        u_pre = cst[:, upp0:upp0 + P]
        prefix_of = [cst[:, sel0 + b * P:sel0 + (b + 1) * P] for b in range(2)]
        u_before = cst[:, before0:before0 + P]
        u_ones = cst[:, ones0:ones0 + P]
        head_of = cst[0:C, head0:same0]
        same_head = cst[0:C, same0:CMAT]
        rows = sbuf("rows", [P, NT, ROW])
        hid = rows[:, :, 0:D]
        logits = sbuf("logits", [P, NT, E])
        moments = sbuf("moments", [P, NT, 2])
        w1s = sbuf("w1s", [C + 1, E, 2, FF])
        empty = sbuf("empty", [P, ROW])
        sorted_rows = nc.dram_tensor("sorted_rows", (SLOT_TILES * P, ROW), F32, kind="Internal").ap()
        w1_in = top.enter_context(nc.semaphore("w1_in"))
        slots_clear = top.enter_context(nc.semaphore("slots_clear"))

        mid = top.enter_context(ExitStack())

        def sbuf(name, shape, dt=F32):
            return mid.enter_context(nc.sbuf_tensor(name, shape, dt))

        qk = sbuf("qk", [P, NT, 2 * D])
        val = sbuf("val", [P, NT, D])
        gates = sbuf("gates", [P, NT, H * NG])
        decay = sbuf("decay", [P, NT, H])
        gain_kv = sbuf("gain_kv", [P, NT, H])
        gain_z = sbuf("gain_z", [P, NT, H])
        clip_hi = sbuf("clip_hi", [P, NT, H])
        clip_lo = sbuf("clip_lo", [P, NT, H])

        with ExitStack() as ctx:
            def sb(name, shape):
                return ctx.enter_context(nc.sbuf_tensor(name, shape, F32))

            def ps(name, shape):
                return ctx.enter_context(nc.psum_tensor(name, shape, F32))

            def sem(name):
                return ctx.enter_context(nc.semaphore(name))

            tokw = sb("tokw", [P, KC, D])
            posb = sb("posb", [P, D])
            firstb = sb("firstb", [P, D])
            convs = sb("convs", [C, 2, 4])
            lng = sb("lng", [C, 2, 2])
            win = sb("win", [C, 2, WCOLS + 1])
            wgain = sb("wgain", [C, 2, WCOLS])
            bin_ = sb("bin_", [P, WCOLS])
            bin_raw = sb("bin_raw", [P, WCOLS])
            win_raw = sb("win_raw", [C, 2, WCOLS])
            ones_d = sb("ones_d", [C, P])
            lnb_wide = sb("lnb_wide", [C, 2, P])
            bn2s = sb("bn2s", [R, H * NG])
            pat = sb("pat", [P, 2, KC, P])
            neg_half = sb("neg_half", [P, 3])
            mv = sb("mv", [P, 3, 2])
            bst = sb("bst", [P, 3, 6])
            vare = sb("vare", [P, 3])
            rstd = sb("rstd", [P, 3])
            xa = sb("xa", [P, 3, D])
            xat = sb("xat", [C, 2, 2, L + 2])
            xct = sb("xct", [C, 2, 2, 2, L])
            xpre = sb("xpre", [C, 2, 2, P])
            xsq = sb("xsq", [C, 2, 2, 3 * P])
            stat = sb("stat", [P, 2, 2])
            nvar = sb("nvar", [P, 2])
            vare2 = sb("vare2", [P, 2])
            rstd2 = sb("rstd2", [P, 2])
            qkr = sb("qkr", [P, 2, 2 * D])
            qkm = sb("qkm", [P, 2, 2 * D])
            qke = sb("qke", [P, 2, 2 * D])
            hr = sb("hr", [P, 2, R])
            ht = sb("ht", [P, 2, R])
            hs = sb("hs", [P, 3, R])
            hst = sb("hst", [R, 3 * P])

            p_tok = ps("p_tok", [P, 512])
            p_tr = ps("p_tr", [P, 2, 512])
            p_qk = ps("p_qk", [P, 2, 512])
            p_v = ps("p_v", [P, 2, 512])
            p_h = ps("p_h", [P, 512])

            weights_in = sem("weights_in")
            small_in = sem("small_in")
            text_in = sem("text_in")
            patches_in = [sem(f"patches_in{u}") for u in range(2)]
            prep_v = sem("prep_v")
            prep_pe = sem("prep_pe")
            halves_set = sem("halves_set")
            w_ready = sem("w_ready")
            pads_zero = sem("pads_zero")
            tok_ready = sem("tok_ready")
            h_ready = sem("h_ready")
            st_done = sem("st_done")
            mv_ready = sem("mv_ready")
            vare_done = sem("vare_done")
            rstd_ready = sem("rstd_ready")
            xa_ready = sem("xa_ready")
            tr_ready = sem("tr_ready")
            xat_ready = sem("xat_ready")
            conv_first = sem("conv_first")
            conv_step = sem("conv_step")
            conv_ready = sem("conv_ready")
            xsq_ready = sem("xsq_ready")
            xpre_ready = sem("xpre_ready")
            proj_ready = sem("proj_ready")
            stat_copied = sem("stat_copied")
            nvar_ready = sem("nvar_ready")
            vare2_done = sem("vare2_done")
            rstd2_ready = sem("rstd2_ready")
            qk_raw = sem("qk_raw")
            banks_read = sem("banks_read")
            hid_raw = sem("hid_raw")
            qk_min = sem("qk_min")
            qk_exp = sem("qk_exp")
            hid_tanh = sem("hid_tanh")
            qk_done = sem("qk_done")
            hid_silu = sem("hid_silu")
            hid_tr = sem("hid_tr")
            hidt_ready = sem("hidt_ready")
            par_ready = sem("par_ready")
            par_read = sem("par_read")

            SMALL = 9

            def bodies(eng, body):
                body(0, 0, 2)
                body(1, 1, 2)
                with eng.Fori(1, PAIRS // 2 - 1) as i:
                    body(2 * i, 0, 2)
                    body(2 * i + 1, 1, 2)
                body(PAIRS - 2, 0, 1)
                body(PAIRS - 1, 1, 0)

            with nc.Block() as block:
                @block.sync
                def _(sp):
                    for u in range(2):
                        sp.dma_start(pat[:, u], patches[u]).then_inc(patches_in[u], 16)
                        if u == 0:
                            sp.dma_start(tokw[:], tok_w).then_inc(weights_in, 16)
                    sp.dma_start(win_raw[:], w_in).then_inc(weights_in, 16)
                    for e in range(E):
                        sp.dma_start(w1s[:, e], w1[:, e]).then_inc(w1_in, 16)
                    with sp.Fori(1, PAIRS // 2) as i:
                        for u in range(2):
                            sp.wait_ge(tok_ready, 2 * i + u - 1)
                            sp.dma_start(pat[:, u], patches[ds(2 * i + u, 1)].rearrange("o p c n -> p (o c) n")).then_inc(patches_in[u], 16)

                @block.scalar
                def _(act):
                    act.dma_start(cst[:], consts).then_inc(small_in, 16)
                    act.dma_start(posb[:], pos_rows).then_inc(small_in, 16)
                    act.dma_start(firstb[:], first_rows).then_inc(small_in, 16)
                    act.dma_start(convs[:], conv_w).then_inc(small_in, 16)
                    act.dma_start(lng[:], ln_gb).then_inc(small_in, 16)
                    act.dma_start(bin_raw[:], b_in).then_inc(small_in, 16)
                    act.dma_start(bn2s[:], bn2).then_inc(small_in, 16)
                    hv = hid.rearrange("p (g j) d -> p g j d", j=3)
                    tv = txt.rearrange("(g b) t d -> t g b d", b=2)
                    for b in range(2):
                        act.dma_start(hv[:, :, 1 + b, :], tv[:, :, b, :]).then_inc(text_in, 16)

                    def transposed(p, u):
                        act.wait_ge(tr_ready, p + 1)
                        act.wait_ge(conv_ready, 2 * p) if not isinstance(p, int) or p else None
                        for c in range(2):
                            nc.scalar.copy(xat[:, c, :, 2:2 + LP],
                                           p_tr[0:C, c, 0:P].rearrange("p (b t) -> p b t", b=2)[:, :, 0:LP]).then_inc(xat_ready, 1)
                            nc.scalar.copy(xat[:, c, :, 2 + LP:],
                                           p_tr[0:C, c, P:3 * P].rearrange("p (b t) -> p b t", b=2)).then_inc(xat_ready, 1)

                    def conv_last_tap(p, u):
                        after(act, proj_ready, 3 * p - 3)
                        act.wait_ge(xat_ready, 4 * p + 4)
                        for c in range(2):
                            nc.scalar.activation(xct[:, u, c], xat[:, c, :, 2:], ACT.Identity,
                                                 scale=convs[:, c, 2:3], bias=convs[:, c, 3:4]).then_inc(conv_first, 1)

                    def squares(p, u):
                        act.wait_ge(conv_ready, 2 * p + 2)
                        for c in range(2):
                            nc.scalar.activation(xsq[:, u, c, 0:P].rearrange("p (b t) -> p b t", b=2),
                                                 xct[:, u, c, :, 0:HALF], ACT.Square).then_inc(xsq_ready, 1)
                            nc.scalar.activation(xsq[:, u, c, P:].rearrange("p (b t) -> p b t", b=2),
                                                 xct[:, u, c, :, LP:], ACT.Square).then_inc(xsq_ready, 1)

                    def nonlinear(p, u, j):
                        s = (u + j) % 2
                        t = 3 * p + j
                        act.wait_ge(hid_raw, t + 1)
                        nc.scalar.activation(ht[:, s], hr[:, s], ACT.Tanh, scale=0.5).then_inc(hid_tanh, 1)
                        act.wait_ge(qk_min, t + 1)
                        nc.scalar.activation(qke[:, s], qkm[:, s], ACT.Exp).then_inc(qk_exp, 1)

                    def hidden_out(p):
                        wait_apart(act, hid_tr, p + 1)
                        nc.scalar.copy(hst[:], p_h[0:R, 0:3 * P]).then_inc(hidt_ready, 1)

                    def params_out(p):
                        wait_apart(act, par_ready, p + 1)
                        nc.scalar.activation(gates[:, ds(3 * p, 3), :], p_h[:, 0:3 * H * NG].rearrange("p (j n) -> p j n", j=3),
                                             ACT.Identity, scale=0.5).then_inc(par_read, 1)

                    def body(p, u, ahead):
                        first = isinstance(p, int) and p == 0
                        if ahead >= 1:
                            transposed(p + 1, 1 - u)
                            conv_last_tap(p + 1, 1 - u)
                        nonlinear(p, u, 0)
                        if not first:
                            hidden_out(p - 1)
                        nonlinear(p, u, 1)
                        if ahead >= 1:
                            squares(p + 1, 1 - u)
                        if not first:
                            params_out(p - 1)
                        nonlinear(p, u, 2)

                    act.wait_ge(pads_zero, 4)
                    transposed(0, 0)
                    conv_last_tap(0, 0)
                    squares(0, 0)
                    bodies(act, body)
                    hidden_out(PAIRS - 1)
                    params_out(PAIRS - 1)

                @block.gpsimd
                def _(pool):
                    pool.wait_ge(pads_zero, 2)
                    pool.dma_start(sorted_rows.rearrange("(i p) c -> p i c", p=P),
                                   empty[:].unsqueeze(1).broadcast_to([P, SLOT_TILES, ROW])).then_inc(slots_clear, 16)
                    nc.gpsimd.memset(neg_half[:], -0.5).then_inc(halves_set, 1)
                    pool.wait_ge(halves_set, 1)

                    def first_norm(p):
                        wait_apart(pool, mv_ready, 3 * p + 3)
                        nc.gpsimd.tensor_scalar(vare[:], mv[:, :, 1], 1e-5, None, ALU.add).then_inc(vare_done, 1)
                        wait_apart(pool, vare_done, p + 1)
                        nc.gpsimd.tensor_tensor(rstd[:], vare[:], neg_half[:], ALU.pow).then_inc(rstd_ready, 1)

                    def second_norm(p, u, j):
                        s = (u + j) % 2
                        t = 3 * p + j
                        wait_apart(pool, nvar_ready, t + 1)
                        nc.gpsimd.tensor_scalar(vare2[:, s:s + 1], nvar[:, s:s + 1], -1.0, 1e-5, ALU.mult, ALU.add).then_inc(vare2_done, 1)
                        wait_apart(pool, vare2_done, t + 1)
                        nc.gpsimd.tensor_tensor(rstd2[:, s:s + 1], vare2[:, s:s + 1], neg_half[:, 0:1], ALU.pow).then_inc(rstd2_ready, 1)

                    def prefixes(p, u):
                        wait_apart(pool, conv_ready, 2 * p + 2)
                        nc.gpsimd.tensor_copy(xpre[:, u].rearrange("p c (b t) -> p c b t", b=2),
                                              xct[:, u, :, :, 0:HALF]).then_inc(xpre_ready, 1)

                    def body(p, u, ahead):
                        second_norm(p, u, 0)
                        if ahead >= 2:
                            first_norm(p + 2)
                        second_norm(p, u, 1)
                        if ahead >= 1:
                            prefixes(p + 1, 1 - u)
                        second_norm(p, u, 2)

                    first_norm(0)
                    first_norm(1)
                    prefixes(0, 0)
                    bodies(pool, body)

                @block.vector
                def _(dve):
                    v = nc.vector
                    v.memset(empty[:, 0:ID_AT], 0.0).then_inc(pads_zero, 1)
                    v.memset(empty[:, ID_AT:], float(NOWHERE)).then_inc(pads_zero, 1)
                    v.memset(xat[:, :, :, 0:2], 0.0).then_inc(pads_zero, 1)
                    v.memset(ones_d[:], 1.0 / D).then_inc(prep_v, 1)
                    dve.wait_ge(small_in, 16 * 7)
                    v.tensor_tensor(posb[:], posb[:], firstb[:], ALU.add).then_inc(prep_v, 1)
                    v.tensor_scalar(convs[:, :, 2], convs[:, :, 2], 1.0, None, ALU.add).then_inc(pads_zero, 1)
                    dve.wait_ge(prep_v, 2)
                    for c in range(2):
                        v.tensor_scalar(lnb_wide[:, c], ones_d[:], float(D), lng[:, c, 1:2], ALU.mult, ALU.mult).then_inc(prep_v, 1)

                    def stats(p):
                        dve.wait_ge(tok_ready, p + 1)
                        v.tensor_tensor(hid[:, ds(3 * p, 1), :], p_tok[:, 0:D].rearrange("p (o d) -> p o d", o=1),
                                        posb[:].rearrange("p (o d) -> p o d", o=1), ALU.add).then_inc(h_ready, 1)
                        for j in (1, 2, 0):
                            if j == 0:
                                wait_apart(dve, h_ready, p + 1)
                            v.bn_stats(bst[:, j], hid[:, ds(3 * p + j, 1), :].rearrange("p o d -> p (o d)")).then_inc(st_done, 1)
                        wait_apart(dve, st_done, 3 * p + 3)
                        for j in range(3):
                            v.bn_aggr(mv[:, j], bst[:, j]).then_inc(mv_ready, 1)

                    def norm(p):
                        after(dve, tr_ready, p)
                        dve.wait_ge(rstd_ready, p + 1)
                        for j in range(3):
                            v.tensor_scalar(xa[:, j:j + 1], hid[:, ds(3 * p + j, 1), :], mv[:, j, 0:1], rstd[:, j:j + 1],
                                            ALU.subtract, ALU.mult).then_inc(xa_ready, 1)

                    def conv(p, u):
                        dve.wait_ge(conv_first, 2 * p + 2)
                        for c in range(2):
                            v.scalar_tensor_tensor(xct[:, u, c], xat[:, c, :, 1:1 + L], convs[:, c, 1:2], xct[:, u, c],
                                                   ALU.mult, ALU.add).then_inc(conv_step, 1)
                        for c in range(2):
                            dve.wait_ge(conv_step, 2 * p + 1 + c)
                            v.scalar_tensor_tensor(xct[:, u, c], xat[:, c, :, 0:L], convs[:, c, 0:1], xct[:, u, c],
                                                   ALU.mult, ALU.add).then_inc(conv_ready, 1)

                    def second_stats(p, u, j):
                        s = (u + j) % 2
                        t = 3 * p + j
                        dve.wait_ge(proj_ready, t + 1)
                        v.tensor_copy(stat[:, s], p_v[:, s, D + R:D + R + 2]).then_inc(stat_copied, 1)
                        dve.wait_ge(stat_copied, t + 1)
                        v.scalar_tensor_tensor(nvar[:, s:s + 1], stat[:, s, 0:1], stat[:, s, 0:1], stat[:, s, 1:2],
                                               ALU.mult, ALU.subtract).then_inc(nvar_ready, 1)

                    def scaled(p, u, j):
                        s = (u + j) % 2
                        t = 3 * p + j
                        dve.wait_ge(rstd2_ready, t + 1)
                        dve.wait_ge(qk_done, t + 1)
                        r = rstd2[:, s:s + 1]
                        v.scalar_tensor_tensor(hr[:, s], p_v[:, s, D:D + R], r, bin_[:, HID0:HID0 + R], ALU.mult, ALU.add).then_inc(hid_raw, 1)
                        v.scalar_tensor_tensor(qkr[:, s], p_qk[:, s, 0:2 * D], r, bin_[:, 0:2 * D], ALU.mult, ALU.add).then_inc(qk_raw, 1)
                        v.scalar_tensor_tensor(val[:, ds(t, 1), :], p_v[:, s:s + 1, 0:D], r,
                                               bin_[:, V0:V0 + D].rearrange("p (o d) -> p o d", o=1), ALU.mult, ALU.add).then_inc(banks_read, 1)
                        dve.wait_ge(qk_raw, t + 1)
                        v.tensor_scalar(qkm[:, s], qkr[:, s], 0.0, None, ALU.min).then_inc(qk_min, 1)

                    def finished(p, u, j):
                        s = (u + j) % 2
                        t = 3 * p + j
                        after(dve, hid_tr, p)
                        dve.wait_ge(hid_tanh, t + 1)
                        v.scalar_tensor_tensor(hs[:, j], ht[:, s], 1.0, hr[:, s], ALU.add, ALU.mult).then_inc(hid_silu, 1)
                        dve.wait_ge(qk_exp, t + 1)
                        v.scalar_tensor_tensor(qk[:, ds(t, 1), :], qkr[:, s:s + 1], 0.0, qke[:, s:s + 1], ALU.max, ALU.add).then_inc(qk_done, 1)

                    def body(p, u, ahead):
                        second_stats(p, u, 0)
                        scaled(p, u, 0)
                        if ahead >= 2:
                            stats(p + 2)
                        second_stats(p, u, 1)
                        finished(p, u, 0)
                        if ahead >= 1:
                            conv(p + 1, 1 - u)
                        scaled(p, u, 1)
                        if ahead >= 2:
                            norm(p + 2)
                        second_stats(p, u, 2)
                        finished(p, u, 1)
                        scaled(p, u, 2)
                        finished(p, u, 2)

                    dve.wait_ge(text_in, 32)
                    dve.wait_ge(prep_v, 2)
                    v.sem_inc(banks_read, 2)
                    v.sem_inc(qk_done, 2)
                    stats(0)
                    norm(0)
                    stats(1)
                    dve.wait_ge(weights_in, 32)
                    for c in range(2):
                        v.tensor_scalar(wgain[:, c], win_raw[:, c], lng[:, c, 0:1], None, ALU.mult).then_inc(prep_v, 1)
                    v.memset(win[:, :, MEAN:MEAN + 1], 1.0 / D).then_inc(w_ready, 1)
                    dve.wait_ge(prep_pe, 4)
                    for c in range(2):
                        v.tensor_tensor(win[:, c, 0:512], wgain[:, c, 0:512], p_qk[0:C, 0, 0:512], ALU.subtract).then_inc(w_ready, 1)
                        v.tensor_tensor(win[:, c, 512:WCOLS], wgain[:, c, 512:WCOLS], p_qk[0:C, 1, 0:WCOLS - 512], ALU.subtract).then_inc(w_ready, 1)
                    v.tensor_tensor(bin_[:, 0:512], bin_raw[:, 0:512], p_v[:, 0, 0:512], ALU.add).then_inc(w_ready, 1)
                    v.tensor_tensor(bin_[:, 512:WCOLS], bin_raw[:, 512:WCOLS], p_v[:, 1, 0:WCOLS - 512], ALU.add).then_inc(w_ready, 1)
                    norm(1)
                    conv(0, 0)
                    dve.wait_ge(w_ready, 7)
                    bodies(dve, body)

                @block.tensor
                def _(pe):
                    mm = nc.tensor.matmul

                    def tokens(p, u, turn):
                        after(pe, h_ready, p)
                        pe.wait_ge(patches_in[u], 16 * turn + 16)
                        for k in range(KC):
                            last = mm(p_tok[:, 0:D], pat[:, u, k], tokw[:, k], start=(k == 0), stop=(k == KC - 1))
                        last.then_inc(tok_ready, 1)

                    def transposes(p):
                        after(pe, xat_ready, 4 * p)
                        pe.wait_ge(xa_ready, 3 * p + 3)
                        for c in range(2):
                            for j in range(3):
                                last = nc.tensor.transpose(p_tr[0:C, c, j * P:(j + 1) * P], xa[:, j, c * C:(c + 1) * C], ident)
                        last.then_inc(tr_ready, 1)

                    def project(p, u, j):
                        s = (u + j) % 2
                        t = 3 * p + j
                        pe.wait_ge(banks_read, t + 1)
                        for c in range(2):
                            rows = [xpre[:, u, c], xct[:, u, c, 0, LP:], xct[:, u, c, 1, LP:]][j]
                            mm(p_qk[:, s, 0:2 * D], rows, win[:, c, 0:2 * D], start=(c == 0), stop=(c == 1))
                        for c in range(2):
                            rows = [xpre[:, u, c], xct[:, u, c, 0, LP:], xct[:, u, c, 1, LP:]][j]
                            mm(p_v[:, s, 0:D + R + 1], rows, win[:, c, V0:MEAN + 1], start=(c == 0), stop=(c == 1))
                        for c in range(2):
                            rows = xsq[:, u, c, j * P:(j + 1) * P]
                            last = mm(p_v[:, s, D + R + 1:D + R + 2], rows, win[:, c, MEAN:MEAN + 1], start=False, stop=(c == 1), skip_group_check=True)
                        last.then_inc(proj_ready, 1)

                    def hidden(p):
                        after(pe, par_read, p)
                        wait_apart(pe, hid_silu, 3 * p + 3)
                        for j in range(3):
                            last = nc.tensor.transpose(p_h[0:R, j * P:(j + 1) * P], hs[:, j], ident)
                        last.then_inc(hid_tr, 1)

                    def gate_params(p):
                        wait_apart(pe, hidt_ready, p + 1)
                        for j in range(3):
                            last = mm(p_h[:, j * H * NG:(j + 1) * H * NG], hst[:, j * P:(j + 1) * P], bn2s[:], start=True, stop=True, skip_group_check=True)
                        last.then_inc(par_ready, 1)

                    def body(p, u, ahead):
                        first = isinstance(p, int) and p == 0
                        if ahead >= 1:
                            transposes(p + 1)
                        wait_apart(pe, xsq_ready, 4 * p + 4)
                        wait_apart(pe, xpre_ready, p + 1)
                        project(p, u, 0)
                        if ahead >= 2:
                            tokens(p + 2, u, (p + 2 - u) // 2)
                        if not first:
                            hidden(p - 1)
                        project(p, u, 1)
                        if not first:
                            gate_params(p - 1)
                        project(p, u, 2)

                    pe.wait_ge(weights_in, 32)
                    pe.wait_ge(small_in, 16 * 7)
                    tokens(0, 0, 0)
                    tokens(1, 1, 0)
                    transposes(0)
                    pe.wait_ge(prep_v, 6)
                    for half, (a, b) in enumerate(((0, 512), (512, WCOLS))):
                        for c in range(2):
                            last = mm(p_qk[0:C, half, 0:b - a], ones_d[:, 0:C], wgain[:, c, a:b], start=(c == 0), stop=(c == 1))
                        last.then_inc(prep_pe, 1)
                    for half, (a, b) in enumerate(((0, 512), (512, WCOLS))):
                        for c in range(2):
                            last = mm(p_v[:, half, 0:b - a], lnb_wide[:, c], win_raw[:, c, a:b], start=(c == 0), stop=(c == 1))
                        last.then_inc(prep_pe, 1)
                    pe.wait_ge(w_ready, 7)
                    bodies(pe, body)
                    hidden(PAIRS - 1)
                    gate_params(PAIRS - 1)

        with ExitStack() as ctx:
            def sb(name, shape):
                return ctx.enter_context(nc.sbuf_tensor(name, shape, F32))

            def sem(name):
                return ctx.enter_context(nc.semaphore(name))

            tanhs = sb("tanhs", [P, NG, NT, H])
            phase = sb("phase", [P, NT, H])
            sine = sb("sine", [P, NT, H])
            cosine = sb("cosine", [P, NT, H])
            amp = sb("amp", [P, NT, H])
            amps = sb("amps", [P, NT, H])
            gate = sb("gate", [P, NT, H])
            rate = sb("rate", [P, NT, H])
            log_rate = sb("log_rate", [P, NT, H])
            keep = sb("keep", [P, NT, H])
            safe = sb("safe", [P, NT, H])
            inv_df = sb("inv_df", [P, NT, H])
            half_temp = sb("half_temp", [P, 1])
            p_sum = ctx.enter_context(nc.psum_tensor("p_sum", [P, 512], F32))
            temp_in, tanh_done, steps, sine_done, rate_log, gate_tanh, sums_ready, df_ready = (
                sem(x) for x in ("temp_in", "tanh_done", "steps", "sine_done", "rate_log", "gate_tanh", "sums_ready", "df_ready"))

            with nc.Block() as block:
                @block.sync
                def _(sp):
                    sp.dma_start(half_temp[:], temp).then_inc(temp_in, 16)

                @block.scalar
                def _(act):
                    raw = gates[:].rearrange("p t (h n) -> p n t h", n=NG)
                    for n in (4, 1, 3, 0, 2):
                        nc.scalar.activation(tanhs[:, n], raw[:, n], ACT.Tanh, scale=1.0 if n % 2 else 0.5).then_inc(tanh_done, 1)
                    act.wait_ge(steps, 3)
                    nc.scalar.activation(sine[:], phase[:], ACT.Sin, scale=1.5707962).then_inc(sine_done, 1)
                    act.wait_ge(steps, 8)
                    nc.scalar.activation(gate[:], amps[:], ACT.Tanh, scale=half_temp[:, 0:1]).then_inc(gate_tanh, 1)
                    act.wait_ge(steps, 1)
                    nc.scalar.activation(log_rate[:], rate[:], ACT.Ln).then_inc(rate_log, 1)
                    act.wait_ge(sums_ready, 1)
                    nc.scalar.activation(decay[:], p_sum[:, 0:NT * H].rearrange("p (t h) -> p t h", h=H), ACT.Exp).then_inc(df_ready, 1)

                @block.tensor
                def _(pe):
                    pe.wait_ge(rate_log, 1)
                    of = log_rate[:].rearrange("p (g j) h -> p j g h", j=3)
                    to = p_sum[:, 0:NT * H].rearrange("p (g j h) -> p j g h", j=3, h=H)
                    nc.tensor.matmul(to[:, 0], u_pre, of[:, 0], start=True, stop=True, skip_group_check=True)
                    for b in range(2):
                        nc.tensor.matmul(to[:, 1 + b], u_txt, of[:, 1 + b], start=False, stop=False, skip_group_check=True)
                        last = nc.tensor.matmul(to[:, 1 + b], prefix_of[b], of[:, 0], start=False, stop=True, skip_group_check=True)
                    last.then_inc(sums_ready, 1)

                @block.vector
                def _(dve):
                    v = nc.vector

                    def step(n, ins):
                        ins.then_inc(steps, 1)
                        dve.wait_ge(steps, n)

                    dve.wait_ge(tanh_done, 1)
                    step(1, v.tensor_scalar(rate[:], tanhs[:, 4], 0.325, 0.625, ALU.mult, ALU.add))
                    step(2, v.tensor_scalar(keep[:], rate[:], -1.0, 1.0, ALU.mult, ALU.add))
                    dve.wait_ge(tanh_done, 3)
                    step(3, v.tensor_tensor(phase[:], tanhs[:, 1], tanhs[:, 3], ALU.subtract))
                    dve.wait_ge(tanh_done, 5)
                    step(4, v.tensor_scalar(amp[:], tanhs[:, 0], 0.5, 0.5, ALU.mult, ALU.add))
                    step(5, v.tensor_scalar(cosine[:], tanhs[:, 2], 0.5, 0.5, ALU.mult, ALU.add))
                    step(6, v.tensor_tensor(amp[:], amp[:], cosine[:], ALU.mult))
                    dve.wait_ge(temp_in, 16)
                    dve.wait_ge(sine_done, 1)
                    v.tensor_scalar(half_temp[:], half_temp[:], 0.5, None, ALU.mult)
                    step(7, v.tensor_tensor(cosine[:], amp[:], sine[:], ALU.mult))
                    v.tensor_tensor(cosine[:], cosine[:], sine[:], ALU.mult).then_inc(temp_in, 1)
                    dve.wait_ge(temp_in, 17)
                    step(8, v.scalar_tensor_tensor(amps[:], cosine[:], -2.0, amp[:], ALU.mult, ALU.add))
                    dve.wait_ge(df_ready, 1)
                    step(9, v.tensor_scalar(safe[:], decay[:], 1e-8, None, ALU.add))
                    step(10, v.reciprocal(inv_df[:], safe[:]))
                    v.tensor_scalar(clip_hi[:], inv_df[:], 5.0, None, ALU.mult).then_inc(steps, 1)
                    v.tensor_scalar(clip_lo[:], inv_df[:], -5.0, None, ALU.mult).then_inc(steps, 1)
                    step(13, v.tensor_tensor(gain_z[:], keep[:], inv_df[:], ALU.mult))
                    dve.wait_ge(gate_tanh, 1)
                    step(14, v.tensor_scalar(gate[:], gate[:], 0.5, 0.5, ALU.mult, ALU.add))
                    step(15, v.tensor_tensor(gain_kv[:], gate[:], gain_z[:], ALU.mult))

        late = mid.enter_context(ExitStack())
        def sbuf(name, shape, dt=F32):
            return late.enter_context(nc.sbuf_tensor(name, shape, dt))

        num = sbuf("num", [P, NT, D])
        den = sbuf("den", [P, NT, H])
        kmax = sbuf("kmax", [P, NT, H])
        vmax = sbuf("vmax", [P, NT, H])
        unit_rank = sbuf("unit_rank", [P, UNITS], mybir.dt.int32)
        pair_flag = sbuf("pair_flag", [P, PAIRS], mybir.dt.int32)

        def heads(ap, n=DH):
            return ap.rearrange("p j (h d) -> p (j h) d", d=n)

        def wide(ap, n):
            return ap.rearrange("p j h -> p (j h)").unsqueeze(2).broadcast_to([P, ap.shape[1] * ap.shape[2], n])

        with ExitStack() as ctx:
            def sb(name, shape):
                return ctx.enter_context(nc.sbuf_tensor(name, shape, F32))

            def ps(name, shape):
                return ctx.enter_context(nc.psum_tensor(name, shape, F32))

            def sem(name):
                return ctx.enter_context(nc.semaphore(name))

            HC = C // DH
            qd = sb("qd", [P, 3, D])
            kg = sb("kg", [P, 3, D])
            kpre = sb("kpre", [P, 2, D])
            kz = sb("kz", [P, 3, D])
            vpad = sb("vpad", [P, 3, 2 * D])
            qkt = sb("qkt", [C, 3, 4, P])
            qm = sb("qm", [C, 3, HC, P])
            st = sb("st", [P, 3, HC, P])
            state = sb("state", [C, 2, 2, C])
            numt = sb("numt", [C, 2, P])
            zd = sb("zd", [P, 1, D])
            zq = sb("zq", [P, 1, D])
            p_s = ps("p_scores", [P, 4, 512])
            p_qt = ps("p_qt", [P, 512])
            p_n = ps("p_numt", [P, 512])
            p_st = ps("p_st", [P, 512])
            p_b = ps("p_b", [P, 512])

            (vpad_zero, qk_ready, kpre_ready, kz_ready, v_ready, t_ready, qkt_ready, qm0_ready, qm1_ready, sc_ready, st_ready,
             av_ready, s_ready, state_in, numt_ready, zb_ready, num_out, z_step, kv_max) = (sem(x) for x in (
                 "vpad_zero", "qk_ready", "kpre_ready", "kz_ready", "v_ready", "t_ready", "qkt_ready", "qm0_ready", "qm1_ready",
                 "sc_ready", "st_ready", "av_ready", "s_ready", "state_in", "numt_ready", "zb_ready", "num_out", "z_step", "kv_max"))

            def pairs(eng, body):
                body(0)
                with eng.Fori(1, PAIRS - 1) as p:
                    body(p)
                body(PAIRS - 1)

            def is_first(p, j):
                return isinstance(p, int) and p == 0 and j == 0

            def is_last(p, j):
                return isinstance(p, int) and p == PAIRS - 1 and j == 2

            with nc.Block() as block:
                @block.gpsimd
                def _(pool):
                    g = nc.gpsimd

                    def body(p):
                        for j in range(3):
                            n = 3 * p + j
                            after(pool, t_ready, n - 2)
                            if j == 0:
                                after(pool, kpre_ready, p)
                            tile = ds(n, 1)
                            g.tensor_tensor(heads(qd[:, j:j + 1]), heads(qk[:, tile, 0:D]), wide(decay[:, tile, :], DH), ALU.mult).then_inc(qk_ready, 1)
                            g.tensor_tensor(heads(kg[:, j:j + 1]), heads(qk[:, tile, D:2 * D]), wide(gain_kv[:, tile, :], DH), ALU.mult).then_inc(qk_ready, 1)
                            if j == 0:
                                after(pool, s_ready, p)
                                wait_apart(pool, qk_ready, 2 * n + 2)
                                rows_of = cst[:, sel0:sel0 + 2 * P].rearrange("p (b t) -> p b t", b=2)[:, :, 0:1].broadcast_to([P, 2, D])
                                g.tensor_tensor(kpre[:], kg[:, 0:1].broadcast_to([P, 2, D]), rows_of, ALU.mult).then_inc(kpre_ready, 1)

                    pairs(pool, body)

                @block.scalar
                def _(act):
                    def v_in(n, j):
                        after(act, av_ready, 2 * n - 4)
                        to = vpad[:, j].rearrange("p (m c) -> p m c", c=64)
                        for b in range(2):
                            nc.scalar.copy(to[:, :, 48 * b:48 * b + DH],
                                           val[:, ds(n, 1), :].rearrange("p o (m b e) -> p (o m) b e", b=2, e=DH)[:, :, b]).then_inc(v_ready, 1)

                    def qk_in(n, j):
                        after(act, av_ready, 2 * n - 4)
                        wait_apart(act, t_ready, n + 1)
                        nc.scalar.copy(qkt[:, j], p_qt[0:C, :].rearrange("p (c t) -> p c t", c=4)).then_inc(qkt_ready, 1)
                        after(act, sc_ready, 2 * n - 1)
                        wait_apart(act, qkt_ready, n + 1)
                        for h in range(HC):
                            nc.scalar.mul(qm[:, (2 * j + 1) % 3, h], qkt[:, j, 1], head_of[:, h:h + 1]).then_inc(qm1_ready, 1)

                    def num_t(n):
                        after(act, zb_ready, n)
                        wait_apart(act, av_ready, 2 * n + 2)
                        nc.scalar.copy(numt[:], p_n[0:C, 0:2 * P].rearrange("p (c t) -> p c t", c=2)).then_inc(numt_ready, 1)

                    def body(p):
                        for j in range(3):
                            n = 3 * p + j
                            if not is_first(p, j):
                                num_t(n - 1)
                            if not is_last(p, j):
                                v_in(n + 1, (j + 1) % 3)
                                qk_in(n + 1, (j + 1) % 3)

                    act.wait_ge(vpad_zero, 1)
                    qk_in(0, 0)
                    v_in(0, 0)
                    pairs(act, body)
                    num_t(NT - 1)

                @block.tensor
                def _(pe):
                    mm = nc.tensor.matmul

                    def transposes(n, j):
                        after(pe, qkt_ready, n)
                        wait_apart(pe, qk_ready, 2 * n + 2)
                        for i in range(4):
                            last = nc.tensor.transpose(p_qt[0:C, i * P:(i + 1) * P], (qd, kg)[i // 2][:, j, (i % 2) * C:(i % 2 + 1) * C], ident)
                        last.then_inc(t_ready, 1)

                    def scores(n, j, c):
                        after(pe, st_ready, 2 * n + c - 1)
                        if c == 0:
                            wait_apart(pe, qkt_ready, n + 1)
                            wait_apart(pe, qm0_ready, n + 1)
                        else:
                            wait_apart(pe, qm1_ready, HC * n + HC)
                        for half in range(2):
                            last = mm(p_s[:, 2 * c + half, 0:3 * P], qkt[:, j, 2 + c], qm[:, (2 * j + c) % 3, 3 * half:3 * half + 3].rearrange("p h t -> p (h t)"),
                                      start=True, stop=True)
                        last.then_inc(sc_ready, 1)

                    def values(p, j, c):
                        n = 3 * p + j
                        wait_apart(pe, st_ready, 2 * n + c + 1)
                        if c == 0:
                            after(pe, numt_ready, n)
                            wait_apart(pe, v_ready, 2 * n + 2)
                        to = p_n[:, c * P:(c + 1) * P]
                        if j:
                            wait_apart(pe, state_in, p + 1)
                            mm(to[0:C], state[:, j - 1, c], qkt[:, j, c], start=True, stop=False, skip_group_check=True)
                        for b in range(2):
                            for a in range(3):
                                h = HC * c + 2 * a + b
                                last = mm(to[32 * a:32 * a + 32], vpad[:, j, 32 * h:32 * h + 32], st[:, (2 * j + c) % 3, 2 * a + b],
                                          start=(j == 0 and b == 0), stop=(b == 1), skip_group_check=True, tile_position=(0, 32 * a))
                        last.then_inc(av_ready, 1)

                    def states(p):
                        wait_apart(pe, kpre_ready, p + 1)
                        after(pe, state_in, p)
                        for b in range(2):
                            for c in range(2):
                                last = mm(p_st[0:C, (2 * b + c) * C:(2 * b + c + 1) * C], kpre[:, b, c * C:(c + 1) * C],
                                          val[:, ds(3 * p, 1), c * C:(c + 1) * C].rearrange("p o d -> p (o d)"), start=True, stop=True, skip_group_check=True)
                        last.then_inc(s_ready, 1)

                    def z_and_back(n, j, z=True, back=True):
                        after(pe, z_step, 3 * n - 2)
                        after(pe, num_out, n - 1)
                        if z:
                            wait_apart(pe, kz_ready, n + 1)
                            last = mm(p_b[:, 0:D], u_txt if j else u_pre, kz[:, j], start=True, stop=(j == 0), skip_group_check=True)
                            if j:
                                last = mm(p_b[:, 0:D], prefix_of[j - 1], kz[:, 0], start=False, stop=True, skip_group_check=True)
                        if back:
                            wait_apart(pe, numt_ready, n)
                            for c in range(2):
                                last = nc.tensor.transpose(p_b[:, D + c * C:D + (c + 1) * C], numt[:, c], ident[0:C, 0:C])
                        last.then_inc(zb_ready, 1)

                    def body(p):
                        for j in range(3):
                            n = 3 * p + j
                            scores(n, j, 0)
                            if not is_first(p, j):
                                values(p - (j == 0), (j - 1) % 3, 1)
                            scores(n, j, 1)
                            if not is_last(p, j):
                                transposes(n + 1, (j + 1) % 3)
                            if j == 0:
                                states(p)
                            values(p, j, 0)
                            z_and_back(n, j, back=not is_first(p, j))

                    pe.wait_ge(vpad_zero, 1)
                    transposes(0, 0)
                    pairs(pe, body)
                    values(PAIRS - 1, 2, 1)
                    z_and_back(NT, 0, z=False)

                @block.vector
                def _(dve):
                    v = nc.vector

                    def q_in(n, j):
                        after(dve, sc_ready, 2 * n - 2)
                        wait_apart(dve, qkt_ready, n + 1)
                        v.tensor_tensor(qm[:, (2 * j) % 3], qkt[:, j, 0].unsqueeze(1).broadcast_to([C, HC, P]),
                                        head_of.unsqueeze(2).broadcast_to([C, HC, P]), ALU.mult).then_inc(qm0_ready, 1)

                    def mask(n, j, c):
                        after(dve, av_ready, 2 * n + c - 2)
                        wait_apart(dve, sc_ready, 2 * n + c + 1)
                        v.tensor_tensor(st[:, (2 * j + c) % 3].rearrange("p (a h) t -> p a h t", a=2), p_s[:, 2 * c:2 * c + 2, 0:3 * P].rearrange("p a (h t) -> p a h t", h=3),
                                        (u_txt if j else u_pre).unsqueeze(1).unsqueeze(1).broadcast_to([P, 2, 3, P]), ALU.mult).then_inc(st_ready, 1)

                    def body(p):
                        for j in range(3):
                            n = 3 * p + j
                            tile = ds(n, 1)
                            mask(n, j, 0)
                            after(dve, zb_ready, n)
                            v.tensor_tensor(heads(kz[:, j:j + 1]), heads(qk[:, tile, D:2 * D]), wide(gain_z[:, tile, :], DH), ALU.mult).then_inc(kz_ready, 1)
                            v.tensor_reduce(kmax[:, tile, :].rearrange("p o h -> p (o h)"), heads(qk[:, tile, D:2 * D]), AX.X, ALU.max).then_inc(kv_max, 1)
                            mask(n, j, 1)
                            v.tensor_reduce(vmax[:, tile, :].rearrange("p o h -> p (o h)"), heads(val[:, tile, :]), AX.X, ALU.max, apply_absolute_value=True).then_inc(kv_max, 1)
                            if not is_last(p, j):
                                q_in(n + 1, (j + 1) % 3)
                            if j == 0:
                                wait_apart(dve, s_ready, p + 1)
                                after(dve, av_ready, 6 * p)
                                v.tensor_tensor(state[:].rearrange("p b c d -> p (b c) d"), p_st[0:C, 0:4 * C].rearrange("p (x d) -> p x d", x=4),
                                                same_head.unsqueeze(1).broadcast_to([C, 4, C]), ALU.mult).then_inc(state_in, 1)
                            wait_apart(dve, zb_ready, n + 1)
                            v.tensor_tensor(heads(zd[:]), p_b[:, 0:D].rearrange("p (h d) -> p h d", d=DH), wide(decay[:, tile, :], DH), ALU.mult).then_inc(z_step, 1)
                            if not is_first(p, j):
                                num_back(n - 1)
                            wait_apart(dve, z_step, 3 * n + 1)
                            v.scalar_tensor_tensor(zq[:], zd[:], 1e4, qk[:, tile, 0:D], ALU.min, ALU.mult).then_inc(z_step, 1)
                            wait_apart(dve, z_step, 3 * n + 2)
                            v.tensor_reduce(den[:, tile, :].rearrange("p o h -> p (o h)"), heads(zq[:]), AX.X, ALU.add).then_inc(z_step, 1)

                    def num_back(n):
                        v.tensor_copy(num[:, ds(n, 1), :], p_b[:, D:2 * D].unsqueeze(1)).then_inc(num_out, 1)

                    v.memset(vpad[:], 0.0).then_inc(vpad_zero, 1)
                    q_in(0, 0)
                    pairs(dve, body)
                    dve.wait_ge(zb_ready, NT + 1)
                    num_back(NT - 1)

        with ExitStack() as ctx:
            def sb(name, shape, dt=F32):
                return ctx.enter_context(nc.sbuf_tensor(name, shape, dt))

            def ps(name, shape):
                return ctx.enter_context(nc.psum_tensor(name, shape, F32))

            def sem(name):
                return ctx.enter_context(nc.semaphore(name))

            UC = HG * DH * DH
            bound = sb("bound", [P, 2, NT, H])
            beyond = sb("beyond", [P, NT, H])
            beyond_hg = sb("beyond_hg", [P, NT, NHG])
            unit_on = sb("unit_on", [P, UNITS])
            counts_up = sb("counts_up", [P, 2, 32 + UNITS])
            k_u = sb("k_u", [P, 3, HG * DH])
            q_u = sb("q_u", [P, 3, HG * DH])
            outer = sb("outer", [P, 3, UC])
            prod = sb("prod", [P, 2, UC])
            p_f = ps("p_f", [P, 512])
            p_g = ps("p_g", [P, 3, 1024])
            flag_step, flags_summed, flags_ready, ku_ready, outer_made, outer_ready, state_ready, state_read, num_ready = (
                sem(x) for x in ("flag_step", "flags_summed", "flags_ready", "ku_ready", "outer_made", "outer_ready",
                                 "state_ready", "state_read", "num_ready"))

            def units(eng, unit):
                eng.wait_ge(flags_ready, 2)
                with eng.Fori(0, PAIRS) as p:
                    flag = eng.value_load(pair_flag[0:1, ds(p, 1)], min_val=0, max_val=UNITS)
                    with eng.If(flag != 0):
                        for g in range(NHG):
                            rank = eng.value_load(unit_rank[0:1, ds(NHG * p + g, 1)], min_val=0, max_val=UNITS)
                            with eng.If(rank != 0):
                                unit(p, g, rank)

            with nc.Block() as block:
                @block.tensor
                def _(pe):
                    mm = nc.tensor.matmul
                    pe.sem_inc(state_ready, 3)
                    pe.wait_ge(flag_step, 4)
                    by_tile = beyond_hg[:].rearrange("p (g j) n -> p j g n", j=3)
                    to = p_f[:, 0:UNITS].rearrange("p (g n) -> p g n", n=NHG)
                    mm(to, prefix_of[0], by_tile[:, 0], start=True, stop=False)
                    mm(to, prefix_of[1], by_tile[:, 0], start=False, stop=False)
                    mm(to, u_ones, by_tile[:, 1], start=False, stop=False)
                    mm(to, u_ones, by_tile[:, 2], start=False, stop=True).then_inc(flags_summed, 1)

                    def unit(p, g, rank):
                        for j in range(3):
                            wait_apart(pe, outer_ready, HG * 3 * rank + HG * (j + 1))
                            wait_apart(pe, state_read, 3 * rank)
                            for half in range(2):
                                cols = slice(512 * half, 512 * half + 512)
                                last = mm(p_g[:, j, cols], u_txt if j else u_pre, outer[:, j, cols], start=True, stop=(j == 0))
                                if j:
                                    last = mm(p_g[:, j, cols], prefix_of[j - 1], outer[:, 0, cols], start=False, stop=True)
                            last.then_inc(state_ready, 1)

                    units(pe, unit)

                @block.vector
                def _(dve):
                    v = nc.vector

                    def step(n, ins):
                        ins.then_inc(flag_step, 1)
                        dve.wait_ge(flag_step, n)

                    v.sem_inc(ku_ready, 2)
                    v.sem_inc(outer_made, 3)
                    v.sem_inc(outer_ready, 3 * HG)
                    v.sem_inc(state_read, 3)
                    v.memset(counts_up[:], 0.0)
                    step(1, v.tensor_tensor(bound[:, 0], kmax[:], vmax[:], ALU.mult))
                    step(2, v.tensor_tensor(bound[:, 1], bound[:, 0], gain_kv[:], ALU.mult))
                    step(3, v.tensor_tensor(beyond[:], bound[:, 1], clip_hi[:], ALU.is_gt))
                    step(4, v.tensor_reduce(beyond_hg[:].rearrange("p t n -> p (t n)"), beyond[:].rearrange("p t (n h) -> p (t n) h", h=HG), AX.X, ALU.max))
                    dve.wait_ge(flags_summed, 1)
                    step(5, v.tensor_scalar(unit_on[:], p_f[:, 0:UNITS], 1.0, None, ALU.min))
                    v.tensor_reduce(pair_flag[:], unit_on[:].rearrange("p (g n) -> p g n", n=NHG), AX.X, ALU.max).then_inc(flags_ready, 1)
                    step(6, v.tensor_copy(counts_up[:, 0, 32:], unit_on[:]))
                    n, shift, u = 7, 1, 0
                    while shift < UNITS:
                        step(n, v.tensor_tensor(counts_up[:, 1 - u, 32:], counts_up[:, u, 32:], counts_up[:, u, 32 - shift:32 + UNITS - shift], ALU.add))
                        n, shift, u = n + 1, 2 * shift, 1 - u
                    v.tensor_tensor(unit_rank[:], counts_up[:, u, 32:], unit_on[:], ALU.mult).then_inc(flags_ready, 1)

                    def unit(p, g, rank):
                        hs = slice(g * HG * DH, (g + 1) * HG * DH)
                        tiles3 = ds(3 * p, 3)

                        def of_heads(x):
                            return x[:, tiles3, g * HG:(g + 1) * HG].unsqueeze(3).broadcast_to([P, 3, HG, DH])

                        def apart(x):
                            return x.rearrange("p j (h d) -> p j h d", d=DH)

                        v.tensor_tensor(apart(k_u[:]), apart(qk[:, tiles3, D + g * HG * DH:D + (g + 1) * HG * DH]), of_heads(gain_kv), ALU.mult).then_inc(ku_ready, 1)
                        v.tensor_tensor(apart(q_u[:]), apart(qk[:, tiles3, hs]), of_heads(decay), ALU.mult).then_inc(ku_ready, 1)
                        wait_apart(dve, ku_ready, 2 * rank + 1)
                        for j in range(3):
                            kk = k_u[:, j].rearrange("p (h d) -> p h d", d=DH).unsqueeze(3).broadcast_to([P, HG, DH, DH])
                            vv = val[:, ds(3 * p + j, 1), hs].rearrange("p o (h e) -> p (o h) e", e=DH).unsqueeze(2).broadcast_to([P, HG, DH, DH])
                            v.tensor_tensor(outer[:, j].rearrange("p (h d e) -> p h d e", d=DH, e=DH), kk, vv, ALU.mult).then_inc(outer_made, 1)
                            wait_apart(dve, outer_made, 3 * rank + j + 1)
                            for h in range(HG):
                                head = g * HG + h
                                hi, lo = (x[:, ds(3 * p + j, 1), head:head + 1].rearrange("p a b -> p (a b)") for x in (clip_hi, clip_lo))
                                o = outer[:, j, h * DH * DH:(h + 1) * DH * DH]
                                v.tensor_scalar(o, o, hi, lo, ALU.min, ALU.max).then_inc(outer_ready, 1)
                        for j in range(3):
                            wait_apart(dve, state_ready, 3 * rank + j + 1)
                            if j == 0:
                                wait_apart(dve, ku_ready, 2 * rank + 2)
                            qq = q_u[:, j].rearrange("p (h d) -> p h d", d=DH).unsqueeze(3).broadcast_to([P, HG, DH, DH])
                            v.tensor_tensor(prod[:, j % 2].rearrange("p (h d e) -> p h d e", d=DH, e=DH), p_g[:, j].rearrange("p (h d e) -> p h d e", d=DH, e=DH),
                                            qq, ALU.mult).then_inc(state_read, 1)
                            wait_apart(dve, state_read, 3 * rank + j + 1)
                            v.tensor_reduce(num[:, ds(3 * p + j, 1), hs].rearrange("p o (h e) -> p (o h) e", e=DH),
                                            prod[:, j % 2].rearrange("p (h d e) -> p h e d", d=DH, e=DH), AX.X, ALU.add).then_inc(num_ready, 1)

                    units(dve, unit)

        with ExitStack() as ctx:
            def sb(name, shape):
                return ctx.enter_context(nc.sbuf_tensor(name, shape, F32))

            def ps(name, shape):
                return ctx.enter_context(nc.psum_tensor(name, shape, F32))

            def sem(name):
                return ctx.enter_context(nc.semaphore(name))

            wout_raw = sb("wout_raw", [C, 2, D])
            wout = sb("wout", [C, 2, D])
            mn = sb("mn", [C, 2])
            mnb_wide = sb("mnb_wide", [C, P])
            bout = sb("bout", [P, D])
            wg_raw = sb("wg_raw", [C, 2, E])
            wgc = sb("wgc", [C, 2, E])
            mean_w = sb("mean_w", [C, P])
            den1 = sb("den1", [P, NT, H])
            rden = sb("rden", [P, NT, H])
            att = sb("att", [P, 3, D])
            sums = sb("sums", [P, 3, H])
            means = sb("means", [P, 3, H])
            centred = sb("centred", [P, 3, D])
            sq = sb("sq", [P, 3, D])
            var = sb("var", [P, 3, H])
            eps = sb("eps", [P, 1])
            deviation = sb("deviation3", [P, 3, H])
            rstd = sb("rstd3", [P, 3, H])
            attn = sb("attn", [P, 3, D])
            attn_t = sb("attn_t", [C, 3, 2, P])
            hid_t = sb("hid_t", [C, 3, 2, P])
            new_hid = sb("new_hid", [P, 3, D])
            bst = sb("bst2", [P, 3, 6])
            mv = sb("mv2", [P, 3, 2])

            p_at = ps("p_at", [P, 2, 512])
            p_ht = ps("p_hid_t", [P, 2, 512])
            p_o = ps("p_o", [P, 2, 512])
            p_l = ps("p_l", [P, 512])

            (small_in, prep, prep_pe, fold, rden_ready, att_step, sq_ready, var_ready, var_step, rstd_ready, attn_ready,
             att_tr, attn_t_ready, proj_ready, hid_ready, hid_tr, hid_t_ready, hid_kept, st_done, mv_ready, mv_kept,
             logit_ready, logit_read) = (sem(x) for x in (
                 "c_small_in", "c_prep", "c_prep_pe", "c_fold", "rden_ready", "att_step", "sq_ready", "var_ready",
                 "var_step", "c_rstd_ready", "attn_ready", "att_tr", "attn_t_ready", "c_proj_ready", "hid_ready",
                 "c_hid_tr", "hid_t_ready", "hid_kept", "c_st_done", "c_mv_ready", "mv_kept", "logit_ready", "logit_read"))

            def bank_of(t, j, n):
                return t[:, j // 2, (j % 2) * n:(j % 2) * n + n]

            with nc.Block() as block:
                @block.sync
                def _(sp):
                    sp.dma_start(wout_raw[:], w_out).then_inc(small_in, 16)
                    sp.dma_start(mn[:], mn_gb).then_inc(small_in, 16)
                    sp.dma_start(bout[:], b_out).then_inc(small_in, 16)
                    sp.dma_start(wg_raw[:], wg).then_inc(small_in, 16)

                @block.gpsimd
                def _(pool):
                    g = nc.gpsimd
                    pool.wait_ge(fold, 4)
                    with pool.Fori(0, PAIRS) as p:
                        g.tensor_tensor(hid[:, ds(3 * p, 3), :], hid[:, ds(3 * p, 3), :], bout[:].unsqueeze(1).broadcast_to([P, 3, D]), ALU.add).then_inc(prep, 1)

                @block.scalar
                def _(act):
                    def square(p):
                        wait_apart(act, att_step, 4 * p + 4)
                        nc.scalar.activation(sq[:], centred[:], ACT.Square).then_inc(sq_ready, 1)

                    def root(p):
                        wait_apart(act, var_ready, p + 1)
                        nc.scalar.activation(deviation[:], var[:], ACT.Sqrt, bias=eps[:, 0:1], scale=1.0 / DH).then_inc(var_step, 1)

                    def to_sbuf(t, bank, done):
                        for i, n in ((0, 2), (1, 1)):
                            nc.scalar.copy(t[:, 2 * i:2 * i + n], bank[0:C, i, 0:n * 2 * P].rearrange("p (j c t) -> p j c t", j=n, c=2)).then_inc(done, 1)

                    def body(p):
                        more = not (isinstance(p, int) and p == PAIRS - 1)
                        wait_apart(act, att_tr, p + 1)
                        after(act, proj_ready, p)
                        to_sbuf(attn_t, p_at, attn_t_ready)
                        if more:
                            square(p + 1)
                        if not (isinstance(p, int) and p == 0):
                            hid_out(p - 1)
                        if more:
                            root(p + 1)

                    def hid_out(p):
                        wait_apart(act, hid_tr, p + 1)
                        wait_apart(act, logit_ready, p + 1)
                        to_sbuf(hid_t, p_ht, hid_t_ready)
                        nc.scalar.copy(hid[:, ds(3 * p, 3), :], new_hid[:]).then_inc(hid_kept, 1)

                    nc.scalar.sem_inc(hid_t_ready, 2)
                    act.wait_ge(rden_ready, 2)
                    square(0)
                    root(0)
                    pairs(act, body)
                    hid_out(PAIRS - 1)

                @block.tensor
                def _(pe):
                    mm = nc.tensor.matmul

                    def turn(rows3, banks):
                        for j in range(3):
                            for c in range(2):
                                last = nc.tensor.transpose(bank_of(banks, j, 2 * P)[0:C, c * P:(c + 1) * P], rows3[:, j, c * C:(c + 1) * C], ident)
                        return last

                    def logit(p):
                        wait_apart(pe, logit_read, p + 1)
                        wait_apart(pe, hid_t_ready, 2 * p + 4)
                        for j in range(3):
                            for c in range(2):
                                last = mm(p_l[:, j * E:(j + 1) * E], hid_t[:, j, c], wgc[:, c], start=(c == 0), stop=(c == 1), skip_group_check=True)
                        last.then_inc(logit_ready, 1)

                    def body(p):
                        first = isinstance(p, int) and p == 0
                        after(pe, attn_t_ready, 2 * p)
                        wait_apart(pe, attn_ready, p + 1)
                        turn(attn, p_at).then_inc(att_tr, 1)
                        if not first:
                            wait_apart(pe, hid_t_ready, 2 * p)
                            wait_apart(pe, hid_ready, 2 * p)
                            turn(new_hid, p_ht).then_inc(hid_tr, 1)
                        after(pe, hid_ready, 2 * p)
                        wait_apart(pe, attn_t_ready, 2 * p + 2)
                        for j in range(3):
                            for c in range(2):
                                last = mm(bank_of(p_o, j, D), attn_t[:, j, c], wout[:, c], start=(c == 0), stop=(c == 1), skip_group_check=True)
                        last.then_inc(proj_ready, 1)
                        if not first:
                            logit(p - 1)

                    nc.tensor.sem_inc(logit_ready, 1)
                    pe.wait_ge(fold, 3)
                    mm(p_o[:, 0, 0:D], mnb_wide[:], wout_raw[:, 0], start=True, stop=False)
                    mm(p_o[:, 0, 0:D], mnb_wide[:], wout_raw[:, 1], start=False, stop=True).then_inc(prep_pe, 1)
                    mm(p_o[0:C, 1, 0:E], mean_w[:, 0:C], wg_raw[:, 0], start=True, stop=False)
                    mm(p_o[0:C, 1, 0:E], mean_w[:, 0:C], wg_raw[:, 1], start=False, stop=True).then_inc(prep_pe, 1)
                    pe.wait_ge(fold, 6)
                    pairs(pe, body)
                    pe.wait_ge(hid_t_ready, 2 * PAIRS)
                    pe.wait_ge(hid_ready, 2 * PAIRS)
                    turn(new_hid, p_ht).then_inc(hid_tr, 1)
                    logit(PAIRS - 1)

                @block.vector
                def _(dve):
                    v = nc.vector
                    v.sem_inc(logit_read, 1)
                    v.memset(eps[:], 1e-5).then_inc(rden_ready, 1)
                    v.tensor_scalar(den1[:], den[:], 1e-4, None, ALU.add).then_inc(rden_ready, 1)
                    dve.wait_ge(rden_ready, 2)
                    v.reciprocal(rden[:], den1[:]).then_inc(rden_ready, 1)
                    dve.wait_ge(small_in, 64)
                    v.memset(mean_w[:], 1.0 / D).then_inc(fold, 1)
                    v.tensor_copy(mnb_wide[:], mn[:, 1:2].broadcast_to([C, P])).then_inc(fold, 1)
                    v.tensor_scalar(wout[:].rearrange("p c d -> p (c d)"), wout_raw[:].rearrange("p c d -> p (c d)"), mn[:, 0:1], None, ALU.mult).then_inc(fold, 1)
                    dve.wait_ge(prep_pe, 2)
                    v.tensor_tensor(bout[:], bout[:], p_o[:, 0, 0:D], ALU.add).then_inc(fold, 1)
                    for c in range(2):
                        v.tensor_tensor(wgc[:, c], wg_raw[:, c], p_o[0:C, 1, 0:E], ALU.subtract).then_inc(fold, 1)
                    dve.wait_ge(rden_ready, 3)

                    def centre(p):
                        v.tensor_tensor(heads(att[:]), heads(num[:, ds(3 * p, 3), :]), wide(rden[:, ds(3 * p, 3), :], DH), ALU.mult).then_inc(att_step, 1)
                        wait_apart(dve, att_step, 4 * p + 1)
                        v.tensor_reduce(sums[:].rearrange("p j h -> p (j h)"), heads(att[:]), AX.X, ALU.add).then_inc(att_step, 1)
                        wait_apart(dve, att_step, 4 * p + 2)
                        v.tensor_scalar(means[:], sums[:], 1.0 / DH, None, ALU.mult).then_inc(att_step, 1)
                        wait_apart(dve, att_step, 4 * p + 3)
                        v.tensor_tensor(heads(centred[:]), heads(att[:]), wide(means[:], DH), ALU.subtract).then_inc(att_step, 1)

                    def variance(p):
                        wait_apart(dve, sq_ready, p + 1)
                        v.tensor_reduce(var[:].rearrange("p j h -> p (j h)"), heads(sq[:]), AX.X, ALU.add).then_inc(var_ready, 1)

                    def normed(p):
                        wait_apart(dve, var_step, p + 1)
                        v.reciprocal(rstd[:], deviation[:]).then_inc(rstd_ready, 1)
                        after(dve, att_tr, p)
                        wait_apart(dve, rstd_ready, p + 1)
                        v.tensor_tensor(heads(attn[:]), heads(centred[:]), wide(rstd[:], DH), ALU.mult).then_inc(attn_ready, 1)

                    def residual(p):
                        after(dve, hid_tr, p)
                        after(dve, hid_kept, p)
                        wait_apart(dve, prep, p + 1)
                        wait_apart(dve, proj_ready, p + 1)
                        for i, n in ((0, 2), (1, 1)):
                            v.tensor_tensor(new_hid[:, 2 * i:2 * i + n], hid[:, ds(3 * p + 2 * i, n), :],
                                            p_o[:, i, 0:n * D].rearrange("p (j d) -> p j d", j=n), ALU.add).then_inc(hid_ready, 1)

                    def stats(p):
                        wait_apart(dve, hid_ready, 2 * p + 2)
                        after(dve, mv_ready, 3 * p)
                        for j in range(3):
                            v.bn_stats(bst[:, j], new_hid[:, j]).then_inc(st_done, 1)
                        after(dve, mv_kept, p)
                        for j in range(3):
                            wait_apart(dve, st_done, 3 * p + j + 1)
                            v.bn_aggr(mv[:, j], bst[:, j]).then_inc(mv_ready, 1)

                    def keep(p):
                        wait_apart(dve, mv_ready, 3 * p + 3)
                        v.tensor_copy(moments[:, ds(3 * p, 3), :], mv[:]).then_inc(mv_kept, 1)

                    def logits_out(p):
                        wait_apart(dve, logit_ready, p + 2)
                        v.tensor_copy(logits[:, ds(3 * p, 3), :], p_l[:, 0:3 * E].rearrange("p (j e) -> p j e", j=3)).then_inc(logit_read, 1)

                    def body(p):
                        more = not (isinstance(p, int) and p == PAIRS - 1)
                        if more:
                            centre(p + 1)
                        residual(p)
                        if more:
                            variance(p + 1)
                        stats(p)
                        if more:
                            normed(p + 1)
                        keep(p)
                        if not (isinstance(p, int) and p == 0):
                            logits_out(p - 1)

                    centre(0)
                    variance(0)
                    normed(0)
                    pairs(dve, body)
                    logits_out(PAIRS - 1)

        if dbg:
            dump(nc, dbg, dict(hid=hid, logits=logits, moments=moments, decay=decay, qk=qk, val=val))
        mid.close()

        def sbuf(name, shape, dt=F32):
            return top.enter_context(nc.sbuf_tensor(name, shape, dt))

        w2s = sbuf("w2s", [P, E, KC, D])
        b2s = sbuf("b2s", [P, E, D])
        expert_of = sbuf("expert_of", [P, SLOT_TILES], mybir.dt.int32)
        w2_in = top.enter_context(nc.semaphore("w2_in"))
        with ExitStack() as ctx:
            def sb(name, shape, dt=F32):
                return ctx.enter_context(nc.sbuf_tensor(name, shape, dt))

            def sem(name):
                return ctx.enter_context(nc.semaphore(name))

            cs = sb("cs", [P, CSMALL])
            valid = cs[:, valid0:valid0 + NT]
            token = cs[:, token0:token0 + NT]
            nowhere = cs[:, nowhere0:nowhere0 + NT]
            down = cs[:, down0:down0 + E]
            tile_steps = cs[:, steps0:steps0 + E * MAXN].rearrange("p (e n) -> p e n", n=MAXN)
            tile_no = cs[:, tile0:tile0 + SLOT_TILES * E].rearrange("p (i e) -> p i e", e=E)
            neg_half = sb("neg_half4", [P, NT])
            var_eps = sb("var_eps4", [P, NT])
            lg = sb("lg", [P, NT, E])
            shifted = sb("shifted", [P, NT, E])
            expd = sb("expd", [P, NT, E])
            total = sb("total", [P, NT])
            best = sb("best", [P, NT])
            mark = sb("mark", [P, NT, E])
            first = sb("first", [P, NT])
            choice = sb("choice", [P, NT, E])
            rank = sb("rank", [P, NT, E])
            tot = sb("tot", [P, NT, E])
            cum = sb("cum", [P, 2, NT, E])
            over = sb("over", [P, E, MAXN])
            tiles_e = sb("tiles_e", [P, E])
            ends = sb("ends", [P, 2, E])
            base = sb("base", [P, E])
            spot = sb("spot", [P, NT, E])
            place = sb("place", [P, NT])
            place_u = sb("place_u", [P, NT], mybir.dt.uint32)
            past = sb("past", [P, SLOT_TILES, E])
            owner = sb("owner", [P, SLOT_TILES])
            p_r = ctx.enter_context(nc.psum_tensor("p_r", [P, 512], F32))
            p_n = ctx.enter_context(nc.psum_tensor("p_n", [P, 512], F32))
            cs_in, steps, halves, deviation, choice_ready, exp_ready, counted, placed, scattered = (
                sem(x) for x in ("cs_in", "d_steps", "d_halves", "deviation", "choice_ready", "exp_ready", "counted",
                                 "placed", "scattered"))

            with nc.Block() as block:
                @block.sync
                def _(sp):
                    sp.dma_start(cs[:], counts).then_inc(cs_in, 16)
                    for e in range(E):
                        sp.dma_start(w2s[:, e], w2[:, e]).then_inc(w2_in, 16)
                    sp.dma_start(b2s[:], b2).then_inc(w2_in, 16)

                @block.gpsimd
                def _(pool):
                    g = nc.gpsimd
                    g.memset(neg_half[:], -0.5).then_inc(halves, 1)
                    g.tensor_scalar(var_eps[:], moments[:, :, 1], 1e-5, None, ALU.add).then_inc(halves, 1)
                    pool.wait_ge(halves, 2)
                    g.tensor_tensor(rows[:, :, RSTD_AT], var_eps[:], neg_half[:], ALU.pow).then_inc(deviation, 1)
                    g.tensor_copy(rows[:, :, MEAN_AT], moments[:, :, 0]).then_inc(deviation, 1)
                    pool.wait_ge(cs_in, 16)
                    g.tensor_copy(rows[:, :, ID_AT], token).then_inc(deviation, 1)
                    pool.wait_ge(deviation, 3)
                    pool.wait_ge(slots_clear, 16)
                    pool.wait_ge(placed, 1)
                    for t in range(NT):
                        g.indirect_dma_start(out=sorted_rows, out_offset=bass.IndirectOffsetOnAxis(ap=place_u[:, t:t + 1], axis=0),
                                             in_=rows[:, t, :], in_offset=None, bounds_check=SLOT_TILES * P - 1,
                                             oob_is_err=False).then_inc(scattered, 16)
                    pool.wait_ge(scattered, 16 * NT)

                @block.scalar
                def _(act):
                    act.wait_ge(steps, 3)
                    nc.scalar.activation(expd[:], shifted[:], ACT.Exp).then_inc(exp_ready, 1)

                @block.tensor
                def _(pe):
                    pe.wait_ge(choice_ready, 1)
                    flat = choice[:].rearrange("p t e -> p (t e)")
                    nc.tensor.matmul(p_r[:, 0:NT * E], u_before, flat, start=True, stop=True).then_inc(counted, 1)
                    nc.tensor.matmul(p_n[:, 0:NT * E], u_ones, flat, start=True, stop=True).then_inc(counted, 1)

                @block.vector
                def _(dve):
                    v = nc.vector
                    made = [0]

                    def step(ins):
                        made[0] += 1
                        ins.then_inc(steps, 1)
                        dve.wait_ge(steps, made[0])

                    def each(ap):
                        return ap.unsqueeze(2).broadcast_to([P, NT, E])

                    dve.wait_ge(deviation, 1)
                    step(v.tensor_tensor(lg[:], logits[:], each(rows[:, :, RSTD_AT]), ALU.mult))
                    step(v.tensor_reduce(best[:], lg[:], AX.X, ALU.max))
                    step(v.tensor_tensor(shifted[:], lg[:], each(best[:]), ALU.subtract))
                    step(v.tensor_scalar(mark[:], shifted[:], 0.0, None, ALU.is_equal))
                    dve.wait_ge(cs_in, 16)
                    down_all = down.unsqueeze(1).broadcast_to([P, NT, E])
                    step(v.tensor_tensor(mark[:], mark[:], down_all, ALU.mult))
                    step(v.tensor_reduce(first[:], mark[:], AX.X, ALU.max))
                    step(v.tensor_tensor(choice[:], each(first[:]), down_all, ALU.is_equal))
                    v.tensor_tensor(choice[:], choice[:], each(valid), ALU.mult).then_inc(choice_ready, 1)
                    dve.wait_ge(exp_ready, 1)
                    step(v.tensor_reduce(total[:], expd[:], AX.X, ALU.add))
                    step(v.reciprocal(rows[:, :, GATE_AT], total[:]))
                    dve.wait_ge(counted, 2)
                    step(v.tensor_copy(rank[:], p_r[:, 0:NT * E].rearrange("p (t e) -> p t e", e=E)))
                    step(v.tensor_copy(tot[:], p_n[:, 0:NT * E].rearrange("p (t e) -> p t e", e=E)))
                    src, shift = tot[:], 1
                    while shift < NT:
                        dst = cum[:, (shift.bit_length() - 1) % 2]
                        step(v.tensor_tensor(dst[:, shift:], src[:, shift:], src[:, :NT - shift], ALU.add))
                        step(v.tensor_copy(dst[:, :shift], src[:, :shift]))
                        src, shift = dst, 2 * shift
                    n_e = src[:, NT - 1].unsqueeze(2).broadcast_to([P, E, MAXN])
                    step(v.tensor_tensor(over[:], n_e, tile_steps, ALU.is_gt))
                    step(v.tensor_reduce(tiles_e[:], over[:], AX.X, ALU.add))
                    end, shift = tiles_e[:], 1
                    while shift < E:
                        dst = ends[:, (shift.bit_length() - 1) % 2]
                        step(v.tensor_tensor(dst[:, shift:], end[:, shift:], end[:, :E - shift], ALU.add))
                        step(v.tensor_copy(dst[:, :shift], end[:, :shift]))
                        end, shift = dst, 2 * shift
                    step(v.tensor_tensor(past[:], tile_no, end.unsqueeze(1).broadcast_to([P, SLOT_TILES, E]), ALU.is_ge))
                    step(v.tensor_reduce(owner[:], past[:], AX.X, ALU.add))
                    step(v.tensor_scalar(expert_of[:], owner[:], float(E - 1), None, ALU.min))
                    step(v.tensor_tensor(base[:], end, tiles_e[:], ALU.subtract))
                    step(v.tensor_scalar(base[:], base[:], float(P), None, ALU.mult))
                    step(v.tensor_tensor(spot[:], src, tot[:], ALU.subtract))
                    step(v.tensor_tensor(spot[:], spot[:], rank[:], ALU.add))
                    step(v.tensor_tensor(spot[:], spot[:], base[:].unsqueeze(1).broadcast_to([P, NT, E]), ALU.add))
                    step(v.tensor_tensor(spot[:], spot[:], choice[:], ALU.mult))
                    step(v.tensor_reduce(place[:], spot[:], AX.X, ALU.add))
                    step(v.tensor_tensor(place[:], place[:], nowhere, ALU.add))
                    v.tensor_copy(place_u[:], place[:]).then_inc(placed, 1)
        if dbg:
            dump(nc, dbg, dict(rows=rows, sorted=sorted_rows, experts=expert_of))

        with ExitStack() as ctx:
            def sb(name, shape, dt=F32):
                return ctx.enter_context(nc.sbuf_tensor(name, shape, dt))

            def ps(name, shape):
                return ctx.enter_context(nc.psum_tensor(name, shape, F32))

            def sem(name):
                return ctx.enter_context(nc.semaphore(name))

            RING = 4
            xs = sb("xs", [P, RING, ROW])
            ids = sb("ids", [P, RING], mybir.dt.uint32)
            xn = sb("xn", [P, D])
            xt = sb("xt", [C + 1, 2, 2, P])
            hidden = sb("hidden", [P, 2, FF])
            hidden_t = sb("hidden_t", [P, 2, KC, P])
            yb = sb("yb", [P, D])
            ys = sb("ys", [P, RING, D])
            p_x = ps("p_x", [P, 512])
            p_h = ps("p_h2", [P, 2, 1024])
            p_ht = ps("p_ht", [P, 1024])
            p_y = ps("p_y", [P, 512])
            xs_in = [sem(f"xs_in{r}") for r in range(RING)]
            stored = [sem(f"stored{r}") for r in range(RING)]
            (ones_set, ids_ready, xn_ready, x_tr, xt_ready, up_ready, hidden_ready, hid_tr, hidt_a, hidt_v, down_ready,
             y_read, y_ready) = (sem(x) for x in (
                 "ones_set", "ids_ready", "xn_ready", "x_tr", "xt_ready", "up_ready", "hidden_ready", "e_hid_tr",
                 "hidt_a", "hidt_v", "down_ready", "y_read", "y_ready"))

            assert SLOT_TILES % RING == 0

            def tiles(eng, body):
                last = SLOT_TILES // RING - 1
                for r in range(RING):
                    body(0, r, 2)
                with eng.Fori(1, last) as turn:
                    for r in range(RING):
                        body(turn, r, 2)
                for r in range(RING):
                    body(last, r, RING - 1 - r)

            with nc.Block() as block:
                @block.sync
                def _(sp):
                    by_tile = sorted_rows.rearrange("(i p) c -> i p c", p=P)
                    for r in range(RING):
                        sp.dma_start(xs[:, r], by_tile[r]).then_inc(xs_in[r], 16)
                    with sp.Fori(1, SLOT_TILES // RING) as turn:
                        for r in range(RING):
                            sp.wait_ge(y_ready, RING * (turn - 1) + r + 1)
                            sp.dma_start(xs[:, r], by_tile[ds(RING * turn + r, 1)].rearrange("o p c -> (o p) c")).then_inc(xs_in[r], 16)

                @block.gpsimd
                def _(pool):
                    def body(turn, r, ahead):
                        i = RING * turn + r
                        done = i + 1 if isinstance(i, int) else pool.to_reg(i + 1)
                        wait_apart(pool, y_ready, done)
                        pool.wait_ge(ids_ready, done)
                        nc.gpsimd.indirect_dma_start(out=out.rearrange("b t d -> (b t) d"),
                                                     out_offset=bass.IndirectOffsetOnAxis(ap=ids[:, r:r + 1], axis=0),
                                                     in_=ys[:, r], in_offset=None, bounds_check=B * L - 1,
                                                     oob_is_err=False).then_inc(stored[r], 16)

                    tiles(pool, body)
                    for r in range(RING):
                        pool.wait_ge(stored[r], 16 * (SLOT_TILES // RING))

                @block.scalar
                def _(act):
                    def x_out(i, u):
                        act.wait_ge(x_tr, i + 1)
                        nc.scalar.copy(xt[0:C, u], p_x[0:C, 0:2 * P].rearrange("p (c t) -> p c t", c=2)).then_inc(xt_ready, 1)

                    def silu(i, u):
                        act.wait_ge(up_ready, i + 1)
                        nc.scalar.activation(hidden[:, u], p_h[:, u, 0:FF], ACT.Silu).then_inc(hidden_ready, 1)

                    def body(turn, r, ahead):
                        i = RING * turn + r
                        u = r % 2
                        if ahead >= 1:
                            silu(i + 1, 1 - u)
                        act.wait_ge(hid_tr, 2 * i + 1)
                        nc.scalar.copy(hidden_t[:, u, 0:4], p_ht[:, 0:512].rearrange("p (k t) -> p k t", k=4)).then_inc(hidt_a, 1)
                        if ahead >= 2:
                            x_out(i + 2, u)

                    act.wait_ge(ones_set, 1)
                    x_out(0, 0)
                    x_out(1, 1)
                    silu(0, 0)
                    tiles(act, body)

                @block.tensor
                def _(pe):
                    mm = nc.tensor.matmul

                    def x_in(i, u):
                        pe.wait_ge(xn_ready, i + 1)
                        for c in range(2):
                            last = nc.tensor.transpose(p_x[0:C, c * P:(c + 1) * P], xn[:, c * C:(c + 1) * C], ident)
                        last.then_inc(x_tr, 1)

                    def up(i, u):
                        e = pe.value_load(expert_of[0:1, ds(i, 1)], min_val=0, max_val=E - 1)
                        pe.wait_ge(xt_ready, i + 1)
                        for a, b in ((0, 512), (512, FF)):
                            for c in range(2):
                                n = C + c
                                last = mm(p_h[:, u, a:b], xt[0:n, u, c], w1s[0:n, ds(e, 1), c, a:b].rearrange("p o f -> p (o f)"),
                                          start=(c == 0), stop=(c == 1))
                        last.then_inc(up_ready, 1)

                    def down(i, u):
                        e = pe.value_load(expert_of[0:1, ds(i, 1)], min_val=0, max_val=E - 1)
                        wait_apart(pe, hidt_a, i + 1)
                        wait_apart(pe, hidt_v, i + 1)
                        for k in range(KC):
                            last = mm(p_y[:, 0:D], hidden_t[:, u, k], w2s[:, ds(e, 1), k].rearrange("p o d -> p (o d)"),
                                      start=(k == 0), stop=(k == KC - 1))
                        last.then_inc(down_ready, 1)

                    def body(turn, r, ahead):
                        i = RING * turn + r
                        u = r % 2
                        if ahead >= 1:
                            up(i + 1, 1 - u)
                        wait_apart(pe, hidden_ready, i + 1)
                        for k in range(KC):
                            last = nc.tensor.transpose(p_ht[:, k * P:(k + 1) * P], hidden[:, u, k * P:(k + 1) * P], ident)
                            if k == 3:
                                last.then_inc(hid_tr, 1)
                        last.then_inc(hid_tr, 1)
                        if ahead >= 2:
                            x_in(i + 2, u)
                        wait_apart(pe, y_read, i + 1)
                        down(i, u)

                    pe.wait_ge(w1_in, 16 * E)
                    x_in(0, 0)
                    pe.wait_ge(xt_ready, 1)
                    x_in(1, 1)
                    up(0, 0)
                    pe.wait_ge(w2_in, 16 * (E + 1))
                    tiles(pe, body)

                @block.vector
                def _(dve):
                    v = nc.vector

                    def norm(i, r, turn):
                        dve.wait_ge(xs_in[r], 16 * turn + 16)
                        v.tensor_scalar(xn[:], xs[:, r, 0:D], xs[:, r, MEAN_AT:MEAN_AT + 1], xs[:, r, RSTD_AT:RSTD_AT + 1],
                                        ALU.subtract, ALU.mult).then_inc(xn_ready, 1)

                    def body(turn, r, ahead):
                        i = RING * turn + r
                        u = r % 2
                        e = dve.value_load(expert_of[0:1, ds(i, 1)], min_val=0, max_val=E - 1)
                        if ahead >= 2:
                            wait_apart(dve, x_tr, i + 2)
                            norm(i + 2, (r + 2) % RING, turn + (r + 2) // RING)
                        dve.wait_ge(hid_tr, 2 * i + 2)
                        v.tensor_copy(hidden_t[:, u, 4:6], p_ht[:, 512:768].rearrange("p (k t) -> p k t", k=2)).then_inc(hidt_v, 1)
                        if not isinstance(turn, int) or turn:
                            wait_apart(dve, stored[r], 16 * turn)
                        v.tensor_copy(ids[:, r:r + 1], xs[:, r, ID_AT:ID_AT + 1]).then_inc(ids_ready, 1)
                        dve.wait_ge(down_ready, i + 1)
                        v.tensor_tensor(yb[:], p_y[:, 0:D], b2s[:, ds(e, 1)].rearrange("p o d -> p (o d)"), ALU.add).then_inc(y_read, 1)
                        wait_apart(dve, y_read, i + 2)
                        v.scalar_tensor_tensor(ys[:, r], yb[:], xs[:, r, GATE_AT:GATE_AT + 1], xs[:, r, 0:D], ALU.mult, ALU.add).then_inc(y_ready, 1)

                    v.sem_inc(y_read, 1)
                    v.memset(xt[C:C + 1, :], 1.0).then_inc(ones_set, 1)
                    norm(0, 0, 0)
                    dve.wait_ge(x_tr, 1)
                    norm(1, 1, 0)
                    tiles(dve, body)


def dump(nc, dbg, what):
    with nc.semaphore("dumped") as s:
        with nc.Block() as block:
            @block.sync
            def _(sp):
                n = 0
                for k, t in what.items():
                    if k in dbg:
                        sp.dma_start(dbg[k], t[:]).then_inc(s, 16)
                        n += 16
                if n:
                    sp.wait_ge(s, n)


def layouts(x, txt, L0_tok_proj_w, L0_tok_proj_b, L0_tok_cls_token, L0_tok_pos_embedding, L0_attn_conv_w,
            L0_attn_conv_b, L0_attn_ln_g, L0_attn_ln_b, L0_attn_qkv_w, L0_attn_qkv_b, L0_attn_bn_w1, L0_attn_bn_w2,
            L0_attn_temperature, L0_attn_proj_w, L0_attn_proj_b, L0_attn_mn_g, L0_attn_mn_b, L0_ffn_Wg, L0_ffn_W1,
            L0_ffn_b1, L0_ffn_W2, L0_ffn_b2):
    import numpy as np

    f = np.float32

    def chunks(a, n, rows):
        return np.ascontiguousarray(np.moveaxis(a.reshape(n, rows, *a.shape[1:]), 0, 1))

    G = 96 // 16
    pt = x.reshape(B, 3, G, 16, G, 16).transpose(1, 3, 5, 0, 2, 4).reshape(KC, P, PAIRS, 2, NPATCH)
    patches = np.zeros((PAIRS, P, KC, 2, HALF), f)
    patches[..., 1:LP] = pt.transpose(2, 1, 0, 3, 4)
    pos_rows = np.zeros((2, HALF, D), f)
    pos_rows[:, :LP] = L0_tok_pos_embedding
    first_rows = np.zeros((2, HALF, D), f)
    first_rows[:, 0] = L0_tok_cls_token[0, 0]
    first_rows[:, 1:LP] = L0_tok_proj_b
    conv_w = np.concatenate([L0_attn_conv_w, L0_attn_conv_b[:, None]], 1)
    w_in = np.concatenate([L0_attn_qkv_w, L0_attn_bn_w1], 0).T
    b_in = np.concatenate([L0_attn_qkv_b, np.zeros(R, f)])
    w1 = np.zeros((C + 1, E, 2, FF), f)
    w1[:C] = L0_ffn_W1.reshape(E, 2, C, FF).transpose(2, 0, 1, 3)
    w1[C, :, 1] = L0_ffn_b1
    s, t = np.arange(P)[:, None], np.arange(P)[None, :]
    u_pre = (s // HALF == t // HALF) & (s <= t) & (s % HALF < LP)
    consts = [s == t, s <= t, u_pre] + [(s // HALF == b) & (s % HALF < LP) & (t >= 0) for b in range(2)] + [s < t, t >= 0]
    counts = np.zeros((P, CSMALL), f)
    r = np.arange(P)
    for g in range(NT):
        b, j = 2 * (g // 3), g % 3
        real = (r % HALF < LP) if j == 0 else r >= 0
        number = (b + r // HALF) * L + r % HALF if j == 0 else (b + j - 1) * L + LP + r
        counts[:, valid0 + g] = real
        counts[:, token0 + g] = number
        counts[:, nowhere0 + g] = np.where(real, 0, NOWHERE)
    counts[:, down0:steps0] = E - np.arange(E)
    counts[:, steps0:tile0] = np.tile(P * np.arange(MAXN), E)
    counts[:, tile0:] = np.repeat(np.arange(SLOT_TILES), E)
    return {
        "patches": patches.reshape(PAIRS, P, KC, P),
        "txt": np.ascontiguousarray(txt),
        "tok_w": chunks(L0_tok_proj_w.T, KC, P),
        "pos_rows": pos_rows.reshape(P, D),
        "first_rows": first_rows.reshape(P, D),
        "conv_w": chunks(conv_w, 2, C),
        "ln_gb": chunks(np.stack([L0_attn_ln_g, L0_attn_ln_b], 1), 2, C),
        "w_in": chunks(w_in, 2, C),
        "b_in": np.tile(b_in, (P, 1)),
        "bn2": np.ascontiguousarray(L0_attn_bn_w2.T),
        "temp": np.tile(L0_attn_temperature, (P, 1)),
        "w_out": chunks(L0_attn_proj_w.T, 2, C),
        "b_out": np.tile(L0_attn_proj_b, (P, 1)),
        "mn_gb": np.tile(np.stack([L0_attn_mn_g, L0_attn_mn_b], 1), (C // DH, 1)),
        "wg": chunks(L0_ffn_Wg, 2, C),
        "w1": w1,
        "w2": np.ascontiguousarray(L0_ffn_W2.reshape(E, KC, P, D).transpose(2, 0, 1, 3)),
        "b2": np.tile(L0_ffn_b2[None], (P, 1, 1)),
        "consts": np.concatenate([np.broadcast_to(c, (P, P)) for c in consts] + [r[:, None] // DH == np.arange(C // DH),
                                 r[:, None] // DH == np.arange(C) // DH], 1).astype(f),
        "counts": counts,
    }


def kernel(**inputs):
    import numpy as np
    import concourse.bacc as bacc
    from concourse.bass_utils import run_bass_kernel_spmd

    nc = bacc.Bacc("TRN2", target_bir_lowering=False, num_devices=1)
    arrays = layouts(**{k: np.asarray(v) for k, v in inputs.items()})
    args = {k: nc.dram_tensor(k, a.shape, mybir.dt.from_np(a.dtype), kind="ExternalInput").ap() for k, a in arrays.items()}
    out = nc.dram_tensor("out", (B, L, D), F32, kind="ExternalOutput").ap()
    early_fusion_layer(nc, out=out, **args)
    r = run_bass_kernel_spmd(nc, [arrays], core_ids=[0])
    return r.results[0]["out"]
```

```python
from contextlib import ExitStack, nullcontext

import concourse.bass as bass
from concourse import mybir

F32 = mybir.dt.float32
ALU = mybir.AluOpType
ACT = mybir.ActivationFunctionType
AX = mybir.AxisListType

B = 16
NPATCH = 36
LP = NPATCH + 1
LT = 128
L = LP + LT
D = 192
KP = 768
H = 12
DH = D // H
R = 64
NG = 5
E = 8
FF = 768

P = 128
C = D // 2
KC = KP // P
PAIRS = B // 2
NT = 3 * PAIRS
HALF = 64
V0, HID0, MEAN = 2 * D, 3 * D, 3 * D + R
WCOLS = 3 * D + R
ident0, before0, ones0, utt0, upp0, sel0 = 0, P, 2 * P, 3 * P, 4 * P, 5 * P
head0 = 7 * P
same0 = head0 + C // DH
pre_mask0 = same0 + C
CMAT = pre_mask0 + 2 * LP
HG = 4
NHG = H // HG
UNITS = PAIRS * NHG
DIGIT = 32
SLOT_TILES = (B * L + E * (P - 1)) // P
MAXN = -(-B * L // P)
ROW = D + 4
MEAN_AT, RSTD_AT, GATE_AT, ID_AT = D, D + 1, D + 2, D + 3
NOWHERE = 1 << 20
token0 = 0
nowhere0 = token0 + NT
down0 = nowhere0 + NT
real0 = down0 + E
steps0 = real0 + NT * E
tile0 = steps0 + E * MAXN
CSMALL = tile0 + SLOT_TILES * E


def wait_apart(eng, sem, value):
    if isinstance(value, int):
        eng.wait_ge(sem, value)
        return
    value = eng.to_reg(value)
    eng.wait_ge(sem, 1)
    eng.wait_ge(sem, value)


def after(eng, sem, value):
    if not isinstance(value, int):
        wait_apart(eng, sem, value)
    elif value > 0:
        eng.wait_ge(sem, value)


def early_fusion_layer(nc, patches, txt, tok_w, pos_rows, first_rows, conv_w, ln_gb, w_in, b_in, bn2, temp,
                       w_out, b_out, mn_gb, wg, w1, w2, b2, consts, counts, out):
    ds = bass.ds
    with ExitStack() as top:
        def sbuf(name, shape, dt=F32):
            return top.enter_context(nc.sbuf_tensor(name, shape, dt))

        cst = sbuf("cst", [P, CMAT])
        ident = cst[:, ident0:ident0 + P]
        u_txt = cst[:, utt0:utt0 + P]
        u_pre = cst[:, upp0:upp0 + P]
        prefix_of = [cst[:, sel0 + b * P:sel0 + (b + 1) * P] for b in range(2)]
        u_before = cst[:, before0:before0 + P]
        u_ones = cst[:, ones0:ones0 + P]
        head_of = cst[0:C, head0:same0]
        pre_mask = cst[:, pre_mask0:CMAT]
        same_head = cst[0:C, same0:pre_mask0]
        rows = sbuf("rows", [P, NT, ROW])
        hid = rows[:, :, 0:D]
        logits = sbuf("logits", [P, NT, E])
        w1s = sbuf("w1s", [C + 1, E, 2, FF])
        empty = sbuf("empty", [P, ROW])
        sorted_rows = nc.dram_tensor("sorted_rows", (SLOT_TILES * P, ROW), F32, kind="Internal").ap()
        w1_in = top.enter_context(nc.semaphore("w1_in"))
        cs_in = top.enter_context(nc.semaphore("cs_in"))
        slots_clear = top.enter_context(nc.semaphore("slots_clear"))

        def heads(ap, n=DH):
            return ap.rearrange("p j (h d) -> p (j h) d", d=n)

        mid = top.enter_context(ExitStack())

        def sbuf(name, shape, dt=F32):
            return mid.enter_context(nc.sbuf_tensor(name, shape, dt))

        qk = sbuf("qk", [P, NT, 2 * D])
        val = sbuf("val", [P, NT, D])
        gates = sbuf("gates", [P, NT, H * NG])
        decay = sbuf("decay", [P, NT, H])
        gain_kv = sbuf("gain_kv", [P, NT, H])
        gain_z = sbuf("gain_z", [P, NT, H])
        clip_hi = sbuf("clip_hi", [P, NT, H])
        clip_lo = sbuf("clip_lo", [P, NT, H])

        kmax = sbuf("kmax", [P, NT, H])
        vmax = sbuf("vmax", [P, NT, H])

        cs = cst[:, utt0:utt0 + CSMALL]
        assert utt0 + CSMALL <= CMAT

        with ExitStack() as ctx:
            def sb(name, shape):
                return ctx.enter_context(nc.sbuf_tensor(name, shape, F32))

            def ps(name, shape):
                return ctx.enter_context(nc.psum_tensor(name, shape, F32))

            def sem(name):
                return ctx.enter_context(nc.semaphore(name))

            tokw = sb("tokw", [P, KC, D])
            posb = sb("posb", [P, D])
            firstb = sb("firstb", [P, D])
            convs = sb("convs", [C, 2, 4])
            lng = sb("lng", [C, 2, 2])
            win = sb("win", [C, 2, WCOLS + 1])
            wgain = sb("wgain", [C, 2, WCOLS])
            bin_ = sb("bin_", [P, WCOLS])
            bin_raw = sb("bin_raw", [P, WCOLS])
            win_raw = sb("win_raw", [C, 2, WCOLS])
            ones_d = sb("ones_d", [C, P])
            lnb_wide = sb("lnb_wide", [C, 2, P])
            bn2s = sb("bn2s", [R, H * NG])
            pat = sb("pat", [P, 2, KC, P])
            neg_half = sb("neg_half", [P, 3])
            mv = sb("mv", [P, 3, 2])
            bst = sb("bst", [P, 3, 6])
            vare = sb("vare", [P, 3])
            rstd = sb("rstd", [P, 3])
            xa = sb("xa", [P, 3, D])
            xat = sb("xat", [C, 2, 2, L + 2])
            xct = sb("xct", [C, 2, 2, 2, L])
            xpre = sb("xpre", [C, 2, 2, P])
            xsq = sb("xsq", [C, 2, 2, 3 * P])
            stat = sb("stat", [P, 2, 2])
            nvar = sb("nvar", [P, 2])
            vare2 = sb("vare2", [P, 2])
            rstd2 = sb("rstd2", [P, 2])
            qkr = sb("qkr", [P, 2, 2 * D])
            qkm = sb("qkm", [P, 2, 2 * D])
            qke = sb("qke", [P, 2, 2 * D])
            hr = sb("hr", [P, 2, R])
            ht = sb("ht", [P, 2, R])
            hs = sb("hs", [P, 3, R])
            hst = sb("hst", [R, 3 * P])

            p_tok = ps("p_tok", [P, 512])
            p_tr = ps("p_tr", [P, 2, 512])
            p_qk = ps("p_qk", [P, 2, 512])
            p_v = ps("p_v", [P, 2, 512])
            p_h = ps("p_h", [P, 512])

            tokw_in = sem("tokw_in")
            later_text_in = sem("later_text_in")
            weights_in = sem("weights_in")
            small_in = sem("small_in")
            text_in = sem("text_in")
            patches_in = [sem(f"patches_in{u}") for u in range(2)]
            prep_v = sem("prep_v")
            prep_pe = sem("prep_pe")
            halves_set = sem("halves_set")
            w_ready = sem("w_ready")
            pads_zero = sem("pads_zero")
            tok_ready = sem("tok_ready")
            h_ready = sem("h_ready")
            st_done = sem("st_done")
            mv_ready = sem("mv_ready")
            vare_done = sem("vare_done")
            rstd_ready = sem("rstd_ready")
            xa_ready = sem("xa_ready")
            tr_ready = sem("tr_ready")
            xat_ready = sem("xat_ready")
            conv_first = sem("conv_first")
            conv_step = sem("conv_step")
            conv_ready = sem("conv_ready")
            xsq_ready = sem("xsq_ready")
            xpre_ready = sem("xpre_ready")
            proj_ready = sem("proj_ready")
            stat_copied = sem("stat_copied")
            nvar_ready = sem("nvar_ready")
            vare2_done = sem("vare2_done")
            rstd2_ready = sem("rstd2_ready")
            qk_raw = sem("qk_raw")
            banks_read = sem("banks_read")
            hid_raw = sem("hid_raw")
            qk_min = sem("qk_min")
            qk_exp = sem("qk_exp")
            hid_tanh = sem("hid_tanh")
            qk_done = sem("qk_done")
            hid_silu = sem("hid_silu")
            hid_tr = sem("hid_tr")
            hidt_ready = sem("hidt_ready")
            par_ready = sem("par_ready")
            par_read = sem("par_read")

            def bodies(eng, body):
                body(0, 0, 2)
                body(1, 1, 2)
                with eng.Fori(1, PAIRS // 2 - 1) as i:
                    body(2 * i, 0, 2)
                    body(2 * i + 1, 1, 2)
                body(PAIRS - 2, 0, 1)
                body(PAIRS - 1, 1, 0)

            with nc.Block() as block:
                @block.sync
                def _(sp):
                    for u in range(2):
                        sp.dma_start(pat[:, u], patches[u]).then_inc(patches_in[u], 16)
                        if u == 0:
                            sp.dma_start(tokw[:], tok_w).then_inc(tokw_in, 16)
                    sp.dma_start(win_raw[:], w_in).then_inc(weights_in, 16)
                    sp.wait_ge(later_text_in, 32)
                    for e in range(E):
                        sp.dma_start(w1s[:, e], w1[:, e]).then_inc(w1_in, 16)
                    with sp.Fori(1, PAIRS // 2) as i:
                        for u in range(2):
                            sp.wait_ge(tok_ready, 2 * i + u - 1)
                            sp.dma_start(pat[:, u], patches[ds(2 * i + u, 1)].rearrange("o p c n -> p (o c) n")).then_inc(patches_in[u], 16)

                @block.scalar
                def _(act):
                    act.dma_start(cst[:], consts).then_inc(small_in, 16)
                    act.dma_start(posb[:], pos_rows).then_inc(small_in, 16)
                    act.dma_start(firstb[:], first_rows).then_inc(small_in, 16)
                    act.dma_start(convs[:], conv_w).then_inc(small_in, 16)
                    act.dma_start(lng[:], ln_gb).then_inc(small_in, 16)
                    act.dma_start(bin_raw[:], b_in).then_inc(small_in, 16)
                    act.dma_start(bn2s[:], bn2).then_inc(small_in, 16)
                    hv = hid.rearrange("p (g j) d -> p g j d", j=3)
                    tv = txt.rearrange("(g b) t d -> t g b d", b=2)
                    for some, arrived in ((slice(0, 2), text_in), (slice(2, PAIRS), later_text_in)):
                        for b in range(2):
                            act.dma_start(hv[:, some, 1 + b, :], tv[:, some, b, :]).then_inc(arrived, 16)

                    def transposed(p, u):
                        act.wait_ge(tr_ready, p + 1)
                        if not isinstance(p, int) or p:
                            act.wait_ge(conv_ready, 2 * p)
                        for c in range(2):
                            nc.scalar.copy(xat[:, c, :, 2:2 + LP],
                                           p_tr[0:C, c, 0:P].rearrange("p (b t) -> p b t", b=2)[:, :, 0:LP]).then_inc(xat_ready, 1)
                            nc.scalar.copy(xat[:, c, :, 2 + LP:],
                                           p_tr[0:C, c, P:3 * P].rearrange("p (b t) -> p b t", b=2)).then_inc(xat_ready, 1)

                    def conv_last_tap(p, u):
                        after(act, proj_ready, 3 * p - 3)
                        act.wait_ge(xat_ready, 4 * p + 4)
                        for c in range(2):
                            nc.scalar.activation(xct[:, u, c], xat[:, c, :, 2:], ACT.Identity,
                                                 scale=convs[:, c, 2:3], bias=convs[:, c, 3:4]).then_inc(conv_first, 1)

                    def squares(p, u):
                        act.wait_ge(conv_ready, 2 * p + 2)
                        for c in range(2):
                            nc.scalar.activation(xsq[:, u, c, 0:P].rearrange("p (b t) -> p b t", b=2),
                                                 xct[:, u, c, :, 0:HALF], ACT.Square).then_inc(xsq_ready, 1)
                            nc.scalar.activation(xsq[:, u, c, P:].rearrange("p (b t) -> p b t", b=2),
                                                 xct[:, u, c, :, LP:], ACT.Square).then_inc(xsq_ready, 1)

                    def nonlinear(p, u, j):
                        s = (u + j) % 2
                        t = 3 * p + j
                        act.wait_ge(hid_raw, t + 1)
                        nc.scalar.activation(ht[:, s], hr[:, s], ACT.Tanh, scale=0.5).then_inc(hid_tanh, 1)
                        act.wait_ge(qk_raw, t + 1)
                        nc.scalar.activation(qkm[:, s], qkr[:, s], ACT.Relu, scale=-1.0).then_inc(qk_min, 1)
                        act.wait_ge(qk_min, t + 1)
                        nc.scalar.activation(qke[:, s], qkm[:, s], ACT.Exp, scale=-1.0).then_inc(qk_exp, 1)

                    def hidden_out(p):
                        wait_apart(act, hid_tr, p + 1)
                        nc.scalar.copy(hst[:], p_h[0:R, 0:3 * P]).then_inc(hidt_ready, 1)

                    def params_out(p):
                        wait_apart(act, par_ready, p + 1)
                        nc.scalar.activation(gates[:, ds(3 * p, 3), :], p_h[:, 0:3 * H * NG].rearrange("p (j n) -> p j n", j=3),
                                             ACT.Identity, scale=0.5).then_inc(par_read, 1)

                    def body(p, u, ahead):
                        first = isinstance(p, int) and p == 0
                        if not first:
                            hidden_out(p - 1)
                        nonlinear(p, u, 0)
                        if ahead >= 1:
                            squares(p + 1, 1 - u)
                        nonlinear(p, u, 1)
                        if not first:
                            params_out(p - 1)
                        if ahead >= 2:
                            transposed(p + 2, u)
                        nonlinear(p, u, 2)
                        if ahead >= 2:
                            conv_last_tap(p + 2, u)

                    act.wait_ge(pads_zero, 4)
                    transposed(0, 0)
                    conv_last_tap(0, 0)
                    squares(0, 0)
                    transposed(1, 1)
                    conv_last_tap(1, 1)
                    bodies(act, body)
                    hidden_out(PAIRS - 1)
                    params_out(PAIRS - 1)

                @block.gpsimd
                def _(pool):
                    def first_norm(p):
                        wait_apart(pool, mv_ready, 3 * p + 3)
                        nc.gpsimd.tensor_scalar(vare[:], mv[:, :, 1], 1e-5, None, ALU.add).then_inc(vare_done, 1)
                        wait_apart(pool, vare_done, p + 1)
                        nc.gpsimd.tensor_tensor(rstd[:], vare[:], neg_half[:], ALU.pow).then_inc(rstd_ready, 1)

                    def second_norm(p, u, j):
                        s = (u + j) % 2
                        t = 3 * p + j
                        wait_apart(pool, nvar_ready, t + 1)
                        nc.gpsimd.tensor_scalar(vare2[:, s:s + 1], nvar[:, s:s + 1], -1.0, 1e-5, ALU.mult, ALU.add).then_inc(vare2_done, 1)
                        wait_apart(pool, vare2_done, t + 1)
                        nc.gpsimd.tensor_tensor(rstd2[:, s:s + 1], vare2[:, s:s + 1], neg_half[:, 0:1], ALU.pow).then_inc(rstd2_ready, 1)

                    def prefixes(p, u):
                        wait_apart(pool, conv_ready, 2 * p + 2)
                        nc.gpsimd.tensor_copy(xpre[:, u].rearrange("p c (b t) -> p c b t", b=2),
                                              xct[:, u, :, :, 0:HALF]).then_inc(xpre_ready, 1)

                    def body(p, u, ahead):
                        second_norm(p, u, 0)
                        if ahead >= 1:
                            prefixes(p + 1, 1 - u)
                        second_norm(p, u, 1)
                        if ahead >= 2:
                            first_norm(p + 2)
                        second_norm(p, u, 2)

                    pool.wait_ge(pads_zero, 2)
                    nc.gpsimd.memset(neg_half[:], -0.5).then_inc(halves_set, 1)
                    pool.wait_ge(halves_set, 1)
                    first_norm(0)
                    first_norm(1)
                    prefixes(0, 0)
                    pool.dma_start(sorted_rows.rearrange("(i p) c -> p i c", p=P),
                                   empty[:].unsqueeze(1).broadcast_to([P, SLOT_TILES, ROW])).then_inc(slots_clear, 16)

                    bodies(pool, body)

                @block.vector
                def _(dve):
                    v = nc.vector
                    v.memset(empty[:, 0:ID_AT], 0.0).then_inc(pads_zero, 1)
                    v.memset(empty[:, ID_AT:], float(NOWHERE)).then_inc(pads_zero, 1)
                    v.memset(xat[:, :, :, 0:2], 0.0).then_inc(pads_zero, 1)
                    v.memset(ones_d[:], 1.0 / D).then_inc(prep_v, 1)
                    dve.wait_ge(small_in, 16 * 7)
                    v.tensor_tensor(posb[:], posb[:], firstb[:], ALU.add).then_inc(prep_v, 1)
                    v.tensor_scalar(convs[:, :, 2], convs[:, :, 2], 1.0, None, ALU.add).then_inc(pads_zero, 1)
                    dve.wait_ge(prep_v, 2)
                    for c in range(2):
                        v.tensor_scalar(lnb_wide[:, c], ones_d[:], float(D), lng[:, c, 1:2], ALU.mult, ALU.mult).then_inc(prep_v, 1)

                    def stats(p):
                        if isinstance(p, int) and p == 2:
                            dve.wait_ge(later_text_in, 32)
                        dve.wait_ge(tok_ready, p + 1)
                        v.tensor_tensor(hid[:, ds(3 * p, 1), :], p_tok[:, 0:D].rearrange("p (o d) -> p o d", o=1),
                                        posb[:].rearrange("p (o d) -> p o d", o=1), ALU.add).then_inc(h_ready, 1)
                        for j in (1, 2, 0):
                            if j == 0:
                                wait_apart(dve, h_ready, p + 1)
                            v.bn_stats(bst[:, j], hid[:, ds(3 * p + j, 1), :].rearrange("p o d -> p (o d)")).then_inc(st_done, 1)
                        wait_apart(dve, st_done, 3 * p + 3)
                        for j in range(3):
                            v.bn_aggr(mv[:, j], bst[:, j]).then_inc(mv_ready, 1)

                    def norm(p):
                        after(dve, tr_ready, p)
                        dve.wait_ge(rstd_ready, p + 1)
                        for j in range(3):
                            v.tensor_scalar(xa[:, j:j + 1], hid[:, ds(3 * p + j, 1), :], mv[:, j, 0:1], rstd[:, j:j + 1],
                                            ALU.subtract, ALU.mult).then_inc(xa_ready, 1)

                    def conv(p, u):
                        dve.wait_ge(conv_first, 2 * p + 2)
                        for c in range(2):
                            v.scalar_tensor_tensor(xct[:, u, c], xat[:, c, :, 1:1 + L], convs[:, c, 1:2], xct[:, u, c],
                                                   ALU.mult, ALU.add).then_inc(conv_step, 1)
                        for c in range(2):
                            dve.wait_ge(conv_step, 2 * p + 1 + c)
                            v.scalar_tensor_tensor(xct[:, u, c], xat[:, c, :, 0:L], convs[:, c, 0:1], xct[:, u, c],
                                                   ALU.mult, ALU.add).then_inc(conv_ready, 1)

                    def second_stats(p, u, j):
                        s = (u + j) % 2
                        t = 3 * p + j
                        dve.wait_ge(proj_ready, t + 1)
                        v.tensor_copy(stat[:, s], p_v[:, s, D + R:D + R + 2]).then_inc(stat_copied, 1)
                        dve.wait_ge(stat_copied, t + 1)
                        v.scalar_tensor_tensor(nvar[:, s:s + 1], stat[:, s, 0:1], stat[:, s, 0:1], stat[:, s, 1:2],
                                               ALU.mult, ALU.subtract).then_inc(nvar_ready, 1)

                    def scaled(p, u, j):
                        s = (u + j) % 2
                        t = 3 * p + j
                        dve.wait_ge(rstd2_ready, t + 1)
                        dve.wait_ge(qk_done, t + 1)
                        r = rstd2[:, s:s + 1]
                        v.scalar_tensor_tensor(hr[:, s], p_v[:, s, D:D + R], r, bin_[:, HID0:HID0 + R], ALU.mult, ALU.add).then_inc(hid_raw, 1)
                        v.scalar_tensor_tensor(qkr[:, s], p_qk[:, s, 0:2 * D], r, bin_[:, 0:2 * D], ALU.mult, ALU.add).then_inc(qk_raw, 1)
                        v.scalar_tensor_tensor(val[:, ds(t, 1), :], p_v[:, s:s + 1, 0:D], r,
                                               bin_[:, V0:V0 + D].rearrange("p (o d) -> p o d", o=1), ALU.mult, ALU.add).then_inc(banks_read, 1)

                    def finished(p, u, j):
                        s = (u + j) % 2
                        t = 3 * p + j
                        after(dve, hid_tr, p)
                        dve.wait_ge(hid_tanh, t + 1)
                        v.scalar_tensor_tensor(hs[:, j], ht[:, s], 1.0, hr[:, s], ALU.add, ALU.mult).then_inc(hid_silu, 1)
                        dve.wait_ge(qk_exp, t + 1)
                        v.scalar_tensor_tensor(qk[:, ds(t, 1), :], qkr[:, s:s + 1], 0.0, qke[:, s:s + 1], ALU.max, ALU.add).then_inc(qk_done, 1)

                    def body(p, u, ahead):
                        second_stats(p, u, 0)
                        if ahead >= 1:
                            conv(p + 1, 1 - u)
                        scaled(p, u, 0)
                        second_stats(p, u, 1)
                        if ahead >= 2:
                            stats(p + 2)
                        finished(p, u, 0)
                        scaled(p, u, 1)
                        second_stats(p, u, 2)
                        if ahead >= 2:
                            norm(p + 2)
                        finished(p, u, 1)
                        scaled(p, u, 2)
                        finished(p, u, 2)

                    dve.wait_ge(text_in, 32)
                    dve.wait_ge(prep_v, 2)
                    v.sem_inc(banks_read, 2)
                    v.sem_inc(qk_done, 2)
                    stats(0)
                    norm(0)
                    stats(1)
                    dve.wait_ge(weights_in, 16)
                    for c in range(2):
                        v.tensor_scalar(wgain[:, c], win_raw[:, c], lng[:, c, 0:1], None, ALU.mult).then_inc(prep_v, 1)
                    v.memset(win[:, :, MEAN:MEAN + 1], 1.0 / D).then_inc(w_ready, 1)
                    norm(1)
                    conv(0, 0)
                    dve.wait_ge(prep_pe, 4)
                    for c in range(2):
                        v.tensor_tensor(win[:, c, 0:512], wgain[:, c, 0:512], p_qk[0:C, 0, 0:512], ALU.subtract).then_inc(w_ready, 1)
                        v.tensor_tensor(win[:, c, 512:WCOLS], wgain[:, c, 512:WCOLS], p_qk[0:C, 1, 0:WCOLS - 512], ALU.subtract).then_inc(w_ready, 1)
                    v.tensor_tensor(bin_[:, 0:512], bin_raw[:, 0:512], p_v[:, 0, 0:512], ALU.add).then_inc(w_ready, 1)
                    v.tensor_tensor(bin_[:, 512:WCOLS], bin_raw[:, 512:WCOLS], p_v[:, 1, 0:WCOLS - 512], ALU.add).then_inc(w_ready, 1)
                    dve.wait_ge(w_ready, 7)
                    bodies(dve, body)

                @block.tensor
                def _(pe):
                    mm = nc.tensor.matmul

                    def tokens(p, u, turn):
                        after(pe, h_ready, p)
                        pe.wait_ge(patches_in[u], 16 * turn + 16)
                        for k in range(KC):
                            last = mm(p_tok[:, 0:D], pat[:, u, k], tokw[:, k], start=(k == 0), stop=(k == KC - 1))
                        last.then_inc(tok_ready, 1)

                    def transposes(p):
                        after(pe, xat_ready, 4 * p)
                        if not isinstance(p, int) or p:
                            for _ in range(9):
                                mm(p_tr[:, 0, 3 * P:4 * P], ident, ident, start=True, stop=True, skip_group_check=True)
                        pe.wait_ge(xa_ready, 3 * p + 3)
                        for c in range(2):
                            for j in range(3):
                                last = nc.tensor.transpose(p_tr[0:C, c, j * P:(j + 1) * P], xa[:, j, c * C:(c + 1) * C], ident)
                        last.then_inc(tr_ready, 1)

                    def project(p, u, j):
                        s = (u + j) % 2
                        t = 3 * p + j
                        pe.wait_ge(banks_read, t + 1)
                        for c in range(2):
                            rows = [xpre[:, u, c], xct[:, u, c, 0, LP:], xct[:, u, c, 1, LP:]][j]
                            mm(p_qk[:, s, 0:2 * D], rows, win[:, c, 0:2 * D], start=(c == 0), stop=(c == 1))
                        for c in range(2):
                            rows = [xpre[:, u, c], xct[:, u, c, 0, LP:], xct[:, u, c, 1, LP:]][j]
                            mm(p_v[:, s, 0:D + R + 1], rows, win[:, c, V0:MEAN + 1], start=(c == 0), stop=(c == 1))
                        for c in range(2):
                            rows = xsq[:, u, c, j * P:(j + 1) * P]
                            last = mm(p_v[:, s, D + R + 1:D + R + 2], rows, win[:, c, MEAN:MEAN + 1], start=False, stop=(c == 1), skip_group_check=True)
                        last.then_inc(proj_ready, 1)

                    def hidden(p):
                        after(pe, par_read, p)
                        wait_apart(pe, hid_silu, 3 * p + 3)
                        for j in range(3):
                            last = nc.tensor.transpose(p_h[0:R, j * P:(j + 1) * P], hs[:, j], ident)
                        last.then_inc(hid_tr, 1)

                    def gate_params(p):
                        wait_apart(pe, hidt_ready, p + 1)
                        for j in range(3):
                            last = mm(p_h[:, j * H * NG:(j + 1) * H * NG], hst[:, j * P:(j + 1) * P], bn2s[:], start=True, stop=True, skip_group_check=True)
                        last.then_inc(par_ready, 1)

                    def body(p, u, ahead):
                        first = isinstance(p, int) and p == 0
                        if ahead >= 1:
                            transposes(p + 1)
                        wait_apart(pe, xsq_ready, 4 * p + 4)
                        wait_apart(pe, xpre_ready, p + 1)
                        project(p, u, 0)
                        if not first:
                            hidden(p - 1)
                        project(p, u, 1)
                        if ahead >= 2:
                            tokens(p + 2, u, (p + 2 - u) // 2)
                        if not first:
                            gate_params(p - 1)
                        project(p, u, 2)

                    pe.wait_ge(tokw_in, 16)
                    tokens(0, 0, 0)
                    tokens(1, 1, 0)
                    pe.wait_ge(small_in, 16 * 7)
                    transposes(0)
                    pe.wait_ge(prep_v, 6)
                    for half, (a, b) in enumerate(((0, 512), (512, WCOLS))):
                        for c in range(2):
                            last = mm(p_qk[0:C, half, 0:b - a], ones_d[:, 0:C], wgain[:, c, a:b], start=(c == 0), stop=(c == 1))
                        last.then_inc(prep_pe, 1)
                    for half, (a, b) in enumerate(((0, 512), (512, WCOLS))):
                        for c in range(2):
                            last = mm(p_v[:, half, 0:b - a], lnb_wide[:, c], win_raw[:, c, a:b], start=(c == 0), stop=(c == 1))
                        last.then_inc(prep_pe, 1)
                    pe.wait_ge(w_ready, 7)
                    bodies(pe, body)
                    hidden(PAIRS - 1)
                    gate_params(PAIRS - 1)

        wout_raw = sbuf("wout_raw", [C, 2, D])
        wout = sbuf("wout", [C, 2, D])
        mn = sbuf("mn", [C, 2])
        mnb_wide = sbuf("mnb_wide", [C, P])
        bout = sbuf("bout", [P, D])
        wg_raw = sbuf("wg_raw", [C, 2, E])
        wgc = sbuf("wgc", [C, 2, E])
        mean_w = sbuf("mean_w", [C, P])
        eps = sbuf("eps", [P, 1])
        neg_half = sbuf("neg_half_c", [P, 3])
        den, rden, rden2 = (gates[:].rearrange("p t n -> p (t n)")[:, i * NT * H:(i + 1) * NT * H].rearrange("p (t h) -> p t h", h=H)
                            for i in range(3))
        vpad = sbuf("vpad", [P, 3, 2 * D])
        numt = sbuf("numt", [C, 2, P])
        out_w_in, zeroed, fold = (top.enter_context(nc.semaphore(x)) for x in ("out_w_in", "zeroed", "c_fold"))

        with ExitStack() as ctx:
            def sb(name, shape):
                return ctx.enter_context(nc.sbuf_tensor(name, shape, F32))

            def sem(name):
                return ctx.enter_context(nc.semaphore(name))

            tanhs = sb("tanhs", [P, NG, NT, H])
            phase = sb("phase", [P, NT, H])
            sine = sb("sine", [P, NT, H])
            cosine = sb("cosine", [P, NT, H])
            amp = sb("amp", [P, NT, H])
            amps = sb("amps", [P, NT, H])
            gate = sb("gate", [P, NT, H])
            rate = sb("rate", [P, NT, H])
            log_rate = sb("log_rate", [P, NT, H])
            keep = sb("keep", [P, NT, H])
            safe = sb("safe", [P, NT, H])
            inv_df = sb("inv_df", [P, NT, H])
            half_temp = sb("half_temp", [P, 1])
            p_sum = ctx.enter_context(nc.psum_tensor("p_sum", [P, 512], F32))
            temp_in, tanh_done, steps, sine_done, rate_log, gate_tanh, sums_ready, df_ready = (
                sem(x) for x in ("temp_in", "tanh_done", "steps", "sine_done", "rate_log", "gate_tanh", "sums_ready", "df_ready"))

            with nc.Block() as block:
                @block.sync
                def _(sp):
                    sp.dma_start(half_temp[:], temp).then_inc(temp_in, 16)
                    sp.dma_start(wout_raw[:], w_out).then_inc(out_w_in, 16)
                    sp.dma_start(mn[:], mn_gb).then_inc(out_w_in, 16)
                    sp.dma_start(bout[:], b_out).then_inc(out_w_in, 16)
                    sp.dma_start(wg_raw[:], wg).then_inc(out_w_in, 16)

                @block.gpsimd
                def _(pool):
                    nc.gpsimd.memset(vpad[:], 0.0).then_inc(zeroed, 1)
                    nc.gpsimd.memset(numt[:], 0.0).then_inc(zeroed, 1)
                    nc.gpsimd.memset(mean_w[:], 1.0 / D).then_inc(zeroed, 1)
                    nc.gpsimd.memset(eps[:], 1e-5).then_inc(zeroed, 1)
                    nc.gpsimd.memset(neg_half[:], -0.5).then_inc(zeroed, 1)

                @block.scalar
                def _(act):
                    raw = gates[:].rearrange("p t (h n) -> p n t h", n=NG)
                    for n in (4, 1, 3, 0, 2):
                        nc.scalar.activation(tanhs[:, n], raw[:, n], ACT.Tanh, scale=1.0 if n % 2 else 0.5).then_inc(tanh_done, 1)
                    act.wait_ge(steps, 1)
                    nc.scalar.activation(log_rate[:], rate[:], ACT.Ln).then_inc(rate_log, 1)
                    act.wait_ge(steps, 3)
                    nc.scalar.activation(sine[:], phase[:], ACT.Sin, scale=1.5707962).then_inc(sine_done, 1)
                    act.wait_ge(sums_ready, 1)
                    nc.scalar.activation(decay[:], p_sum[:, 0:NT * H].rearrange("p (t h) -> p t h", h=H), ACT.Exp).then_inc(df_ready, 1)
                    act.wait_ge(steps, 8)
                    nc.scalar.activation(gate[:], amps[:], ACT.Tanh, scale=half_temp[:, 0:1]).then_inc(gate_tanh, 1)

                @block.tensor
                def _(pe):
                    pe.wait_ge(rate_log, 1)
                    of = log_rate[:].rearrange("p (g j) h -> p j g h", j=3)
                    to = p_sum[:, 0:NT * H].rearrange("p (g j h) -> p j g h", j=3, h=H)
                    nc.tensor.matmul(to[:, 0], u_pre, of[:, 0], start=True, stop=True, skip_group_check=True)
                    for b in range(2):
                        nc.tensor.matmul(to[:, 1 + b], u_txt, of[:, 1 + b], start=False, stop=False, skip_group_check=True)
                        last = nc.tensor.matmul(to[:, 1 + b], prefix_of[b], of[:, 0], start=False, stop=True, skip_group_check=True)
                    last.then_inc(sums_ready, 1)

                @block.vector
                def _(dve):
                    v = nc.vector

                    def step(n, ins):
                        ins.then_inc(steps, 1)
                        dve.wait_ge(steps, n)

                    dve.wait_ge(tanh_done, 1)
                    step(1, v.tensor_scalar(rate[:], tanhs[:, 4], 0.325, 0.625, ALU.mult, ALU.add))
                    step(2, v.tensor_scalar(keep[:], rate[:], -1.0, 1.0, ALU.mult, ALU.add))
                    dve.wait_ge(tanh_done, 3)
                    step(3, v.tensor_tensor(phase[:], tanhs[:, 1], tanhs[:, 3], ALU.subtract))
                    dve.wait_ge(tanh_done, 5)
                    step(4, v.tensor_scalar(amp[:], tanhs[:, 0], 0.5, 0.5, ALU.mult, ALU.add))
                    step(5, v.tensor_scalar(cosine[:], tanhs[:, 2], 0.5, 0.5, ALU.mult, ALU.add))
                    step(6, v.tensor_tensor(amp[:], amp[:], cosine[:], ALU.mult))
                    dve.wait_ge(temp_in, 16)
                    dve.wait_ge(sine_done, 1)
                    v.tensor_scalar(half_temp[:], half_temp[:], 0.5, None, ALU.mult)
                    step(7, v.tensor_tensor(cosine[:], amp[:], sine[:], ALU.mult))
                    v.tensor_tensor(cosine[:], cosine[:], sine[:], ALU.mult).then_inc(temp_in, 1)
                    dve.wait_ge(temp_in, 17)
                    step(8, v.scalar_tensor_tensor(amps[:], cosine[:], -2.0, amp[:], ALU.mult, ALU.add))
                    dve.wait_ge(df_ready, 1)
                    step(9, v.tensor_scalar(safe[:], decay[:], 1e-8, None, ALU.add))
                    step(10, v.reciprocal(inv_df[:], safe[:]))
                    v.tensor_scalar(clip_hi[:], inv_df[:], 5.0, None, ALU.mult).then_inc(steps, 1)
                    v.tensor_scalar(clip_lo[:], inv_df[:], -5.0, None, ALU.mult).then_inc(steps, 1)
                    step(13, v.tensor_tensor(gain_z[:], keep[:], inv_df[:], ALU.mult))
                    dve.wait_ge(gate_tanh, 1)
                    step(14, v.tensor_scalar(gate[:], gate[:], 0.5, 0.5, ALU.mult, ALU.add))
                    step(15, v.tensor_tensor(gain_kv[:], gate[:], gain_z[:], ALU.mult))

        num = sbuf("num", [P, NT, D])
        pair_code = sbuf("pair_code", [P, PAIRS], mybir.dt.int32)
        half_flag = sbuf("half_flag", [P, 2], mybir.dt.int32)

        def wide(ap, n):
            return ap.rearrange("p j h -> p (j h)").unsqueeze(2).broadcast_to([P, ap.shape[1] * ap.shape[2], n])

        with ExitStack() as ctx:
            def sb(name, shape):
                return ctx.enter_context(nc.sbuf_tensor(name, shape, F32))

            def ps(name, shape):
                return ctx.enter_context(nc.psum_tensor(name, shape, F32))

            def sem(name):
                return ctx.enter_context(nc.semaphore(name))

            HC = C // DH
            qd = sb("qd", [P, 3, D])
            kg = sb("kg", [P, 3, D])
            kpre = sb("kpre", [P, 2, D])
            kz = sb("kz", [P, 3, D])
            qkt = sb("qkt", [C, 3, 4, P])
            qm = sb("qm", [C, 3, HC, P])
            st = sb("st", [P, 3, HC, P])
            state = sb("state", [C, 2, 2, C])
            z = sb("z", [P, 3, D])
            zd = sb("zd", [P, 3, D])
            zq = sb("zq", [P, 1, D])
            p_s = ps("p_scores", [P, 4, 512])
            p_qt = ps("p_qt", [P, 512])
            p_n = ps("p_numt", [P, 512])
            p_st = ps("p_st", [P, 512])
            p_b = ps("p_b", [P, 512])

            (fold_sums, bias_added, kv_max, qk_ready, kpre_ready, kz_ready, v_ready, t_ready, qkt_ready, qm0_ready, qm1_ready, sc_ready, st_ready,
             av_ready, s_ready, state_in, numt_ready, zb_ready, num_out, z_step, z_out, zd_ready) = (sem(x) for x in (
                 "fold_sums", "bias_added", "kv_max", "qk_ready", "kpre_ready", "kz_ready", "v_ready", "t_ready", "qkt_ready", "qm0_ready", "qm1_ready",
                 "sc_ready", "st_ready", "av_ready", "s_ready", "state_in", "numt_ready", "zb_ready", "num_out", "z_step", "z_out", "zd_ready"))

            def pairs(eng, body, ahead=1):
                body(0)
                with eng.Fori(1, PAIRS - ahead) as p:
                    body(p)
                for p in range(PAIRS - ahead, PAIRS):
                    body(p)

            def real(ap):
                return ap.rearrange("p (b t) -> p b t", b=2)[:, :, 0:LP]

            def is_first(p, j):
                return isinstance(p, int) and p == 0 and j == 0

            def is_last(p, j):
                return isinstance(p, int) and p == PAIRS - 1 and j == 2

            with nc.Block() as block:
                @block.gpsimd
                def _(pool):
                    g = nc.gpsimd

                    def k_for_z(n, j):
                        after(pool, zb_ready, n if j == 0 else n - 2)
                        g.tensor_tensor(heads(kz[:, j:j + 1]), heads(qk[:, ds(n, 1), D:2 * D]), wide(gain_z[:, ds(n, 1), :], DH), ALU.mult).then_inc(kz_ready, 1)

                    def z_scaled(n, j):
                        wait_apart(pool, z_out, n + 1)
                        after(pool, z_step, 2 * n)
                        g.tensor_tensor(heads(zd[:, j:j + 1]), heads(z[:, j:j + 1]), wide(decay[:, ds(n, 1), :], DH), ALU.mult).then_inc(zd_ready, 1)

                    def body(p):
                        for j in range(3):
                            n = 3 * p + j
                            after(pool, t_ready, n - 2)
                            if j == 0:
                                after(pool, kpre_ready, p)
                            tile = ds(n, 1)
                            g.tensor_tensor(heads(qd[:, j:j + 1]), heads(qk[:, tile, 0:D]), wide(decay[:, tile, :], DH), ALU.mult).then_inc(qk_ready, 1)
                            g.tensor_tensor(heads(kg[:, j:j + 1]), heads(qk[:, tile, D:2 * D]), wide(gain_kv[:, tile, :], DH), ALU.mult).then_inc(qk_ready, 1)
                            if j == 0:
                                after(pool, s_ready, p)
                                wait_apart(pool, qk_ready, 2 * n + 2)
                                rows_of = cst[:, sel0:sel0 + 2 * P].rearrange("p (b t) -> p b t", b=2)[:, :, 0:1].broadcast_to([P, 2, D])
                                g.tensor_tensor(kpre[:], kg[:, 0:1].broadcast_to([P, 2, D]), rows_of, ALU.mult).then_inc(kpre_ready, 1)
                            if not is_first(p, j):
                                k_for_z(n - 1, (j - 1) % 3)
                            if not (isinstance(n, int) and n < 2):
                                z_scaled(n - 2, (j - 2) % 3)
                            if j == 2:
                                pool.wait_ge(fold, 5)
                                g.tensor_tensor(hid[:, ds(3 * p, 3), :], hid[:, ds(3 * p, 3), :],
                                                bout[:].unsqueeze(1).broadcast_to([P, 3, D]), ALU.add).then_inc(bias_added, 1)

                    pairs(pool, body)
                    k_for_z(NT - 1, 2)
                    z_scaled(NT - 2, 1)
                    z_scaled(NT - 1, 2)

                @block.scalar
                def _(act):
                    def v_in(n, j):
                        after(act, av_ready, 2 * n - 4)
                        to = vpad[:, j].rearrange("p (m c) -> p m c", c=64)
                        for b in range(2):
                            nc.scalar.copy(to[:, :, 48 * b:48 * b + DH],
                                           val[:, ds(n, 1), :].rearrange("p o (m b e) -> p (o m) b e", b=2, e=DH)[:, :, b]).then_inc(v_ready, 1)

                    def qk_in(n, j):
                        after(act, av_ready, 2 * n - 4)
                        wait_apart(act, t_ready, n + 1)
                        nc.scalar.copy(qkt[:, j], p_qt[0:C, :].rearrange("p (c t) -> p c t", c=4)).then_inc(qkt_ready, 1)

                    def q_in(n, j):
                        after(act, sc_ready, 2 * n - 1)
                        wait_apart(act, qkt_ready, n + 1)
                        for h in range(HC):
                            if j:
                                nc.scalar.mul(qm[:, (2 * j + 1) % 3, h], qkt[:, j, 1], head_of[:, h:h + 1]).then_inc(qm1_ready, 1)
                            else:
                                nc.scalar.mul(qm[:, 1, h, 0:2 * LP].rearrange("p (b t) -> p b t", b=2), real(qkt[:, j, 1]),
                                              head_of[:, h:h + 1]).then_inc(qm1_ready, 1)

                    def out(n, j, z_of=True, num_of=True):
                        if z_of:
                            after(act, zd_ready, n - 2)
                        wait_apart(act, zb_ready, n + 1)
                        if z_of:
                            nc.scalar.copy(z[:, j:j + 1], p_b[:, 0:D].unsqueeze(1)).then_inc(z_out, 1)
                        if num_of:
                            nc.scalar.copy(num[:, ds(n - 1, 1), :], p_b[:, D:2 * D].unsqueeze(1)).then_inc(num_out, 1)

                    def num_t(n, j):
                        after(act, zb_ready, n)
                        wait_apart(act, av_ready, 2 * n + 2)
                        if j:
                            nc.scalar.copy(numt[:], p_n[0:C, 0:2 * P].rearrange("p (c t) -> p c t", c=2)).then_inc(numt_ready, 1)
                        else:
                            nc.scalar.copy(numt[:].rearrange("p c (b t) -> p (c b) t", b=2)[:, :, 0:LP],
                                           p_n[0:C, 0:2 * P].rearrange("p (x t) -> p x t", x=4)[:, :, 0:LP]).then_inc(numt_ready, 1)

                    def body(p):
                        for j in range(3):
                            n = 3 * p + j
                            if not is_last(p, j):
                                qk_in(n + 1, (j + 1) % 3)
                                v_in(n + 1, (j + 1) % 3)
                            if not is_first(p, j):
                                num_t(n - 1, (j - 1) % 3)
                            if not is_last(p, j):
                                q_in(n + 1, (j + 1) % 3)
                            out(n, j, num_of=not is_first(p, j))

                    act.wait_ge(zeroed, 5)
                    qk_in(0, 0)
                    q_in(0, 0)
                    v_in(0, 0)
                    pairs(act, body)
                    num_t(NT - 1, 2)
                    out(NT, 0, z_of=False)

                @block.tensor
                def _(pe):
                    mm = nc.tensor.matmul

                    def transposes(n, j):
                        after(pe, qkt_ready, n)
                        wait_apart(pe, qk_ready, 2 * n + 2)
                        for i in range(4):
                            last = nc.tensor.transpose(p_qt[0:C, i * P:(i + 1) * P], (qd, kg)[i // 2][:, j, (i % 2) * C:(i % 2 + 1) * C], ident)
                        last.then_inc(t_ready, 1)

                    def scores(n, j, c):
                        after(pe, st_ready, 2 * n + c - 1)
                        if c == 0:
                            wait_apart(pe, qkt_ready, n + 1)
                            wait_apart(pe, qm0_ready, n + 1)
                        else:
                            wait_apart(pe, qm1_ready, HC * n + HC)
                        t = P if j else 2 * LP
                        for half in range(2):
                            last = mm(p_s[:, 2 * c + half, 0:3 * t].rearrange("p (h t) -> p h t", h=3), qkt[:, j, 2 + c],
                                      qm[:, (2 * j + c) % 3, 3 * half:3 * half + 3, 0:t], start=True, stop=True)
                        last.then_inc(sc_ready, 1)

                    def values(p, j, c):
                        n = 3 * p + j
                        wait_apart(pe, st_ready, 2 * n + c + 1)
                        if c == 0:
                            after(pe, numt_ready, n)
                            wait_apart(pe, v_ready, 2 * n + 2)
                        to = p_n[:, c * P:(c + 1) * P]
                        if j:
                            wait_apart(pe, state_in, p + 1)
                            mm(to[0:C], state[:, j - 1, c], qkt[:, j, c], start=True, stop=False, skip_group_check=True)
                        for b in range(2):
                            for a in range(3):
                                h = HC * c + 2 * a + b
                                rows32 = to[32 * a:32 * a + 32]
                                t = P if j else 2 * LP
                                last = mm(rows32 if j else real(rows32), vpad[:, j, 32 * h:32 * h + 32], st[:, (2 * j + c) % 3, 2 * a + b, 0:t],
                                          start=(j == 0 and b == 0), stop=(b == 1), skip_group_check=True, tile_position=(0, 32 * a))
                        last.then_inc(av_ready, 1)

                    def states(p):
                        wait_apart(pe, kpre_ready, p + 1)
                        after(pe, state_in, p)
                        for b in range(2):
                            for c in range(2):
                                last = mm(p_st[0:C, (2 * b + c) * C:(2 * b + c + 1) * C], kpre[:, b, c * C:(c + 1) * C],
                                          val[:, ds(3 * p, 1), c * C:(c + 1) * C].rearrange("p o d -> p (o d)"), start=True, stop=True, skip_group_check=True)
                        last.then_inc(s_ready, 1)

                    def z_and_back(n, j, z=True, back=True):
                        after(pe, z_out, n)
                        after(pe, num_out, n - 1)
                        if z:
                            wait_apart(pe, kz_ready, n + 1)
                            last = mm(p_b[:, 0:D], u_txt if j else u_pre, kz[:, j], start=True, stop=(j == 0), skip_group_check=True)
                            if j:
                                last = mm(p_b[:, 0:D], prefix_of[j - 1], kz[:, 0], start=False, stop=True, skip_group_check=True)
                        if back:
                            wait_apart(pe, numt_ready, n)
                            for c in range(2):
                                last = nc.tensor.transpose(p_b[:, D + c * C:D + (c + 1) * C], numt[:, c], ident[0:C, 0:C])
                        last.then_inc(zb_ready, 1)

                    def body(p):
                        for j in range(3):
                            n = 3 * p + j
                            if not is_last(p, j):
                                transposes(n + 1, (j + 1) % 3)
                            scores(n, j, 0)
                            if not is_first(p, j):
                                values(p - (j == 0), (j - 1) % 3, 1)
                            scores(n, j, 1)
                            if j == 0:
                                states(p)
                            values(p, j, 0)
                            z_and_back(n, j, back=not is_first(p, j))

                    pe.wait_ge(zeroed, 5)
                    pe.wait_ge(fold, 2)
                    mm(p_b[:, 0:D], mnb_wide[:], wout_raw[:, 0], start=True, stop=False, skip_group_check=True)
                    mm(p_b[:, 0:D], mnb_wide[:], wout_raw[:, 1], start=False, stop=True, skip_group_check=True)
                    mm(p_b[0:C, D:D + E], mean_w[:, 0:C], wg_raw[:, 0], start=True, stop=False, skip_group_check=True)
                    mm(p_b[0:C, D:D + E], mean_w[:, 0:C], wg_raw[:, 1], start=False, stop=True, skip_group_check=True).then_inc(fold_sums, 1)
                    transposes(0, 0)
                    pe.wait_ge(fold, 5)
                    pairs(pe, body)
                    values(PAIRS - 1, 2, 1)
                    z_and_back(NT, 0, z=False)

                @block.vector
                def _(dve):
                    v = nc.vector

                    def q_in(n, j):
                        after(dve, sc_ready, 2 * n - 2)
                        wait_apart(dve, qkt_ready, n + 1)
                        if j:
                            v.tensor_tensor(qm[:, (2 * j) % 3], qkt[:, j, 0].unsqueeze(1).broadcast_to([C, HC, P]),
                                            head_of.unsqueeze(2).broadcast_to([C, HC, P]), ALU.mult).then_inc(qm0_ready, 1)
                        else:
                            v.tensor_tensor(qm[:, 0, :, 0:2 * LP].rearrange("p h (b t) -> p h b t", b=2),
                                            real(qkt[:, j, 0]).unsqueeze(1).broadcast_to([C, HC, 2, LP]),
                                            head_of.unsqueeze(2).unsqueeze(3).broadcast_to([C, HC, 2, LP]), ALU.mult).then_inc(qm0_ready, 1)

                    def mask(n, j, c):
                        after(dve, av_ready, 2 * n + c - 2)
                        wait_apart(dve, sc_ready, 2 * n + c + 1)
                        t = P if j else 2 * LP
                        v.tensor_tensor(st[:, (2 * j + c) % 3].rearrange("p (a h) t -> p a h t", a=2)[:, :, :, 0:t],
                                        p_s[:, 2 * c:2 * c + 2, 0:3 * t].rearrange("p a (h t) -> p a h t", h=3),
                                        (u_txt if j else pre_mask).unsqueeze(1).unsqueeze(1).broadcast_to([P, 2, 3, t]), ALU.mult).then_inc(st_ready, 1)

                    def body(p):
                        for j in range(3):
                            n = 3 * p + j
                            if not is_last(p, j):
                                q_in(n + 1, (j + 1) % 3)
                            mask(n, j, 0)
                            v.tensor_reduce(kmax[:, ds(n, 1), :].rearrange("p o h -> p (o h)"), heads(qk[:, ds(n, 1), D:2 * D]), AX.X, ALU.max).then_inc(kv_max, 1)
                            v.tensor_reduce(vmax[:, ds(n, 1), :].rearrange("p o h -> p (o h)"), heads(val[:, ds(n, 1), :]), AX.X, ALU.max,
                                            apply_absolute_value=True).then_inc(kv_max, 1)
                            mask(n, j, 1)
                            if not (isinstance(n, int) and n < 2):
                                denominators(n - 2, (j - 2) % 3)
                            if j == 0:
                                wait_apart(dve, s_ready, p + 1)
                                after(dve, av_ready, 6 * p)
                                v.tensor_tensor(state[:].rearrange("p b c d -> p (b c) d"), p_st[0:C, 0:4 * C].rearrange("p (x d) -> p x d", x=4),
                                                same_head.unsqueeze(1).broadcast_to([C, 4, C]), ALU.mult).then_inc(state_in, 1)

                    def denominators(n, j):
                        wait_apart(dve, z_step, 2 * n + 4)
                        wait_apart(dve, zd_ready, n + 1)
                        v.scalar_tensor_tensor(zq[:], zd[:, j:j + 1], 1e4, qk[:, ds(n, 1), 0:D], ALU.min, ALU.mult).then_inc(z_step, 1)
                        wait_apart(dve, z_step, 2 * n + 5)
                        v.tensor_reduce(den[:, ds(n, 1), :].rearrange("p o h -> p (o h)"), heads(zq[:]), AX.X, ALU.add).then_inc(z_step, 1)

                    v.sem_inc(z_step, 4)
                    dve.wait_ge(zeroed, 5)
                    dve.wait_ge(out_w_in, 64)
                    v.tensor_copy(mnb_wide[:], mn[:, 1:2].broadcast_to([C, P])).then_inc(fold, 1)
                    v.tensor_scalar(wout[:].rearrange("p c d -> p (c d)"), wout_raw[:].rearrange("p c d -> p (c d)"), mn[:, 0:1], None, ALU.mult).then_inc(fold, 1)
                    q_in(0, 0)
                    dve.wait_ge(fold_sums, 1)
                    v.tensor_tensor(bout[:], bout[:], p_b[:, 0:D], ALU.add).then_inc(fold, 1)
                    for c in range(2):
                        v.tensor_tensor(wgc[:, c], wg_raw[:, c], p_b[0:C, D:D + E], ALU.subtract).then_inc(fold, 1)
                    pairs(dve, body)
                    denominators(NT - 2, 1)
                    denominators(NT - 1, 2)

        with ExitStack() as ctx:
            def sb(name, shape, dt=F32):
                return ctx.enter_context(nc.sbuf_tensor(name, shape, dt))

            def ps(name, shape):
                return ctx.enter_context(nc.psum_tensor(name, shape, F32))

            def sem(name):
                return ctx.enter_context(nc.semaphore(name))

            HB = HG // 2
            BC = HB * DH * DH
            STEPS = 2 * 3
            bound = sb("bound", [P, 2, NT, H])
            den1 = sb("den1", [P, NT, H])
            beyond = sb("beyond", [P, NT, H])
            beyond_hg = sb("beyond_hg", [P, NT, NHG])
            unit_on = sb("unit_on", [P, UNITS])
            counts_up = sb("counts_up", [P, 2, 32 + UNITS])
            unit_rank = sb("unit_rank", [P, UNITS])
            code01 = sb("code01", [P, PAIRS])
            k_u = sb("k_u", [P, 3, HG * DH])
            q_u = sb("q_u", [P, 3, HG * DH])
            outer = sb("outer", [P, STEPS, BC])
            prod = sb("prod", [P, 2, BC])
            p_f = ps("p_f", [P, 512])
            p_g = ps("p_g", [P, STEPS, BC])
            rden_step, flag_step, flags_summed, flags_ready, ku_ready, outer_made, outer_ready, state_ready, state_read, num_ready = (
                sem(x) for x in ("rden_step", "flag_step", "flags_summed", "flags_ready", "ku_ready", "outer_made", "outer_ready",
                                 "state_ready", "state_read", "num_ready"))

            def units(eng, unit):
                eng.wait_ge(flags_ready, 2)
                with eng.Fori(0, 2) as half:
                    some = eng.value_load(half_flag[0:1, ds(half, 1)], min_val=0, max_val=1)
                    with eng.If(some != 0):
                        with eng.Fori(0, PAIRS // 2) as i:
                            p = PAIRS // 2 * half + i
                            code = eng.value_load(pair_code[0:1, ds(p, 1)], min_val=0, max_val=DIGIT ** NHG - 1)
                            with eng.If(code != 0):
                                ranks = [code // DIGIT ** g % DIGIT for g in range(NHG)]
                                for g, rank in enumerate(ranks):
                                    with eng.If(rank != 0):
                                        unit(p, g, rank)

            with nc.Block() as block:
                @block.tensor
                def _(pe):
                    mm = nc.tensor.matmul
                    pe.sem_inc(state_ready, STEPS)
                    pe.wait_ge(flag_step, 4)
                    by_tile = beyond_hg[:].rearrange("p (g j) n -> p j g n", j=3)
                    to = p_f[:, 0:UNITS].rearrange("p (g n) -> p g n", n=NHG)
                    mm(to, prefix_of[0], by_tile[:, 0], start=True, stop=False)
                    mm(to, prefix_of[1], by_tile[:, 0], start=False, stop=False)
                    mm(to, u_ones, by_tile[:, 1], start=False, stop=False)
                    mm(to, u_ones, by_tile[:, 2], start=False, stop=True).then_inc(flags_summed, 1)

                    def unit(p, g, rank):
                        wait_apart(pe, state_read, STEPS * rank)
                        for n in range(STEPS):
                            j, half = divmod(n, 2)
                            wait_apart(pe, outer_ready, HB * (STEPS * rank + n + 1))
                            last = mm(p_g[:, n], u_txt if j else u_pre, outer[:, n], start=True, stop=(j == 0))
                            if j:
                                last = mm(p_g[:, n], prefix_of[j - 1], outer[:, half], start=False, stop=True)
                            last.then_inc(state_ready, 1)

                    units(pe, unit)

                @block.vector
                def _(dve):
                    v = nc.vector

                    def step(n, ins):
                        ins.then_inc(flag_step, 1)
                        dve.wait_ge(flag_step, n)

                    v.sem_inc(ku_ready, 2)
                    v.sem_inc(outer_made, STEPS)
                    v.sem_inc(outer_ready, STEPS * HB)
                    v.sem_inc(state_read, STEPS)
                    v.sem_inc(num_ready, STEPS)
                    v.memset(counts_up[:], 0.0)
                    step(1, v.tensor_tensor(bound[:, 0], kmax[:], vmax[:], ALU.mult))
                    step(2, v.tensor_tensor(bound[:, 1], bound[:, 0], gain_kv[:], ALU.mult))
                    step(3, v.tensor_tensor(beyond[:], bound[:, 1], clip_hi[:], ALU.is_gt))
                    step(4, v.tensor_reduce(beyond_hg[:].rearrange("p t n -> p (t n)"), beyond[:].rearrange("p t (n h) -> p (t n) h", h=HG), AX.X, ALU.max))
                    v.tensor_scalar(den1[:], den[:], 1e-4, None, ALU.add).then_inc(rden_step, 1)
                    dve.wait_ge(rden_step, 1)
                    v.reciprocal(rden[:], den1[:]).then_inc(rden_step, 1)
                    dve.wait_ge(rden_step, 2)
                    v.tensor_tensor(rden2[:], rden[:], rden[:], ALU.mult).then_inc(rden_step, 1)
                    dve.wait_ge(flags_summed, 1)
                    step(5, v.tensor_scalar(unit_on[:], p_f[:, 0:UNITS], 1.0, None, ALU.min))
                    v.tensor_reduce(half_flag[:], unit_on[:].rearrange("p (g n) -> p g n", g=2), AX.X, ALU.max).then_inc(flags_ready, 1)
                    step(6, v.tensor_copy(counts_up[:, 0, 32:], unit_on[:]))
                    n, shift, u = 7, 1, 0
                    while shift < UNITS:
                        step(n, v.tensor_tensor(counts_up[:, 1 - u, 32:], counts_up[:, u, 32:], counts_up[:, u, 32 - shift:32 + UNITS - shift], ALU.add))
                        n, shift, u = n + 1, 2 * shift, 1 - u
                    step(n, v.tensor_tensor(unit_rank[:], counts_up[:, u, 32:], unit_on[:], ALU.mult))
                    ranks = unit_rank[:].rearrange("p (g n) -> p g n", n=NHG)
                    step(n + 1, v.scalar_tensor_tensor(code01[:], ranks[:, :, 1], float(DIGIT), ranks[:, :, 0], ALU.mult, ALU.add))
                    v.scalar_tensor_tensor(pair_code[:], ranks[:, :, 2], float(DIGIT ** 2), code01[:], ALU.mult, ALU.add).then_inc(flags_ready, 1)

                    def unit(p, g, rank):
                        hs = slice(g * HG * DH, (g + 1) * HG * DH)
                        tiles3 = ds(3 * p, 3)

                        def of_heads(x):
                            return x[:, tiles3, g * HG:(g + 1) * HG].unsqueeze(3).broadcast_to([P, 3, HG, DH])

                        def apart(x):
                            return x.rearrange("p j (h d) -> p j h d", d=DH)

                        v.tensor_tensor(apart(k_u[:]), apart(qk[:, tiles3, D + g * HG * DH:D + (g + 1) * HG * DH]), of_heads(gain_kv), ALU.mult).then_inc(ku_ready, 1)
                        v.tensor_tensor(apart(q_u[:]), apart(qk[:, tiles3, hs]), of_heads(decay), ALU.mult).then_inc(ku_ready, 1)

                        def place(n):
                            j, half = divmod(n, 2)
                            return j, half, g * HG + half * HB

                        def cube(x):
                            return x.rearrange("p (h d e) -> p h d e", d=DH, e=DH)

                        def product(n):
                            j, half, first = place(n)
                            kk = k_u[:, j, half * HB * DH:(half + 1) * HB * DH].rearrange("p (h d) -> p h d", d=DH).unsqueeze(3).broadcast_to([P, HB, DH, DH])
                            vv = heads(val[:, ds(3 * p + j, 1), first * DH:(first + HB) * DH]).unsqueeze(2).broadcast_to([P, HB, DH, DH])
                            v.tensor_tensor(cube(outer[:, n]), kk, vv, ALU.mult).then_inc(outer_made, 1)

                        def clip(n):
                            j, half, first = place(n)
                            wait_apart(dve, outer_made, STEPS * rank + n + 1)
                            for h in range(HB):
                                hi, lo = (x[:, ds(3 * p + j, 1), first + h:first + h + 1].rearrange("p a b -> p (a b)") for x in (clip_hi, clip_lo))
                                o = outer[:, n, h * DH * DH:(h + 1) * DH * DH]
                                v.tensor_scalar(o, o, hi, lo, ALU.min, ALU.max).then_inc(outer_ready, 1)

                        def times_q(n):
                            j, half, first = place(n)
                            wait_apart(dve, num_ready, STEPS * rank + max(n - 1, 0))
                            wait_apart(dve, state_ready, STEPS * rank + n + 1)
                            qq = q_u[:, j, half * HB * DH:(half + 1) * HB * DH].rearrange("p (h d) -> p h d", d=DH).unsqueeze(3).broadcast_to([P, HB, DH, DH])
                            v.tensor_tensor(cube(prod[:, n % 2]), cube(p_g[:, n]), qq, ALU.mult).then_inc(state_read, 1)

                        def summed(n):
                            j, half, first = place(n)
                            wait_apart(dve, state_read, STEPS * rank + n + 1)
                            v.tensor_reduce(heads(num[:, ds(3 * p + j, 1), first * DH:(first + HB) * DH]),
                                            prod[:, n % 2].rearrange("p (h d e) -> p h e d", d=DH, e=DH), AX.X, ALU.add).then_inc(num_ready, 1)

                        wait_apart(dve, ku_ready, 2 * rank + 1)
                        product(0)
                        for n in range(STEPS):
                            if n + 1 < STEPS:
                                product(n + 1)
                            clip(n)
                        wait_apart(dve, ku_ready, 2 * rank + 2)
                        times_q(0)
                        for n in range(STEPS):
                            if n + 1 < STEPS:
                                times_q(n + 1)
                            summed(n)

                    units(dve, unit)

        with ExitStack() as ctx:
            def sb(name, shape):
                return ctx.enter_context(nc.sbuf_tensor(name, shape, F32))

            def ps(name, shape):
                return ctx.enter_context(nc.psum_tensor(name, shape, F32))

            def sem(name):
                return ctx.enter_context(nc.semaphore(name))

            sums = sb("sums", [P, 3, H])
            centred = sb("centred", [P, 3, D])
            sq = sb("sq", [P, 3, D])
            var = sb("var", [P, 3, H])
            deviation = sb("deviation3", [P, 3, H])
            att_var = sb("att_var", [P, 3, H])
            inv_dev = sb("inv_dev", [P, 3, H])
            rstd = sb("rstd3", [P, 3, H])
            attn = sb("attn", [P, 3, D])
            attn_t = sb("attn_t", [C, 3, 2, P])
            hid_t = sb("hid_t", [C, 3, 2, P])
            new_hid = sb("new_hid", [P, 3, D])
            bst = sb("bst2", [P, 3, 6])
            mv = sb("mv2", [P, 3, 2])
            var_eps = sb("var_eps", [P, 3])

            p_at = ps("p_at", [P, 2, 512])
            p_ht = ps("p_hid_t", [P, 2, 512])
            p_o = ps("p_o", [P, 2, 512])
            p_l = ps("p_l", [P, 512])
            p_idle = ps("p_idle", [P, 512])

            (att_step, sq_ready, var_ready, var_step, rstd_ready, attn_ready,
             att_tr, attn_t_ready, proj_ready, hid_ready, hid_tr, hid_t_ready, hid_kept, st_done, mv_ready, mv_kept,
             logit_ready, logit_read) = (sem(x) for x in (
                 "att_step", "sq_ready", "var_ready",
                 "var_step", "c_rstd_ready", "attn_ready", "att_tr", "attn_t_ready", "c_proj_ready", "hid_ready",
                 "c_hid_tr", "hid_t_ready", "hid_kept", "c_st_done", "c_mv_ready", "mv_kept", "logit_ready", "logit_read"))

            def bank_of(t, j, n):
                return t[:, j // 2, (j % 2) * n:(j % 2) * n + n]

            with nc.Block() as block:
                @block.sync
                def _(sp):
                    sp.dma_start(cs, counts).then_inc(cs_in, 16)

                @block.gpsimd
                def _(pool):
                    g = nc.gpsimd

                    def body(p):
                        wait_apart(pool, hid_ready, 2 * p + 2)
                        g.tensor_copy(hid[:, ds(3 * p, 3), :], new_hid[:]).then_inc(hid_kept, 1)
                        after(pool, mv_kept, 3 * p)
                        wait_apart(pool, mv_ready, 3 * p + 3)
                        g.tensor_scalar(var_eps[:], mv[:, :, 1], 1e-5, None, ALU.add).then_inc(mv_kept, 1)
                        g.tensor_copy(rows[:, ds(3 * p, 3), MEAN_AT:MEAN_AT + 1], mv[:, :, 0:1]).then_inc(mv_kept, 1)
                        wait_apart(pool, mv_kept, 3 * p + 2)
                        g.tensor_tensor(rows[:, ds(3 * p, 3), RSTD_AT:RSTD_AT + 1], var_eps[:].unsqueeze(2), neg_half[:].unsqueeze(2),
                                        ALU.pow).then_inc(mv_kept, 1)

                    pairs(pool, body)

                @block.scalar
                def _(act):
                    def square(p):
                        wait_apart(act, att_step, 2 * p + 2)
                        nc.scalar.activation(sq[:], centred[:], ACT.Square).then_inc(sq_ready, 1)

                    def root(p):
                        wait_apart(act, var_ready, 2 * p + 2)
                        nc.scalar.activation(deviation[:], att_var[:], ACT.Sqrt, bias=eps[:, 0:1], scale=1.0 / DH).then_inc(var_step, 1)

                    def to_sbuf(t, bank, done):
                        for i, n in ((0, 2), (1, 1)):
                            nc.scalar.copy(t[:, 2 * i:2 * i + n], bank[0:C, i, 0:n * 2 * P].rearrange("p (j c t) -> p j c t", j=n, c=2)).then_inc(done, 1)

                    def logits_out(p):
                        wait_apart(act, logit_ready, p + 1)
                        nc.scalar.copy(logits[:, ds(3 * p, 3), :], p_l[:, 0:3 * E].rearrange("p (j e) -> p j e", j=3)).then_inc(logit_read, 1)

                    def att_out(p):
                        after(act, proj_ready, p)
                        wait_apart(act, att_tr, p + 1)
                        to_sbuf(attn_t, p_at, attn_t_ready)

                    def body(p):
                        ahead = PAIRS - 1 - p if isinstance(p, int) else 2
                        hid_out(p)
                        if ahead >= 1:
                            att_out(p + 1)
                        if ahead >= 2:
                            square(p + 2)
                        logits_out(p)
                        if ahead >= 2:
                            root(p + 2)

                    def hid_out(p):
                        wait_apart(act, hid_tr, p + 1)
                        after(act, logit_ready, p)
                        to_sbuf(hid_t, p_ht, hid_t_ready)

                    square(0)
                    root(0)
                    square(1)
                    att_out(0)
                    root(1)
                    pairs(act, body, 2)

                @block.tensor
                def _(pe):
                    mm = nc.tensor.matmul

                    def turn(rows3, banks):
                        for j in range(3):
                            for c in range(2):
                                last = nc.tensor.transpose(bank_of(banks, j, 2 * P)[0:C, c * P:(c + 1) * P], rows3[:, j, c * C:(c + 1) * C], ident)
                        return last

                    def keep_warm(n):
                        for _ in range(n):
                            mm(p_idle[:, 0:D], ident[0:C, :], wout[:, 0], start=True, stop=True)

                    def logit(p):
                        wait_apart(pe, logit_read, p + 1)
                        wait_apart(pe, hid_t_ready, 2 * p + 2)
                        for j in range(3):
                            for c in range(2):
                                last = mm(p_l[:, j * E:(j + 1) * E], hid_t[:, j, c], wgc[:, c], start=(c == 0), stop=(c == 1), skip_group_check=True)
                        last.then_inc(logit_ready, 1)

                    def att_turn(p):
                        after(pe, attn_t_ready, 2 * p)
                        wait_apart(pe, attn_ready, p + 1)
                        turn(attn, p_at).then_inc(att_tr, 1)

                    def project(p):
                        after(pe, hid_ready, 2 * p)
                        wait_apart(pe, attn_t_ready, 2 * p + 2)
                        for j in range(3):
                            for c in range(2):
                                last = mm(bank_of(p_o, j, D), attn_t[:, j, c], wout[:, c], start=(c == 0), stop=(c == 1), skip_group_check=True)
                        last.then_inc(proj_ready, 1)

                    def hid_turn(p):
                        after(pe, hid_t_ready, 2 * p)
                        wait_apart(pe, hid_ready, 2 * p + 2)
                        turn(new_hid, p_ht).then_inc(hid_tr, 1)

                    def body(p):
                        more = not (isinstance(p, int) and p == PAIRS - 1)
                        if more:
                            att_turn(p + 1)
                        if isinstance(p, int) and p == PAIRS - 2:
                            project(p + 1)
                            logit(p)
                            hid_turn(p + 1)
                        else:
                            logit(p)
                            if more:
                                project(p + 1)
                                keep_warm(3)
                                hid_turn(p + 1)

                    keep_warm(10)
                    att_turn(0)
                    project(0)
                    hid_turn(0)
                    pairs(pe, body)

                @block.vector
                def _(dve):
                    v = nc.vector
                    v.sem_inc(logit_read, 1)
                    def sum_up(p):
                        v.tensor_reduce(sums[:].rearrange("p j h -> p (j h)"), heads(num[:, ds(3 * p, 3), :]), AX.X, ALU.add).then_inc(att_step, 1)

                    def centre(p):
                        wait_apart(dve, att_step, 2 * p + 1)
                        v.scalar_tensor_tensor(heads(centred[:]), wide(sums[:], DH), -1.0 / DH, heads(num[:, ds(3 * p, 3), :]),
                                               ALU.mult, ALU.add).then_inc(att_step, 1)

                    def variance(p):
                        wait_apart(dve, sq_ready, p + 1)
                        v.tensor_reduce(var[:].rearrange("p j h -> p (j h)"), heads(sq[:]), AX.X, ALU.add).then_inc(var_ready, 1)
                        wait_apart(dve, var_ready, 2 * p + 1)
                        v.tensor_tensor(att_var[:], var[:], rden2[:, ds(3 * p, 3), :], ALU.mult).then_inc(var_ready, 1)

                    def normed(p):
                        wait_apart(dve, var_step, p + 1)
                        v.reciprocal(inv_dev[:], deviation[:]).then_inc(rstd_ready, 1)
                        after(dve, att_tr, p)
                        wait_apart(dve, rstd_ready, 2 * p + 1)
                        v.tensor_tensor(rstd[:], inv_dev[:], rden[:, ds(3 * p, 3), :], ALU.mult).then_inc(rstd_ready, 1)
                        wait_apart(dve, rstd_ready, 2 * p + 2)
                        v.tensor_tensor(heads(attn[:]), heads(centred[:]), wide(rstd[:], DH), ALU.mult).then_inc(attn_ready, 1)

                    def residual(p):
                        after(dve, hid_tr, p)
                        after(dve, hid_kept, p)
                        wait_apart(dve, proj_ready, p + 1)
                        for i, n in ((0, 2), (1, 1)):
                            v.tensor_tensor(new_hid[:, 2 * i:2 * i + n], hid[:, ds(3 * p + 2 * i, n), :],
                                            p_o[:, i, 0:n * D].rearrange("p (j d) -> p j d", j=n), ALU.add).then_inc(hid_ready, 1)

                    def stats(p, some):
                        for j in some:
                            v.bn_stats(bst[:, j], new_hid[:, j]).then_inc(st_done, 1)

                    def moments(p):
                        after(dve, mv_kept, 3 * p)
                        for j in range(3):
                            wait_apart(dve, st_done, 3 * p + j + 1)
                            v.bn_aggr(mv[:, j], bst[:, j]).then_inc(mv_ready, 1)

                    def body(p):
                        ahead = PAIRS - 1 - p if isinstance(p, int) else 2
                        if ahead >= 2:
                            sum_up(p + 2)
                        wait_apart(dve, hid_ready, 2 * p + 2)
                        after(dve, mv_ready, 3 * p)
                        stats(p, (0,))
                        if ahead >= 2:
                            centre(p + 2)
                        stats(p, (1, 2))
                        moments(p)
                        if ahead >= 2:
                            variance(p + 2)
                        if ahead >= 1:
                            residual(p + 1)
                        if ahead >= 2:
                            normed(p + 2)

                    for p in range(2):
                        sum_up(p)
                        centre(p)
                        variance(p)
                        normed(p)
                    residual(0)
                    pairs(dve, body, 2)

        mid.close()

        def sbuf(name, shape, dt=F32):
            return top.enter_context(nc.sbuf_tensor(name, shape, dt))

        w2s = sbuf("w2s", [P, E, KC, D])
        b2s = sbuf("b2s", [P, E, D])
        expert_of = sbuf("expert_of", [P, SLOT_TILES], mybir.dt.int32)
        used_tiles = sbuf("used_tiles", [P, 1], mybir.dt.int32)
        w2_in = top.enter_context(nc.semaphore("w2_in"))
        with ExitStack() as ctx:
            def sb(name, shape, dt=F32):
                return ctx.enter_context(nc.sbuf_tensor(name, shape, dt))

            def sem(name):
                return ctx.enter_context(nc.semaphore(name))

            token = cs[:, token0:token0 + NT]
            nowhere = cs[:, nowhere0:nowhere0 + NT]
            down = cs[:, down0:real0]
            down_real = cs[:, real0:steps0].rearrange("p (t e) -> p t e", e=E)
            tile_steps = cs[:, steps0:steps0 + E * MAXN].rearrange("p (e n) -> p e n", n=MAXN)
            tile_no = cs[:, tile0:tile0 + SLOT_TILES * E].rearrange("p (i e) -> p i e", e=E)
            shifted = sb("shifted", [P, NT, E])
            expd = sb("expd", [P, NT, E])
            total = sb("total", [P, NT])
            best = sb("best", [P, NT])
            mark = sb("mark", [P, NT, E])
            first = sb("first", [P, NT])
            choice = sb("choice", [P, NT, E])
            scaled = sb("scaled", [P, NT, E])
            tot = sb("tot", [P, NT, E])
            cum = sb("cum", [P, 2, NT, E])
            over = sb("over", [P, E, MAXN])
            tiles_e = sb("tiles_e", [P, E])
            ends = sb("ends", [P, 2, E])
            base = sb("base", [P, E])
            spot = sb("spot", [P, 2, NT, E])
            place = sb("place", [P, NT])
            place_u = sb("place_u", [P, NT], mybir.dt.uint32)
            past = sb("past", [P, SLOT_TILES, E])
            owner = sb("owner", [P, SLOT_TILES])
            p_r = ctx.enter_context(nc.psum_tensor("p_r", [P, 512], F32))
            p_n = ctx.enter_context(nc.psum_tensor("p_n", [P, 512], F32))
            steps, numbered, scaled_ready, choice_ready, exp_ready, counted, placed, scattered = (
                sem(x) for x in ("d_steps", "numbered", "scaled_ready", "choice_ready", "exp_ready", "counted",
                                 "placed", "scattered"))

            with nc.Block() as block:
                @block.sync
                def _(sp):
                    for e in range(E):
                        sp.dma_start(w2s[:, e], w2[:, e]).then_inc(w2_in, 16)
                    sp.dma_start(b2s[:], b2).then_inc(w2_in, 16)

                @block.gpsimd
                def _(pool):
                    g = nc.gpsimd
                    pool.wait_ge(cs_in, 16)
                    g.tensor_copy(rows[:, :, ID_AT], token).then_inc(numbered, 1)
                    pool.wait_ge(numbered, 1)
                    pool.wait_ge(slots_clear, 16)
                    pool.wait_ge(placed, 1)
                    for t in range(NT):
                        g.indirect_dma_start(out=sorted_rows, out_offset=bass.IndirectOffsetOnAxis(ap=place_u[:, t:t + 1], axis=0),
                                             in_=rows[:, t, :], in_offset=None, bounds_check=SLOT_TILES * P - 1,
                                             oob_is_err=False).then_inc(scattered, 16)
                    pool.wait_ge(scattered, 16 * NT)

                @block.scalar
                def _(act):
                    act.wait_ge(scaled_ready, 1)
                    nc.scalar.activation(expd[:], scaled[:], ACT.Exp).then_inc(exp_ready, 1)

                @block.tensor
                def _(pe):
                    pe.wait_ge(choice_ready, 1)
                    flat = choice[:].rearrange("p t e -> p (t e)")
                    nc.tensor.matmul(p_r[:, 0:NT * E], u_before, flat, start=True, stop=True).then_inc(counted, 1)
                    nc.tensor.matmul(p_n[:, 0:NT * E], u_ones, flat, start=True, stop=True).then_inc(counted, 1)

                @block.vector
                def _(dve):
                    v = nc.vector
                    made = [0]

                    def step(ins):
                        made[0] += 1
                        ins.then_inc(steps, 1)
                        dve.wait_ge(steps, made[0])

                    def each(ap):
                        return ap.unsqueeze(2).broadcast_to([P, NT, E])

                    step(v.tensor_reduce(best[:], logits[:], AX.X, ALU.max))
                    step(v.tensor_tensor(shifted[:], logits[:], each(best[:]), ALU.subtract))
                    dve.wait_ge(cs_in, 16)
                    step(v.scalar_tensor_tensor(mark[:], shifted[:], 0.0, down_real, ALU.is_equal, ALU.mult))
                    step(v.tensor_reduce(first[:], mark[:], AX.X, ALU.max))
                    v.tensor_tensor(choice[:], each(first[:]), down.unsqueeze(1).broadcast_to([P, NT, E]), ALU.is_equal).then_inc(choice_ready, 1)
                    v.tensor_tensor(scaled[:], shifted[:], each(rows[:, :, RSTD_AT]), ALU.mult).then_inc(scaled_ready, 1)
                    dve.wait_ge(counted, 2)
                    step(v.tensor_copy(tot[:], p_n[:, 0:NT * E].rearrange("p (t e) -> p t e", e=E)))
                    src, shift = tot[:], 1
                    while shift < NT:
                        dst = cum[:, (shift.bit_length() - 1) % 2]
                        v.tensor_copy(dst[:, :shift], src[:, :shift]).then_inc(steps, 1)
                        made[0] += 1
                        step(v.tensor_tensor(dst[:, shift:], src[:, shift:], src[:, :NT - shift], ALU.add))
                        src, shift = dst, 2 * shift
                    n_e = src[:, NT - 1].unsqueeze(2).broadcast_to([P, E, MAXN])
                    step(v.tensor_tensor(over[:], n_e, tile_steps, ALU.is_gt))
                    step(v.tensor_reduce(tiles_e[:], over[:], AX.X, ALU.add))
                    end, shift = tiles_e[:], 1
                    while shift < E:
                        dst = ends[:, (shift.bit_length() - 1) % 2]
                        v.tensor_copy(dst[:, :shift], end[:, :shift]).then_inc(steps, 1)
                        made[0] += 1
                        step(v.tensor_tensor(dst[:, shift:], end[:, shift:], end[:, :E - shift], ALU.add))
                        end, shift = dst, 2 * shift
                    v.tensor_tensor(base[:], end, tiles_e[:], ALU.subtract).then_inc(steps, 1)
                    made[0] += 1
                    step(v.tensor_tensor(spot[:, 0], src, tot[:], ALU.subtract))
                    step(v.tensor_tensor(spot[:, 1], spot[:, 0], p_r[:, 0:NT * E].rearrange("p (t e) -> p t e", e=E), ALU.add))
                    step(v.scalar_tensor_tensor(spot[:, 0], base[:].unsqueeze(1).broadcast_to([P, NT, E]), float(P), spot[:, 1], ALU.mult, ALU.add))
                    step(v.tensor_tensor(spot[:, 1], spot[:, 0], choice[:], ALU.mult))
                    step(v.tensor_reduce(place[:], spot[:, 1], AX.X, ALU.add))
                    dve.wait_ge(exp_ready, 1)
                    step(v.tensor_reduce(total[:], expd[:], AX.X, ALU.add))
                    step(v.reciprocal(rows[:, :, GATE_AT], total[:]))
                    v.tensor_tensor(place_u[:], place[:], nowhere, ALU.add).then_inc(placed, 1)
                    v.tensor_copy(used_tiles[:], end[:, E - 1:]).then_inc(steps, 1)
                    made[0] += 1
                    step(v.tensor_tensor(past[:], tile_no, end.unsqueeze(1).broadcast_to([P, SLOT_TILES, E]), ALU.is_ge))
                    step(v.tensor_reduce(owner[:], past[:], AX.X, ALU.add))
                    step(v.tensor_scalar(expert_of[:], owner[:], float(E - 1), None, ALU.min))

        with ExitStack() as ctx:
            def sb(name, shape, dt=F32):
                return ctx.enter_context(nc.sbuf_tensor(name, shape, dt))

            def ps(name, shape):
                return ctx.enter_context(nc.psum_tensor(name, shape, F32))

            def sem(name):
                return ctx.enter_context(nc.semaphore(name))

            RING = 4
            MAYBE = 2
            xs = sb("xs", [P, RING, ROW])
            ids = sb("ids", [P, RING], mybir.dt.uint32)
            xn = sb("xn", [P, 2, D])
            xt = sb("xt", [C + 1, 2, 2, P])
            w1t = sb("w1t", [C + 1, 2, 2, FF])
            hidden_t = sb("hidden_t", [P, 2, KC, P])
            yb = sb("yb", [P, D])
            ys = sb("ys", [P, RING, D])
            p_x = ps("p_x", [P, 512])
            p_h = ps("p_h2", [P, 2, 1024])
            p_y = ps("p_y", [P, 512])
            xs_in = [sem(f"xs_in{r}") for r in range(RING)]
            stored = [sem(f"stored{r}") for r in range(RING)]
            (ones_set, ids_ready, xn_ready, w1t_ready, x_tr, xt_ready, up_ready, hidden_ready, down_ready, y_read, y_ready) = (
                sem(x) for x in ("ones_set", "ids_ready", "xn_ready", "w1t_ready", "x_tr", "xt_ready", "up_ready", "hidden_ready",
                                 "down_ready", "y_read", "y_ready"))

            assert SLOT_TILES % RING == 0

            def tiles(eng, body):
                last = SLOT_TILES // RING - 1
                for r in range(RING):
                    body(0, r, 3)
                with eng.Fori(1, last) as turn:
                    for r in range(RING):
                        body(turn, r, 3)
                for r in range(RING):
                    body(last, r, RING - 1 - r)

            def used_by(eng):
                return eng.value_load(used_tiles[0:1, 0:1], min_val=0, max_val=SLOT_TILES)

            def taken(eng, used, i):
                return eng.If(used > i) if isinstance(i, int) and i >= SLOT_TILES - MAYBE else nullcontext()

            with nc.Block() as block:
                @block.sync
                def _(sp):
                    by_tile = sorted_rows.rearrange("(i p) c -> i p c", p=P)
                    for r in range(RING):
                        sp.dma_start(xs[:, r], by_tile[r]).then_inc(xs_in[r], 16)
                    with sp.Fori(1, SLOT_TILES // RING) as turn:
                        for r in range(RING):
                            sp.wait_ge(y_ready, RING * (turn - 1) + r + 1)
                            sp.dma_start(xs[:, r], by_tile[ds(RING * turn + r, 1)].rearrange("o p c -> (o p) c")).then_inc(xs_in[r], 16)

                @block.gpsimd
                def _(pool):
                    def body(turn, r, ahead):
                        i = RING * turn + r
                        done = i + 1 if isinstance(i, int) else pool.to_reg(i + 1)
                        with taken(pool, used, i):
                            wait_apart(pool, y_ready, done)
                            pool.wait_ge(ids_ready, done)
                            nc.gpsimd.indirect_dma_start(out=out.rearrange("b t d -> (b t) d"),
                                                         out_offset=bass.IndirectOffsetOnAxis(ap=ids[:, r:r + 1], axis=0),
                                                         in_=ys[:, r], in_offset=None, bounds_check=B * L - 1,
                                                         oob_is_err=False).then_inc(stored[r], 16)

                    used = used_by(pool)
                    tiles(pool, body)
                    turns = SLOT_TILES // RING
                    for r in range(RING):
                        pool.wait_ge(stored[r], 16 * (turns - 1))
                        with taken(pool, used, RING * (turns - 1) + r):
                            pool.wait_ge(stored[r], 16 * turns)

                @block.scalar
                def _(act):
                    def x_out(i, u):
                        act.wait_ge(x_tr, i + 1)
                        nc.scalar.copy(xt[0:C, u], p_x[0:C, 0:2 * P].rearrange("p (c t) -> p c t", c=2)).then_inc(xt_ready, 1)

                    def silu(i, u):
                        after(act, down_ready, i - 1)
                        act.wait_ge(up_ready, i + 1)
                        nc.scalar.activation(hidden_t[:, u].rearrange("p k t -> p (k t)"), p_h[:, u, 0:FF], ACT.Silu).then_inc(hidden_ready, 1)

                    def body(turn, r, ahead):
                        i = RING * turn + r
                        u = r % 2
                        if ahead >= 1:
                            with taken(act, used, i + 1):
                                silu(i + 1, 1 - u)
                        if ahead >= 2:
                            with taken(act, used, i + 2):
                                x_out(i + 2, u)

                    used = used_by(act)
                    act.wait_ge(ones_set, 1)
                    x_out(0, 0)
                    x_out(1, 1)
                    silu(0, 0)
                    tiles(act, body)

                @block.tensor
                def _(pe):
                    mm = nc.tensor.matmul

                    def x_in(i, u):
                        pe.wait_ge(xn_ready, i + 1)
                        for c in range(2):
                            last = nc.tensor.transpose(p_x[0:C, c * P:(c + 1) * P], xn[:, u, c * C:(c + 1) * C], ident)
                        last.then_inc(x_tr, 1)

                    def up(i, u):
                        wait_apart(pe, w1t_ready, i + 1)
                        wait_apart(pe, xt_ready, i + 1)
                        for k in range(KC):
                            for c in range(2):
                                n = C + c
                                last = mm(p_h[:, u, k * P:(k + 1) * P], w1t[0:n, u, c, k * P:(k + 1) * P], xt[0:n, u, c],
                                          start=(c == 0), stop=(c == 1), skip_group_check=True)
                        last.then_inc(up_ready, 1)

                    def down(i, u, e):
                        wait_apart(pe, hidden_ready, i + 1)
                        for k in range(KC):
                            last = mm(p_y[:, 0:D], hidden_t[:, u, k], w2s[:, ds(e, 1), k].rearrange("p o d -> p (o d)"),
                                      start=(k == 0), stop=(k == KC - 1))
                        last.then_inc(down_ready, 1)

                    def body(turn, r, ahead):
                        i = RING * turn + r
                        u = r % 2
                        e = pe.value_load(expert_of[0:1, ds(i, 1)], min_val=0, max_val=E - 1)
                        if ahead >= 1:
                            with taken(pe, used, i + 1):
                                up(i + 1, 1 - u)
                        if ahead >= 2:
                            with taken(pe, used, i + 2):
                                x_in(i + 2, u)
                        with taken(pe, used, i):
                            wait_apart(pe, y_read, i + 1)
                            down(i, u, e)

                    used = used_by(pe)
                    for _ in range(12):
                        mm(p_y[:, 0:P], ident, ident, start=True, stop=True)
                    x_in(0, 0)
                    pe.wait_ge(xt_ready, 1)
                    x_in(1, 1)
                    up(0, 0)
                    pe.wait_ge(w2_in, 16 * (E + 1))
                    tiles(pe, body)

                @block.vector
                def _(dve):
                    v = nc.vector

                    def norm(i, r, turn, u):
                        after(dve, x_tr, i - 1)
                        dve.wait_ge(xs_in[r], 16 * turn + 16)
                        v.tensor_scalar(xn[:, u], xs[:, r, 0:D], xs[:, r, MEAN_AT:MEAN_AT + 1], xs[:, r, RSTD_AT:RSTD_AT + 1],
                                        ALU.subtract, ALU.mult).then_inc(xn_ready, 1)

                    def expert_of_tile(i):
                        return dve.value_load(expert_of[0:1, ds(i, 1)], min_val=0, max_val=E - 1)

                    def expert_in(i, u, e):
                        after(dve, up_ready, i - 1)
                        v.tensor_copy(w1t[:, u:u + 1].rearrange("p o c f -> p (o c) f"), w1s[:, ds(e, 1)].rearrange("p o c f -> p (o c) f")).then_inc(w1t_ready, 1)

                    def body(turn, r, ahead):
                        i = RING * turn + r
                        u = r % 2
                        e = expert_of_tile(i)
                        if ahead >= 2:
                            e_ahead = expert_of_tile(i + 2)
                            with taken(dve, used, i + 2):
                                expert_in(i + 2, u, e_ahead)
                        with taken(dve, used, i):
                            leave(turn, r, i, e)
                        if ahead >= 3:
                            norm(i + 3, (r + 3) % RING, turn + (r + 3) // RING, 1 - u)

                    def leave(turn, r, i, e):
                        if not isinstance(turn, int) or turn:
                            wait_apart(dve, stored[r], 16 * turn)
                        v.tensor_copy(ids[:, r:r + 1], xs[:, r, ID_AT:ID_AT + 1]).then_inc(ids_ready, 1)
                        after(dve, y_ready, i)
                        dve.wait_ge(down_ready, i + 1)
                        v.tensor_tensor(yb[:], p_y[:, 0:D], b2s[:, ds(e, 1)].rearrange("p o d -> p (o d)"), ALU.add).then_inc(y_read, 1)
                        wait_apart(dve, y_read, i + 2)
                        v.scalar_tensor_tensor(ys[:, r], yb[:], xs[:, r, GATE_AT:GATE_AT + 1], xs[:, r, 0:D], ALU.mult, ALU.add).then_inc(y_ready, 1)

                    used = used_by(dve)
                    v.sem_inc(y_read, 1)
                    v.memset(xt[C:C + 1, :], 1.0).then_inc(ones_set, 1)
                    norm(0, 0, 0, 0)
                    dve.wait_ge(w1_in, 16 * E)
                    expert_in(0, 0, expert_of_tile(0))
                    norm(1, 1, 0, 1)
                    expert_in(1, 1, expert_of_tile(1))
                    norm(2, 2, 0, 0)
                    tiles(dve, body)


def layouts(x, txt, L0_tok_proj_w, L0_tok_proj_b, L0_tok_cls_token, L0_tok_pos_embedding, L0_attn_conv_w,
            L0_attn_conv_b, L0_attn_ln_g, L0_attn_ln_b, L0_attn_qkv_w, L0_attn_qkv_b, L0_attn_bn_w1, L0_attn_bn_w2,
            L0_attn_temperature, L0_attn_proj_w, L0_attn_proj_b, L0_attn_mn_g, L0_attn_mn_b, L0_ffn_Wg, L0_ffn_W1,
            L0_ffn_b1, L0_ffn_W2, L0_ffn_b2):
    import numpy as np

    f = np.float32

    def chunks(a, n, rows):
        return np.ascontiguousarray(np.moveaxis(a.reshape(n, rows, *a.shape[1:]), 0, 1))

    G = 96 // 16
    pt = x.reshape(B, 3, G, 16, G, 16).transpose(1, 3, 5, 0, 2, 4).reshape(KC, P, PAIRS, 2, NPATCH)
    patches = np.zeros((PAIRS, P, KC, 2, HALF), f)
    patches[..., 1:LP] = pt.transpose(2, 1, 0, 3, 4)
    pos_rows = np.zeros((2, HALF, D), f)
    pos_rows[:, :LP] = L0_tok_pos_embedding
    first_rows = np.zeros((2, HALF, D), f)
    first_rows[:, 0] = L0_tok_cls_token[0, 0]
    first_rows[:, 1:LP] = L0_tok_proj_b
    conv_w = np.concatenate([L0_attn_conv_w, L0_attn_conv_b[:, None]], 1)
    w_in = np.concatenate([L0_attn_qkv_w, L0_attn_bn_w1], 0).T
    b_in = np.concatenate([L0_attn_qkv_b, np.zeros(R, f)])
    w1 = np.zeros((C + 1, E, 2, FF), f)
    w1[:C] = L0_ffn_W1.reshape(E, 2, C, FF).transpose(2, 0, 1, 3)
    w1[C, :, 1] = L0_ffn_b1
    s, t = np.arange(P)[:, None], np.arange(P)[None, :]
    u_pre = (s // HALF == t // HALF) & (s <= t) & (s % HALF < LP)
    consts = [s == t, s < t, t >= 0, s <= t, u_pre] + [(s // HALF == b) & (s % HALF < LP) & (t >= 0) for b in range(2)]
    counts = np.zeros((P, CSMALL), f)
    r = np.arange(P)
    for g in range(NT):
        b, j = 2 * (g // 3), g % 3
        real = (r % HALF < LP) if j == 0 else r >= 0
        number = (b + r // HALF) * L + r % HALF if j == 0 else (b + j - 1) * L + LP + r
        counts[:, real0 + g * E:real0 + (g + 1) * E] = np.where(real[:, None], E - np.arange(E), 0)
        counts[:, token0 + g] = number
        counts[:, nowhere0 + g] = np.where(real, 0, NOWHERE)
    counts[:, down0:real0] = E - np.arange(E)
    counts[:, steps0:tile0] = np.tile(P * np.arange(MAXN), E)
    counts[:, tile0:] = np.repeat(np.arange(SLOT_TILES), E)
    return {
        "patches": patches.reshape(PAIRS, P, KC, P),
        "txt": np.ascontiguousarray(txt),
        "tok_w": chunks(L0_tok_proj_w.T, KC, P),
        "pos_rows": pos_rows.reshape(P, D),
        "first_rows": first_rows.reshape(P, D),
        "conv_w": chunks(conv_w, 2, C),
        "ln_gb": chunks(np.stack([L0_attn_ln_g, L0_attn_ln_b], 1), 2, C),
        "w_in": chunks(w_in, 2, C),
        "b_in": np.tile(b_in, (P, 1)),
        "bn2": np.ascontiguousarray(L0_attn_bn_w2.T),
        "temp": np.tile(L0_attn_temperature, (P, 1)),
        "w_out": chunks(L0_attn_proj_w.T, 2, C),
        "b_out": np.tile(L0_attn_proj_b, (P, 1)),
        "mn_gb": np.tile(np.stack([L0_attn_mn_g, L0_attn_mn_b], 1), (C // DH, 1)),
        "wg": chunks(L0_ffn_Wg, 2, C),
        "w1": w1,
        "w2": np.ascontiguousarray(L0_ffn_W2.reshape(E, KC, P, D).transpose(2, 0, 1, 3)),
        "b2": np.tile(L0_ffn_b2[None], (P, 1, 1)),
        "consts": np.concatenate([np.broadcast_to(c, (P, P)) for c in consts] + [r[:, None] // DH == np.arange(C // DH),
                                 r[:, None] // DH == np.arange(C) // DH, u_pre[:, :LP], u_pre[:, HALF:HALF + LP]], 1).astype(f),
        "counts": counts,
    }


def kernel(**inputs):
    import numpy as np
    import concourse.bacc as bacc
    from concourse.bass_utils import run_bass_kernel_spmd

    nc = bacc.Bacc("TRN2", target_bir_lowering=False, num_devices=1)
    arrays = layouts(**{k: np.asarray(v) for k, v in inputs.items()})
    args = {k: nc.dram_tensor(k, a.shape, mybir.dt.from_np(a.dtype), kind="ExternalInput").ap() for k, a in arrays.items()}
    out = nc.dram_tensor("out", (B, L, D), F32, kind="ExternalOutput").ap()
    early_fusion_layer(nc, out=out, **args)
    r = run_bass_kernel_spmd(nc, [arrays], core_ids=[0])
    return r.results[0]["out"]
```
